# Optimizing a Trainium2 kernel written in Bass

```python
import numpy as np
import jax
import jax.numpy as jnp

def _softmax(x, axis=-1):
    return jax.nn.softmax(x, axis=axis)

def _gelu(x):
    return jax.nn.gelu(x, approximate=True)

def _silu(x):
    return jax.nn.silu(x)

def _sigmoid(x):
    return jax.nn.sigmoid(x)

def _layernorm(x, axis=-1, eps=1e-05):
    m = jnp.mean(x, axis=axis, keepdims=True)
    v = jnp.var(x, axis=axis, keepdims=True)
    return (x - m) / jnp.sqrt(v + eps)

def _scatter_add(tgt, idx, src, axis=0):
    return tgt.at[idx].add(src)

def _segment_sum(src, seg, n):
    return jax.ops.segment_sum(src, seg, n)
kernel_name = 'mk_flamingo_gated_d2_seqx_r8_af14be'

def setup_inputs(seed: int=0):
    np.random.seed(seed)
    _w = jnp.asarray

    def _rec_inputs():
        import jax
        import jax.numpy as jnp
        _rk = jax.random.key(seed)
        x = -0.0002928 + 1 * jax.random.normal(jax.random.fold_in(_rk, 1), (64, 64, 128), jnp.float32)
        _lenS = 64 - jax.random.randint(jax.random.fold_in(_rk, 7), (64,), 0, max(1, 64 // 4) + 1, jnp.int32)
        _lenS2 = 64 - jax.random.randint(jax.random.fold_in(_rk, 8), (64,), 0, max(1, 64 // 4) + 1, jnp.int32)
        _ctx_1024P = jax.random.normal(jax.random.fold_in(_rk, 11), (64, 16, 128), jnp.float32)
        _ctx_1024c = jax.random.dirichlet(jax.random.fold_in(_rk, 511), 0.3 * jnp.ones((16,), jnp.float32), (64, 64))
        _ctx_1024t = jnp.einsum('bsk,bkd->bsd', _ctx_1024c, _ctx_1024P)
        _ctx_1024t = _ctx_1024t * jax.lax.rsqrt(jnp.mean(jnp.square(_ctx_1024t)) + 1e-12) * 0.953939
        ctx_1024 = -1.39393e-06 + 0.999914 * (_ctx_1024t + 0.3 * jax.random.normal(jax.random.fold_in(_rk, 611), (64, 64, 128), jnp.float32))
        _validS = jnp.arange(64)[None, :] < _lenS[:, None]
        _validS2 = jnp.arange(64)[None, :] < _lenS2[:, None]
        _causal = jnp.tril(jnp.ones((64, 64), dtype=bool))
        mask_1x1xSx1024_fk0 = jnp.where(jnp.ones((1, 1, 64, 128), dtype=bool), 0.0, 1.0).astype(jnp.float32)
        _g = jax.random.normal(jax.random.fold_in(_rk, 9001), (2, 2), jnp.float32)
        _g = jnp.sign(_g) * jnp.maximum(jnp.abs(_g), 1.0) + (_g == 0) * 1.0
        g_xattn = _g[0]
        g_ffn = _g[1]
        return (x, ctx_1024, mask_1x1xSx1024_fk0, g_xattn, g_ffn)
    x, ctx_1024, mask_1x1xSx1024_fk0, g_xattn, g_ffn = _rec_inputs()

    def _L0_xattn_setup():
        import jax, jax.numpy as jnp
        import numpy as np
        NEG_INF = -1000000000.0
        HIDDEN = 128
        HEADS = 16
        SPH = HIDDEN // HEADS
        B, Q, M = (8, 64, 64)
        R = Q + M

        def rel_shift(x):
            N, H, Qd, Rd = x.shape
            x = jnp.pad(x, ((0, 0), (0, 0), (0, 0), (1, 0)))
            x = x.reshape(N, H, Rd + 1, Qd)
            return x[:, :, 1:, :].reshape(N, H, Qd, Rd)
        key = jax.random.key(seed)
        ks = jax.random.split(key, 11)
        std = 1.0 / np.sqrt(HIDDEN)
        q_pos = jnp.arange(Q)[:, None] + M
        r_pos = jnp.arange(R)[None, :]
        token_mask = (r_pos > q_pos).astype(jnp.float32)[None, None]
        return {'query_seqs': jax.random.normal(ks[0], (B, Q, HIDDEN), jnp.float32), 'memory_seqs': jax.random.normal(ks[1], (B, M, HIDDEN), jnp.float32), 'positional_encoding': jax.random.normal(ks[2], (R, HIDDEN), jnp.float32), 'token_mask': token_mask, 'content_bias': jax.random.normal(ks[3], (HEADS, SPH), jnp.float32) * 0.02, 'position_bias': jax.random.normal(ks[4], (HEADS, SPH), jnp.float32) * 0.02, 'Wq': jax.random.normal(ks[5], (HIDDEN, HEADS, SPH), jnp.float32) * std, 'Wkc': jax.random.normal(ks[6], (HIDDEN, HEADS, SPH), jnp.float32) * std, 'Wkp': jax.random.normal(ks[7], (HIDDEN, HEADS, SPH), jnp.float32) * std, 'Wv': jax.random.normal(ks[8], (HIDDEN, HEADS, SPH), jnp.float32) * std, 'Wo': jax.random.normal(ks[9], (HEADS, SPH, HIDDEN), jnp.float32) * std}
    _L0_xattn_all = _L0_xattn_setup()
    _L0_xattn_in = {k: v for k, v in _L0_xattn_all.items() if k in ('positional_encoding', 'content_bias', 'position_bias', 'Wq', 'Wkc', 'Wkp', 'Wv', 'Wo')}
    del _L0_xattn_all

    def _L0_ffn_setup():
        import jax, jax.numpy as jnp
        import numpy as np
        LORA_DIM = 16
        LORA_TOKEN_INDEX = 1
        B, S, D, H = (4, 256, 128, 512)
        key = jax.random.key(seed)
        ks = jax.random.split(key, 6)
        x = jax.random.normal(ks[0], (B, S, D), dtype=jnp.float32)
        W1 = jax.random.normal(ks[1], (H, D), dtype=jnp.float32) * 0.02
        b1 = jnp.zeros((H,), dtype=jnp.float32)
        W2 = jax.random.normal(ks[2], (D, H), dtype=jnp.float32) * 0.02
        b2 = jnp.zeros((D,), dtype=jnp.float32)
        scale = jnp.asarray(0.001, dtype=jnp.float32)
        return {'x': x, 'W1': W1, 'b1': b1, 'W2': W2, 'b2': b2, 'scale': scale}
    _L0_ffn_all = _L0_ffn_setup()
    _L0_ffn_in = {k: v for k, v in _L0_ffn_all.items() if k in ('W1', 'b1', 'W2', 'b2', 'scale')}
    del _L0_ffn_all

    def _L1_xattn_setup():
        import jax, jax.numpy as jnp
        import numpy as np
        import math
        D = 128
        H = 8
        HD = D // H
        TEMP = math.sqrt(D)
        EPS = 1e-05

        def _layernorm(x, g, b):
            mu = jnp.mean(x, axis=-1, keepdims=True)
            var = jnp.var(x, axis=-1, keepdims=True)
            return (x - mu) * jax.lax.rsqrt(var + EPS) * g + b
        key = jax.random.key(seed)
        ks = jax.random.split(key, 8)
        B, Lq, Lk = (4, 256, 256)
        Q = jax.random.normal(ks[0], (B, Lq, D), dtype=jnp.float32)
        K = jax.random.normal(ks[1], (B, Lk, D), dtype=jnp.float32)
        V = jax.random.normal(ks[2], (B, Lk, D), dtype=jnp.float32)
        Wq = jax.random.normal(ks[3], (D, D), dtype=jnp.float32) * 0.02
        Wk = jax.random.normal(ks[4], (D, D), dtype=jnp.float32) * 0.02
        Wv = jax.random.normal(ks[5], (D, D), dtype=jnp.float32) * 0.02
        Wo = jax.random.normal(ks[6], (D, D), dtype=jnp.float32) * 0.02
        pre_g = jnp.ones((D,), jnp.float32)
        pre_b = jnp.zeros((D,), jnp.float32)
        ln_g = jnp.ones((D,), jnp.float32)
        ln_b = jnp.zeros((D,), jnp.float32)
        return {'Q': Q, 'K': K, 'V': V, 'Wq': Wq, 'Wk': Wk, 'Wv': Wv, 'Wo': Wo, 'pre_g': pre_g, 'pre_b': pre_b, 'ln_g': ln_g, 'ln_b': ln_b}
    _L1_xattn_all = _L1_xattn_setup()
    _L1_xattn_in = {k: v for k, v in _L1_xattn_all.items() if k in ('Wq', 'Wk', 'Wv', 'Wo', 'pre_g', 'pre_b', 'ln_g', 'ln_b')}
    del _L1_xattn_all

    def _L1_ffn_setup():
        import jax, jax.numpy as jnp
        import numpy as np
        D = 128
        H = 512
        O = 128
        E = 8
        K = 2
        key = jax.random.key(seed)
        ks = jax.random.split(key, 8)
        B, S = (2, 256)
        x = jax.random.normal(ks[0], (B, S, D), dtype=jnp.float32)
        s = 0.02
        Wr = jax.random.normal(ks[1], (D, E), dtype=jnp.float32) * s
        br = jnp.zeros((E,), dtype=jnp.float32)
        W1 = jax.random.normal(ks[2], (E, D, H), dtype=jnp.float32) * s
        b1 = jnp.zeros((E, H), dtype=jnp.float32)
        W2 = jax.random.normal(ks[3], (E, H, O), dtype=jnp.float32) * s
        b2 = jnp.zeros((E, O), dtype=jnp.float32)
        return {'x': x, 'Wr': Wr, 'br': br, 'W1': W1, 'b1': b1, 'W2': W2, 'b2': b2}
    _L1_ffn_all = _L1_ffn_setup()
    _L1_ffn_in = {k: v for k, v in _L1_ffn_all.items() if k in ('Wr', 'br', 'W1', 'b1', 'W2', 'b2')}
    del _L1_ffn_all
    return {'x': x, 'ctx_1024': ctx_1024, 'mask_1x1xSx1024_fk0': mask_1x1xSx1024_fk0, 'g_xattn': g_xattn, 'g_ffn': g_ffn, 'L0_xattn_positional_encoding': _L0_xattn_in['positional_encoding'], 'L0_xattn_content_bias': _L0_xattn_in['content_bias'], 'L0_xattn_position_bias': _L0_xattn_in['position_bias'], 'L0_xattn_Wq': _L0_xattn_in['Wq'], 'L0_xattn_Wkc': _L0_xattn_in['Wkc'], 'L0_xattn_Wkp': _L0_xattn_in['Wkp'], 'L0_xattn_Wv': _L0_xattn_in['Wv'], 'L0_xattn_Wo': _L0_xattn_in['Wo'], 'L0_ffn_W1': _L0_ffn_in['W1'], 'L0_ffn_b1': _L0_ffn_in['b1'], 'L0_ffn_W2': _L0_ffn_in['W2'], 'L0_ffn_b2': _L0_ffn_in['b2'], 'L0_ffn_scale': _L0_ffn_in['scale'], 'L1_xattn_Wq': _L1_xattn_in['Wq'], 'L1_xattn_Wk': _L1_xattn_in['Wk'], 'L1_xattn_Wv': _L1_xattn_in['Wv'], 'L1_xattn_Wo': _L1_xattn_in['Wo'], 'L1_xattn_pre_g': _L1_xattn_in['pre_g'], 'L1_xattn_pre_b': _L1_xattn_in['pre_b'], 'L1_xattn_ln_g': _L1_xattn_in['ln_g'], 'L1_xattn_ln_b': _L1_xattn_in['ln_b'], 'L1_ffn_Wr': _L1_ffn_in['Wr'], 'L1_ffn_br': _L1_ffn_in['br'], 'L1_ffn_W1': _L1_ffn_in['W1'], 'L1_ffn_b1': _L1_ffn_in['b1'], 'L1_ffn_W2': _L1_ffn_in['W2'], 'L1_ffn_b2': _L1_ffn_in['b2']}

def reference(x, ctx_1024, mask_1x1xSx1024_fk0, g_xattn, g_ffn, L0_xattn_positional_encoding, L0_xattn_content_bias, L0_xattn_position_bias, L0_xattn_Wq, L0_xattn_Wkc, L0_xattn_Wkp, L0_xattn_Wv, L0_xattn_Wo, L0_ffn_W1, L0_ffn_b1, L0_ffn_W2, L0_ffn_b2, L0_ffn_scale, L1_xattn_Wq, L1_xattn_Wk, L1_xattn_Wv, L1_xattn_Wo, L1_xattn_pre_g, L1_xattn_pre_b, L1_xattn_ln_g, L1_xattn_ln_b, L1_ffn_Wr, L1_ffn_br, L1_ffn_W1, L1_ffn_b1, L1_ffn_W2, L1_ffn_b2):
    import jax
    import jax.numpy as jnp

    def _L0_xattn_ref(query_seqs, memory_seqs, positional_encoding, token_mask, content_bias, position_bias, Wq, Wkc, Wkp, Wv, Wo):
        import jax, jax.numpy as jnp
        import numpy as np
        NEG_INF = -1000000000.0
        HIDDEN = 128
        HEADS = 16
        SPH = HIDDEN // HEADS
        B, Q, M = (8, 64, 64)
        R = Q + M

        def rel_shift(x):
            N, H, Qd, Rd = x.shape
            x = jnp.pad(x, ((0, 0), (0, 0), (0, 0), (1, 0)))
            x = x.reshape(N, H, Rd + 1, Qd)
            return x[:, :, 1:, :].reshape(N, H, Qd, Rd)
        reference_seqs = jnp.concatenate([memory_seqs, query_seqs], axis=1)
        query = jnp.einsum('nqd,dhs->nqhs', query_seqs, Wq)
        key_content = jnp.einsum('nrd,dhs->nrhs', reference_seqs, Wkc)
        key_position = jnp.einsum('rd,dhs->rhs', positional_encoding, Wkp)
        value = jnp.einsum('nrd,dhs->nrhs', reference_seqs, Wv)
        content = jnp.einsum('nqhs,nrhs->nhqr', query + content_bias, key_content)
        positions = jnp.einsum('nqhs,rhs->nhqr', query + position_bias, key_position)
        positions = rel_shift(positions)
        scores = (content + positions) / np.sqrt(SPH) + token_mask * NEG_INF
        attn = jax.nn.softmax(scores, axis=3)
        out = jnp.einsum('nhqr,nrhs->nqhs', attn, value)
        return jnp.einsum('nqhs,hsd->nqd', out, Wo)

    def _L0_ffn_ref(x, W1, b1, W2, b2, scale):
        import jax, jax.numpy as jnp
        import numpy as np
        LORA_DIM = 16
        LORA_TOKEN_INDEX = 1
        B, S, D, H = (4, 256, 128, 512)
        Bx, Sx, Dx = x.shape
        Hx = W1.shape[0]
        lt = jax.lax.dynamic_slice_in_dim(x, LORA_TOKEN_INDEX, LORA_DIM, axis=1)
        even = lt[:, ::2, :]
        odd = lt[:, 1::2, :]
        m1 = (even[:, :4, :, None] * odd[:, :4, None, :]).reshape(Bx, Hx, Dx)
        m2 = (even[:, 4:, :, None] * odd[:, 4:, None, :]).reshape(Bx, Dx, Hx)
        h = jnp.einsum('bsd,hd->bsh', x, W1) + scale * jnp.einsum('bsd,bhd->bsh', x, m1) + b1
        h = jax.nn.gelu(h, approximate=False)
        out = jnp.einsum('bsh,oh->bso', h, W2) + scale * jnp.einsum('bsh,boh->bso', h, m2) + b2
        return out

    def _L1_xattn_ref(Q, K, V, Wq, Wk, Wv, Wo, pre_g, pre_b, ln_g, ln_b):
        import jax, jax.numpy as jnp
        import numpy as np
        import math
        D = 128
        H = 8
        HD = D // H
        TEMP = math.sqrt(D)
        EPS = 1e-05

        def _layernorm(x, g, b):
            mu = jnp.mean(x, axis=-1, keepdims=True)
            var = jnp.var(x, axis=-1, keepdims=True)
            return (x - mu) * jax.lax.rsqrt(var + EPS) * g + b
        B, Lq, _ = Q.shape
        Lk = K.shape[1]
        Qn = _layernorm(Q, pre_g, pre_b)
        Kn = _layernorm(K, pre_g, pre_b)
        q = (Qn @ Wq).reshape(B, Lq, H, HD)
        k = (Kn @ Wk).reshape(B, Lk, H, HD)
        v = (V @ Wv).reshape(B, Lk, H, HD)
        scores = jnp.einsum('bqhd,bkhd->bhqk', q, k) / TEMP
        scores = jnp.clip(scores, -10000.0, 10000.0)
        A = jax.nn.softmax(scores, axis=-1)
        O = jnp.einsum('bhqk,bkhd->bqhd', A, v).reshape(B, Lq, D)
        O = _layernorm(O, ln_g, ln_b)
        O = O + jax.nn.gelu(O @ Wo, approximate=False)
        return O

    def _L1_ffn_ref(x, Wr, br, W1, b1, W2, b2):
        import jax, jax.numpy as jnp
        import numpy as np
        D = 128
        H = 512
        O = 128
        E = 8
        K = 2
        B, S, _ = x.shape
        T = B * S
        xf = x.reshape(T, D)
        logits = xf @ Wr + br
        topk_logits, topk_idx = jax.lax.top_k(logits, K)
        gates = jax.nn.softmax(topk_logits, axis=1)
        dense_gates = jnp.zeros((T, E), dtype=logits.dtype).at[jnp.arange(T)[:, None], topk_idx].set(gates)
        h = jax.nn.relu(jnp.einsum('td,edh->teh', xf, W1) + b1)
        y = jnp.einsum('teh,eho->teo', h, W2) + b2
        out = jnp.einsum('te,teo->to', dense_gates, y)
        return out.reshape(B, S, O)
    x = x + jnp.tanh(g_xattn[0]) * _L0_xattn_ref(_layernorm(x, axis=-1), ctx_1024, L0_xattn_positional_encoding, mask_1x1xSx1024_fk0, L0_xattn_content_bias, L0_xattn_position_bias, L0_xattn_Wq, L0_xattn_Wkc, L0_xattn_Wkp, L0_xattn_Wv, L0_xattn_Wo)
    x = x + jnp.tanh(g_ffn[0]) * _L0_ffn_ref(_layernorm(x, axis=-1), L0_ffn_W1, L0_ffn_b1, L0_ffn_W2, L0_ffn_b2, L0_ffn_scale)
    x = x + jnp.tanh(g_xattn[1]) * _L1_xattn_ref(_layernorm(x, axis=-1), ctx_1024, ctx_1024, L1_xattn_Wq, L1_xattn_Wk, L1_xattn_Wv, L1_xattn_Wo, L1_xattn_pre_g, L1_xattn_pre_b, L1_xattn_ln_g, L1_xattn_ln_b)
    x = x + jnp.tanh(g_ffn[1]) * _L1_ffn_ref(_layernorm(x, axis=-1), L1_ffn_Wr, L1_ffn_br, L1_ffn_W1, L1_ffn_b1, L1_ffn_W2, L1_ffn_b2)
    return x

_drawn_inputs = setup_inputs


def setup_inputs(seed=0):
    import zlib

    import numpy as np

    out = dict(_drawn_inputs(seed))
    spreads = {'g_ffn': (-1.0, 0.6),
     'L0_ffn_b1': (0.0, 0.55),
     'L0_ffn_b2': (0.0, 0.1),
     'L1_xattn_pre_g': (1.0, 0.6),
     'L1_xattn_pre_b': (0.0, 0.8),
     'L1_xattn_ln_g': (1.0, 0.2),
     'L1_xattn_ln_b': (0.0, 0.1),
     'L1_ffn_br': (0.0, 0.1),
     'L1_ffn_b1': (0.0, 0.617),
     'L1_ffn_b2': (0.0, 0.1)}
    factors = {'L0_xattn_content_bias': 8.0,
     'L0_xattn_position_bias': 8.0,
     'L1_xattn_Wq': 8.0,
     'L1_xattn_Wk': 8.0}
    for name, (base, spread) in spreads.items():
        noise = np.random.default_rng([zlib.crc32(name.encode()), seed]).standard_normal(out[name].shape)
        drawn = base * np.exp(spread * noise) if base else spread * noise
        out[name] = jnp.asarray(drawn.astype(out[name].dtype))
    for name, factor in factors.items():
        out[name] = (out[name] * factor).astype(out[name].dtype)
    return out
```

```python
from contextlib import ExitStack

import numpy as np

import concourse.bass as bass
from concourse import mybir

F32 = mybir.dt.float32
BF16 = mybir.dt.bfloat16
U32 = mybir.dt.uint32
ALU = mybir.AluOpType
ACT = mybir.ActivationFunctionType
AX = mybir.AxisListType.X

P = 128
NSEQ, SEQ, D = 64, 64, 128
TILES = NSEQ * SEQ // P
GROUPS, GT = 8, 4
GN = NSEQ // GROUPS
GTOK = GT * P
NEG_INF = -1.0e9
EPS = 1e-5

H0, S0 = 16, 8
KEYS = 2 * SEQ
BLK = 16
NBLK = NSEQ // BLK
SCALE0 = 1.0 / float(np.sqrt(S0))
PARTS = 3
WIN = SEQ - 1 + KEYS + 1
REV = KEYS + 1

H1, S1 = 8, 16
SCALE1 = 1.0 / float(np.sqrt(D))
CLIP = 10000.0

HID = 512
HC = HID // P
NE = 8


def layout(widths):
    at, out = 0, {}
    for name, w in widths:
        out[name] = (at, at + w)
        at += w
    return out, at


CONSTS, CONST_W = layout([
    ("ident", P), ("tokens_of_i", 2 * 512), ("sel_first", GT * 32), ("sel_second", 32),
    ("same_seq", GTOK), ("same_e", 4), ("same_r", P), ("same_seq_tok", 8), ("head_rows", H0), ("iota", NE), ("bias_on", 1)])
PARAMS, PARAM_W = layout([
    ("cb", 1), ("pb", 1), ("b1_0", HC), ("pre_g", 1), ("pre_b", 1), ("b1_1", NE * HC),
    ("b2_0", D), ("ln_g", D), ("ln_b", D), ("br", NE), ("scale", 1), ("g_xattn", 2), ("g_ffn", 2)])
WEIGHTS0, WEIGHT0_W = layout([("wq", D), ("wkc", D), ("wkp", D), ("wv", D), ("pe", D)])
WEIGHTS1, WEIGHT1_W = layout([
    ("wo0", D), ("w1t", HID), ("w2t", HID), ("wq1", 2 * D), ("wk1", 2 * D), ("wv1", D), ("wo1", D), ("wr", NE)])


def constants():
    c = np.zeros((P, CONST_W), np.float32)

    def put(name, a):
        c[:a.shape[0], CONSTS[name][0]:CONSTS[name][0] + a.shape[1]] = a

    p = np.arange(P)[:, None]
    put("ident", np.eye(P))
    i_of = np.repeat(np.arange(SEQ), BLK)[None, :]
    put("tokens_of_i", np.arange(SEQ)[:, None] == i_of)
    col = np.arange(32)[None, :]
    put("sel_first", np.concatenate(
        [(2 * t + p // SEQ == col // 4) & (p % SEQ == 1 + 2 * (col % 4)) for t in range(GT)], 1))
    put("sel_second", (p // SEQ == col // 4 % 2) & (p % SEQ == 9 + 2 * (col % 4)))
    row = np.arange(32)[:, None]
    put("same_seq", row // 4 == np.arange(GTOK)[None, :] // SEQ)
    put("same_e", row % 4 == np.arange(4)[None, :])
    put("same_r", row // 8 == np.arange(P)[None, :] % 4)
    put("same_seq_tok", p // SEQ == np.arange(8)[None, :] // 4)
    put("head_rows", p // S0 == np.arange(H0)[None, :])
    put("bias_on", (p % 64 >= 48) & (p % 64 < 48 + PARTS))
    put("iota", np.broadcast_to(np.arange(NE), (P, NE)))
    return c


class Count:

    def __init__(self, eng, sem):
        self.eng, self.sem, self.base, self.it, self.per, self.k = eng, sem, 0, 0, 0, 0

    def enter(self, it, per):
        self.base, self.it, self.per, self.k = self.base + self.k, it, per, 0

    def leave(self, rounds):
        assert self.k == self.per, (self.k, self.per)
        self.base, self.it, self.per, self.k = self.base + rounds * self.per, 0, 0, 0

    def step(self, ins):
        self.k += 1
        ins.then_inc(self.sem, 1)
        self.eng.wait_ge(self.sem, self.base + self.it * self.per + self.k)


def flamingo_kernel(nc, x, ctx_in, mask, consts, params, weights0, weights1, w1e, w2e, b2e,
                    q_scratch, k_scratch, kp_scratch, out):
    with ExitStack() as ctx:
        def sb(name, shape, dt=F32, stack=ctx):
            return stack.enter_context(nc.sbuf_tensor(name, shape, dt))

        def sem(name):
            return ctx.enter_context(nc.semaphore(name))

        psum = ctx.enter_context(nc.psum_tensor("psum", [P, 8, 512], F32))
        X = sb("X", [P, GROUPS, GTOK])
        C = sb("C", [P, GROUPS, GTOK])
        CST = sb("CST", [P, CONST_W])
        PRM = sb("PRM", [P, PARAM_W])
        WT1 = sb("WT1", [P, WEIGHT1_W])
        O_all = sb("O_all", [P, TILES, H0, S0])
        xn = sb("xn", [P, GT, D])
        stats = sb("stats", [P, GT, 6])
        moments = sb("moments", [P, GT, 2])
        rstd = sb("rstd", [P, GT])
        neg_half = sb("neg_half", [P, GT])
        eps_tile = sb("eps_tile", [P, GT])
        tanh_x = sb("tanh_x", [P, 2])
        tanh_f = sb("tanh_f", [P, 2])

        def cst(name, rows=P):
            return CST[0:rows, CONSTS[name][0]:CONSTS[name][1]]

        def prm(name, k=None):
            a, b = PARAMS[name]
            return PRM[:, a:b] if k is None else PRM[:, a + k:a + k + 1]

        def wt1(name):
            return WT1[:, WEIGHTS1[name][0]:WEIGHTS1[name][1]]

        ident = cst("ident")

        passed = sem("passed")

        def carry(eng):
            eng.sem_inc(passed, 1)

        def ln_stats(dve, count, src, ready):
            for t in range(GT):
                ins = dve.bn_stats(stats[:, t, :], src[:, t, :])
                if t == GT - 1:
                    count.step(ins)
            carry(dve)
            for t in range(GT):
                ins = dve.bn_aggr(moments[:, t, :], stats[:, t, :])
            ins.then_inc(ready, 1)

        def ln_rstd(pool, count, done):
            count.step(pool.tensor_tensor(rstd[:, :], moments[:, :, 1], eps_tile[:, :], ALU.add))
            pool.tensor_tensor(rstd[:, :], rstd[:, :], neg_half[:, :], ALU.pow).then_inc(done, 1)

        def ln_apply(dve, dst, src):
            for t in range(GT):
                ins = dve.tensor_scalar(dst[:, t, :], src[:, t, :], moments[:, t, 0:1], rstd[:, t:t + 1],
                                        ALU.subtract, ALU.mult)
            return ins

        def tiles(ap):
            return ap.rearrange("p (t c) -> p t c", t=GT)

        heads_ctx = ExitStack()
        V_all = sb("V_all", [P, NSEQ, H0, S0 + 1], stack=heads_ctx)
        kp_stack = sb("kp_stack", [P, H0, WIN], BF16, heads_ctx)
        proj_ctx = ExitStack()
        WT0 = sb("WT0", [P, WEIGHT0_W], stack=proj_ctx)
        c_now = sb("c_now", [P, GT, D], stack=proj_ctx)
        refT = sb("refT", [P, GN, KEYS], stack=proj_ctx)
        qz = sb("qz", [P, GTOK], stack=proj_ctx)
        qr = sb("qr", [P, GTOK], stack=proj_ctx)
        kr = sb("kr", [P, 2 * GTOK], stack=proj_ctx)
        q_part = sb("q_part", [P, PARTS, GTOK], BF16, proj_ctx)
        k_part = sb("k_part", [P, PARTS, 2 * GTOK], BF16, proj_ctx)
        peT = sb("peT", [P, KEYS], stack=proj_ctx)
        kpT = sb("kpT", [P, KEYS], stack=proj_ctx)
        kp_r = sb("kp_r", [P, KEYS], stack=proj_ctx)
        kp_part = sb("kp_part", [P, PARTS, KEYS], BF16, proj_ctx)
        bias_rows = sb("bias_rows", [P, H0], stack=proj_ctx)
        bias_diff = sb("bias_diff", [P, 1], stack=proj_ctx)
        bp = sb("bp", [H0, KEYS], stack=proj_ctx)
        bp_part = sb("bp_part", [H0, PARTS, KEYS], BF16, proj_ctx)

        def wt0(name):
            return WT0[:, WEIGHTS0[name][0]:WEIGHTS0[name][1]]

        loaded = sem("loaded")
        x_loaded = sem("x_loaded")
        dve_p = sem("dve_p")
        pool_p = sem("pool_p")
        half_set = sem("half_set")
        stats_p = sem("stats_p")
        rstd_p = sem("rstd_p")
        xn_p = sem("xn_p")
        pe_turned = sem("pe_turned")
        peT_ready = sem("peT_ready")
        kp_done = sem("kp_done")
        kpT_ready = sem("kpT_ready")
        bias_ready = sem("bias_ready")
        bp_done = sem("bp_done")
        kp_split = sem("kp_split")
        kp_stored = sem("kp_stored")
        stack_zero = sem("stack_zero")
        kp_stacked = sem("kp_stacked")
        turned_p = sem("turned_p")
        c_staged = sem("c_staged")
        loaded1 = sem("loaded1")
        refx_ready = sem("refx_ready")
        refc_ready = sem("refc_ready")
        q_done = sem("q_done")
        k_done = sem("k_done")
        v_done = sem("v_done")
        qz_ready = sem("qz_ready")
        q_first = sem("q_first")
        qr_ready = sem("qr_ready")
        q_second = sem("q_second")
        q_third = sem("q_third")
        k_first = sem("k_first")
        kr_ready = sem("kr_ready")
        k_second = sem("k_second")
        k_third = sem("k_third")
        v_kept = sem("v_kept")
        q_stored = sem("q_stored")
        k_stored = sem("k_stored")
        gates_ready = sem("gates_ready")
        T_x, T_c, Q_ps = psum[:, 0, :], psum[:, 1, :], psum[:, 2, :]
        K_ps, V_ps = psum[:, 3:5, :], psum[:, 5:7, :]

        with nc.Block() as block:
            @block.sync
            def _(sp):
                sp.dma_start(PRM[:, :], params).then_inc(loaded, 16)
                sp.dma_start(CST[:, :], consts).then_inc(loaded, 16)
                sp.dma_start(WT0[:, :], weights0).then_inc(loaded, 16)
                xv = x.rearrange("(g t m) s d -> (m s) g t d", t=GT, m=2)
                cv = ctx_in.rearrange("(g t m) s d -> (m s) g t d", t=GT, m=2)
                for g in range(GROUPS):
                    sp.dma_start(tiles(X[:, g, :]), xv[:, g]).then_inc(x_loaded, 16)
                    sp.dma_start(tiles(C[:, g, :]), cv[:, g]).then_inc(x_loaded, 16)
                sp.dma_start(WT1[:, :], weights1).then_inc(loaded1, 16)
                sp.wait_ge(kp_split, 1)
                sp.dma_start(kp_scratch.rearrange("a p r -> p a r"), kp_part[:, :, :]).then_inc(kp_stored, 16)
                sp.wait_ge(kp_stored, 16)
                sp.wait_ge(stack_zero, 1)
                kv = kp_scratch.rearrange("a (h s) r -> a s h r", s=S0)
                for half, at in ((0, 0), (64, REV)):
                    w = min(KEYS, WIN - at)
                    for row, part in enumerate((0, 0, 0, 1, 1, 2)):
                        sp.dma_start(kp_stack[half + S0 * row:half + S0 * (row + 1), :, at:at + w],
                                     kv[part, :, :, 0:w]).then_inc(kp_stacked, 16)
                    for part in range(PARTS):
                        sp.dma_start(kp_stack[half + 48 + part:half + 49 + part, :, at:at + w],
                                     bp_part[:, part, 0:w]).then_inc(kp_stacked, 16)
                with sp.Fori(0, GROUPS) as g:
                    sp.wait_ge(q_third, g + 1)
                    sp.dma_start(q_scratch[:, :, g, :].rearrange("a p c -> p a c"), q_part[:, :, :])\
                        .then_inc(q_stored, 16)
                    sp.wait_ge(k_third, g + 1)
                    sp.dma_start(k_scratch[:, :, g, :].rearrange("a p c -> p a c"), k_part[:, :, :])\
                        .then_inc(k_stored, 16)
                sp.wait_ge(q_stored, 16 * GROUPS)
                sp.wait_ge(k_stored, 16 * GROUPS)
                sp.wait_ge(kp_stacked, 16 * 18)
                sp.wait_ge(loaded1, 16)

            @block.gpsimd
            def _(pool):
                count = Count(pool, pool_p)
                pool.memset(neg_half[:, :], -0.5).then_inc(half_set, 1)
                pool.memset(eps_tile[:, :], EPS).then_inc(half_set, 1)
                pool.wait_ge(half_set, 2)
                pool.memset(kp_stack[:, :, :], 0.0).then_inc(stack_zero, 1)
                pool.memset(V_all[:, :, :, :], 1.0).then_inc(v_kept, 1)
                pool.wait_ge(x_loaded, 32 * GROUPS)
                with pool.Fori(0, GROUPS) as g:
                    count.enter(g, 1)
                    pool.wait_ge(turned_p, 2 * g)
                    pool.tensor_copy(c_now[:, :, :], tiles(C[:, g, :])).then_inc(c_staged, 1)
                    pool.wait_ge(stats_p, g + 1)
                    ln_rstd(pool, count, rstd_p)
                    pool.wait_ge(q_second, g + 1)
                    pool.tensor_tensor(q_part[:, 2, :], qr[:, :], q_part[:, 1, :], ALU.subtract)\
                        .then_inc(q_third, 1)
                    pool.wait_ge(k_second, g + 1)
                    pool.tensor_tensor(k_part[:, 2, :], kr[:, :], k_part[:, 1, :], ALU.subtract)\
                        .then_inc(k_third, 1)
                    count.leave(GROUPS)

            @block.scalar
            def _(act):
                act.wait_ge(loaded, 48)
                act.activation(tanh_x[:, :], prm("g_xattn"), ACT.Tanh).then_inc(gates_ready, 1)
                act.activation(tanh_f[:, :], prm("g_ffn"), ACT.Tanh).then_inc(gates_ready, 1)
                with act.Fori(0, GROUPS) as g:
                    act.wait_ge(turned_p, 2 * g + 2)
                    act.wait_ge(v_done, g)
                    act.activation(refT[:, :, 0:SEQ], T_c.rearrange("p (n i) -> p n i", n=GN), ACT.Copy)\
                        .then_inc(refc_ready, 1)
                    act.wait_ge(qz_ready, g + 1)
                    act.wait_ge(q_stored, 16 * g)
                    act.activation(q_part[:, 0, :], qz[:, :], ACT.Copy).then_inc(q_first, 1)
                    act.wait_ge(k_done, g + 1)
                    act.wait_ge(k_stored, 16 * g)
                    act.activation(k_part[:, 0, :], K_ps.rearrange("p a b -> p (a b)"), ACT.Copy)\
                        .then_inc(k_first, 1)
                    act.wait_ge(qr_ready, g + 1)
                    act.activation(q_part[:, 1, :], qr[:, :], ACT.Copy).then_inc(q_second, 1)
                    act.wait_ge(kr_ready, g + 1)
                    act.activation(k_part[:, 1, :], kr[:, :], ACT.Copy).then_inc(k_second, 1)

            @block.vector
            def _(dve):
                count = Count(dve, dve_p)
                dve.wait_ge(loaded, 48)
                dve.wait_ge(pe_turned, 1)
                dve.tensor_copy(peT[:, :], T_x[:, 0:P]).then_inc(peT_ready, 1)
                count.step(dve.tensor_tensor(bias_diff[:, :], prm("pb"), prm("cb"), ALU.subtract))
                dve.tensor_scalar(bias_rows[:, :], cst("head_rows"), bias_diff[:, :], SCALE0,
                                  ALU.mult, ALU.mult).then_inc(bias_ready, 1)
                dve.wait_ge(kp_done, 1)
                dve.tensor_copy(kpT[:, :], T_c[:, 0:P]).then_inc(kpT_ready, 1)
                dve.wait_ge(kpT_ready, 1)

                def split(src, rest, part):
                    count.step(dve.tensor_copy(part[:, 0, :], src))
                    count.step(dve.tensor_tensor(rest, src, part[:, 0, :], ALU.subtract))
                    count.step(dve.tensor_copy(part[:, 1, :], rest))
                    return dve.tensor_tensor(part[:, 2, :], rest, part[:, 1, :], ALU.subtract)

                count.step(split(kpT[:, :], kp_r[:, :], kp_part))
                dve.wait_ge(bp_done, 1)
                count.step(dve.tensor_copy(bp[:, :], Q_ps[0:H0, 0:KEYS]))
                split(bp[:, :], kp_r[0:H0, :], bp_part).then_inc(kp_split, 1)
                dve.wait_ge(x_loaded, 32 * GROUPS)
                with dve.Fori(0, GROUPS) as g:
                    count.enter(g, 1)
                    ln_stats(dve, count, tiles(X[:, g, :]), stats_p)
                    dve.wait_ge(stats_p, g + 1)
                    dve.wait_ge(rstd_p, g + 1)
                    dve.wait_ge(turned_p, 2 * g)
                    ln_apply(dve, xn, tiles(X[:, g, :])).then_inc(xn_p, 1)
                    dve.wait_ge(turned_p, 2 * g + 1)
                    dve.wait_ge(v_done, g)
                    dve.tensor_copy(refT[:, :, SEQ:KEYS], T_x.rearrange("p (n i) -> p n i", n=GN))\
                       .then_inc(refx_ready, 1)
                    dve.wait_ge(q_done, g + 1)
                    dve.wait_ge(q_first, g)
                    dve.tensor_scalar(qz[:, :], Q_ps, prm("cb"), SCALE0, ALU.add, ALU.mult)\
                       .then_inc(qz_ready, 1)
                    dve.wait_ge(q_first, g + 1)
                    dve.wait_ge(q_third, g)
                    dve.tensor_tensor(qr[:, :], qz[:, :], q_part[:, 0, :], ALU.subtract).then_inc(qr_ready, 1)
                    dve.wait_ge(k_first, g + 1)
                    dve.wait_ge(k_third, g)
                    dve.tensor_tensor(kr[:, :], K_ps.rearrange("p a b -> p (a b)"), k_part[:, 0, :],
                                      ALU.subtract).then_inc(kr_ready, 1)
                    dve.wait_ge(v_done, g + 1)
                    dve.wait_ge(v_kept, 1)
                    dve.tensor_copy(
                        V_all[:, :, :, :].rearrange("p (g n) h s -> p g n h s", n=GN)[:, g, :, :, 0:S0]
                        .rearrange("p n h s -> p (n h) s"),
                        V_ps.rearrange("p a (n h s) -> p (a n h) s", h=H0, s=S0)).then_inc(v_kept, 1)
                    count.leave(GROUPS)

            @block.tensor
            def _(pe):
                pe.wait_ge(loaded, 48)
                pe.transpose(T_x[:, 0:P], wt0("pe"), ident).then_inc(pe_turned, 1)
                pe.wait_ge(peT_ready, 1)
                pe.matmul(T_c[:, 0:P], wt0("wkp"), peT[:, :], start=True, stop=True).then_inc(kp_done, 1)
                pe.wait_ge(kpT_ready, 1)
                pe.wait_ge(bias_ready, 1)
                pe.matmul(Q_ps[0:H0, 0:KEYS], bias_rows[:, :], kpT[:, :], start=True, stop=True)\
                  .then_inc(bp_done, 1)
                pe.wait_ge(kp_split, 1)
                with pe.Fori(0, GROUPS) as g:
                    pe.wait_ge(xn_p, g + 1)
                    pe.wait_ge(refx_ready, g)
                    for t in range(GT):
                        mm = pe.transpose(T_x[:, t * P:(t + 1) * P], xn[:, t, :], ident)
                    mm.then_inc(turned_p, 1)
                    pe.wait_ge(refc_ready, g)
                    pe.wait_ge(c_staged, g + 1)
                    for t in range(GT):
                        mm = pe.transpose(T_c[:, t * P:(t + 1) * P], c_now[:, t, :], ident)
                    mm.then_inc(turned_p, 1)
                    pe.wait_ge(refx_ready, g + 1)
                    pe.wait_ge(qz_ready, g)
                    pe.matmul(Q_ps, wt0("wq"), refT[:, :, SEQ:KEYS], start=True, stop=True).then_inc(q_done, 1)
                    pe.wait_ge(refc_ready, g + 1)
                    pe.wait_ge(kr_ready, g)
                    for a in range(2):
                        mm = pe.matmul(K_ps[:, a, :], wt0("wkc"), refT[:, a * 4:a * 4 + 4, :],
                                       start=True, stop=True)
                    mm.then_inc(k_done, 1)
                    pe.wait_ge(v_kept, g + 1)
                    for n in range(GN):
                        mm = pe.matmul(V_ps[:, n // 4, (n % 4) * P:(n % 4 + 1) * P], refT[:, n, :],
                                       wt0("wv"), start=True, stop=True)
                    mm.then_inc(v_done, 1)

        proj_ctx.close()

        att_ctx = ExitStack()
        UNITS = 2 * NBLK
        UTOK = BLK * SEQ
        q_stack = [sb(f"q_stack{b}", [P, UTOK], BF16, att_ctx) for b in range(2)]
        k_stack = [sb(f"k_stack{b}", [64, BLK * KEYS], BF16, att_ctx) for b in range(2)]
        window = [sb(f"window{b}", [P, WIN], BF16, att_ctx) for b in range(2)]
        probs = [sb(f"probs{b}", [P, UTOK], stack=att_ctx) for b in range(2)]
        max_row = [sb(f"max_row{b}", [1, UTOK], stack=att_ctx) for b in range(2)]
        max_quads = [sb(f"max_quads{b}", [P, 32], stack=att_ctx) for b in range(2)]
        neg_max = [sb(f"neg_max{b}", [32, 32], stack=att_ctx) for b in range(2)]
        ones_row = sb("ones_row", [1, P], stack=att_ctx)
        mask_sb = sb("mask_sb", [SEQ, KEYS], stack=att_ctx)
        neg_mask = sb("neg_mask", [SEQ, KEYS], stack=att_ctx)
        inv_sum = [sb(f"inv_sum{b}", [P, 8], stack=att_ctx) for b in range(2)]
        stack_set = sem("stack_set")
        mask_loaded = sem("mask_loaded")
        mask_ready = sem("mask_ready")
        unit_loaded = [sem(f"unit_loaded{b}") for b in range(2)]
        window_ready = sem("window_ready")
        scored = sem("scored")
        quads_ready = sem("quads_ready")
        quads_turned = sem("quads_turned")
        max_ready = sem("max_ready")
        row_ready = [sem(f"row_ready{b}") for b in range(2)]
        shifted = sem("shifted")
        exp_done = sem("exp_done")
        values_done = sem("values_done")
        dve_a = sem("dve_a")
        normed = sem("normed")
        S_ps = [psum[:, 2 * b:2 * b + 2, :] for b in range(2)]
        R_ps = [psum[0:32, 4 + b, 0:P] for b in range(2)]
        O_ps = [psum[:, 6 + b, 0:8 * 2 * (S0 + 1)] for b in range(2)]
        qv = q_scratch.rearrange("a (h s) g c -> a h s (g c)", s=S0)
        kv = k_scratch.rearrange("a (h s) g c -> a h s (g c)", s=S0)

        with nc.Block() as block:
            @block.sync
            def _(sp):
                sp.dma_start(mask_sb[:, :], mask).then_inc(mask_loaded, 16)
                sp.wait_ge(stack_set, 4)

                def load_unit(hh, k):
                    h, blk, b = 2 * hh + k // NBLK, k % NBLK, k % 2
                    row = 0
                    for n in (3, 2, 1):
                        for half, shift in ((0, 0), (64, 1)):
                            for a in range(n):
                                sp.dma_start(q_stack[b][half + row + 8 * a:half + row + 8 * a + 8, 0:UTOK - shift],
                                             qv[a, h, :, blk * UTOK + shift:(blk + 1) * UTOK])\
                                  .then_inc(unit_loaded[b], 16)
                        for a in range(n):
                            sp.dma_start(k_stack[b][row + 8 * a:row + 8 * a + 8, :],
                                         kv[3 - n, h, :, blk * 2 * UTOK:(blk + 1) * 2 * UTOK])\
                              .then_inc(unit_loaded[b], 16)
                        row += 8 * n

                with sp.Fori(0, H0 // 2) as hh:
                    for k in range(2):
                        sp.wait_ge(scored, UNITS * hh + k)
                        load_unit(hh, k)
                    for k in range(UNITS):
                        sp.wait_ge(max_ready, UNITS * hh + k + 1)
                        sp.wait_ge(shifted, UNITS * hh + max(k - 1, 0))
                        sp.dma_start(max_row[k % 2][0:1, :].rearrange("o (b c) -> o b c", c=32),
                                     neg_max[k % 2][:, :]).then_inc(row_ready[k % 2], 16)
                        if k + 2 < UNITS:
                            sp.wait_ge(scored, UNITS * hh + k + 1)
                            load_unit(hh, k + 2)

            @block.gpsimd
            def _(pool):
                for b in range(2):
                    pool.memset(k_stack[b][:, :], 0.0).then_inc(stack_set, 1)
                with pool.Fori(0, H0 // 2) as hh:
                    pool.wait_ge(scored, UNITS * hh)
                    for a in range(2):
                        pool.tensor_copy(window[a][:, :], kp_stack[:, 2 * hh + a, :]).then_inc(window_ready, 1)

            @block.scalar
            def _(act):
                with act.Fori(0, H0 // 2) as hh:
                    for k in range(UNITS):
                        act.wait_ge(shifted, UNITS * hh + k + 1)
                        act.wait_ge(values_done, UNITS * hh + max(k - 1, 0))
                        act.activation(probs[k % 2][:, :].rearrange("p (n i) -> p i n", n=BLK),
                                       S_ps[k % 2].rearrange("p a (i n) -> p (a i) n", n=BLK), ACT.Exp)\
                           .then_inc(exp_done, 1)

            @block.vector
            def _(dve):
                count = Count(dve, dve_a)
                for b in range(2):
                    dve.tensor_copy(q_stack[b][:, :], cst("bias_on").broadcast_to([P, UTOK])).then_inc(stack_set, 1)
                dve.memset(ones_row[:, :], 1.0).then_inc(mask_ready, 1)
                dve.wait_ge(mask_loaded, 16)
                dve.tensor_scalar(neg_mask[:, :], mask_sb[:, :], NEG_INF, None, ALU.mult).then_inc(mask_ready, 1)
                with dve.Fori(0, H0 // 2) as hh:
                    count.enter(hh, UNITS)
                    for k in range(UNITS + 2):
                        if k < UNITS:
                            b = k % 2
                            dve.wait_ge(scored, UNITS * hh + k + 1)
                            dve.tensor_reduce(max_quads[b][:, :],
                                              S_ps[b].rearrange("p a (b c) -> p (a b) c", c=32), AX, ALU.max,
                                              apply_transpose=True).then_inc(quads_ready, 1)
                        if 1 <= k <= UNITS:
                            j, b = k - 1, (k - 1) % 2
                            dve.wait_ge(quads_turned, UNITS * hh + j + 1)
                            dve.wait_ge(row_ready[b], 8 * UNITS * hh + 16 * (j // 2))
                            dve.tensor_reduce(neg_max[b][:, :], R_ps[b].rearrange("p (q c) -> p c q", q=4), AX,
                                              ALU.max, negate=True).then_inc(max_ready, 1)
                        if k >= 2:
                            j, b = k - 2, (k - 2) % 2
                            h, t0 = 2 * hh + j // NBLK, (j % NBLK) * 8
                            dve.wait_ge(values_done, UNITS * hh + j + 1)
                            dve.wait_ge(normed, UNITS * hh + max(j - 1, 0))
                            ov = O_ps[b].rearrange("p (t c) -> p t c", t=8)
                            dve.reciprocal(inv_sum[b][0:64, :], ov[0:64, :, S0])
                            count.step(dve.reciprocal(inv_sum[b][64:128, :], ov[64:128, :, 2 * S0 + 1]))
                            for m in range(2):
                                r = slice(64 * m, 64 * m + 64)
                                ins = dve.tensor_tensor(
                                    O_all[r, t0:t0 + 8, h, :], ov[r, :, m * (S0 + 1):m * (S0 + 1) + S0],
                                    inv_sum[b][r, :].rearrange("p (t o) -> p t o", o=1).broadcast_to([64, 8, S0]),
                                    ALU.mult)
                            ins.then_inc(normed, 1)
                    count.leave(H0 // 2)

            @block.tensor
            def _(pe):
                pe.wait_ge(mask_ready, 2)
                pe.wait_ge(stack_set, 4)

                def scores(hh, k):
                    b, wnd = k % 2, window[k // NBLK]
                    if k % NBLK == 0:
                        pe.wait_ge(window_ready, 2 * hh + k // NBLK + 1)
                    pe.wait_ge(exp_done, UNITS * hh + max(k - 1, 0))
                    for a in range(2):
                        pe.matmul(S_ps[b][:, a, :], neg_mask[:, :], cst("tokens_of_i", SEQ)[:, 512 * a:512 * a + 512],
                                  start=True, stop=False, skip_group_check=True)
                    pe.wait_ge(unit_loaded[b], 16 * 18 * (UNITS // 2) * hh + 16 * 18 * (k // 2 + 1))
                    sv = S_ps[b].rearrange("p a (i n) -> p a i n", n=BLK)
                    qn = q_stack[b][0:64, :].rearrange("p (n a i) -> p n a i", n=BLK, a=2)
                    for n in range(BLK):
                        for a in range(2):
                            pe.matmul(sv[:, a, :, n], k_stack[b][:, n * KEYS:(n + 1) * KEYS], qn[:, n, a, :],
                                      start=False, stop=False, skip_group_check=True)
                    qi = q_stack[b][:, :].rearrange("p (n i) -> p i n", n=BLK)
                    for i in range(SEQ):
                        mm = pe.matmul(sv[:, i // 32, i % 32, :], wnd[:, SEQ - 1 - i:SEQ - 1 - i + KEYS], qi[:, i, :],
                                       start=False, stop=False, skip_group_check=True)
                    mm.then_inc(scored, 1)

                with pe.Fori(0, H0 // 2) as hh:
                    for k in range(UNITS + 2):
                        if k < UNITS:
                            scores(hh, k)
                        if 1 <= k <= UNITS:
                            j, b = k - 1, (k - 1) % 2
                            pe.wait_ge(quads_ready, UNITS * hh + j + 1)
                            pe.transpose(R_ps[b], max_quads[b][:, :], ident).then_inc(quads_turned, 1)
                        if k >= 2:
                            j, b = k - 2, (k - 2) % 2
                            h, n0 = 2 * hh + j // NBLK, (j % NBLK) * BLK
                            pe.wait_ge(exp_done, UNITS * hh + j + 1)
                            pe.wait_ge(normed, UNITS * hh + max(j - 1, 0))
                            ov = O_ps[b].rearrange("p (t c) -> p t c", t=8)
                            for t in range(8):
                                mm = pe.matmul(ov[:, t, :], probs[b][:, t * P:(t + 1) * P],
                                               V_all[:, n0 + 2 * t:n0 + 2 * t + 2, h, :], start=True, stop=True)
                            mm.then_inc(values_done, 1)
                        if 1 <= k <= UNITS:
                            j, b = k - 1, (k - 1) % 2
                            pe.wait_ge(row_ready[b], 8 * UNITS * hh + 16 * (j // 2 + 1))
                            for a in range(2):
                                mm = pe.matmul(S_ps[b][:, a, :], ones_row[:, :], max_row[b][:, 512 * a:512 * a + 512],
                                               start=False, stop=True, skip_group_check=True)
                            mm.then_inc(shifted, 1)
        att_ctx.close()
        heads_ctx.close()

        W1E = sb("W1E", [P, NE, HID])
        W2E = sb("W2E", [P, NE, HC, D])
        B2E = sb("B2E", [NE, D])
        experts_loaded = sem("experts_loaded")

        ffn_ctx = ExitStack()
        o_now = sb("o_now", [P, GT, D], stack=ffn_ctx)
        oT = sb("oT", [P, GTOK], stack=ffn_ctx)
        x1 = sb("x1", [P, GT, D], stack=ffn_ctx)
        xT = sb("xT", [P, GTOK], stack=ffn_ctx)
        odd1 = sb("odd1", [P, GN, 4], stack=ffn_ctx)
        odd2 = sb("odd2", [P, GN, 4], stack=ffn_ctx)
        up = sb("up", [32, GTOK], stack=ffn_ctx)
        even1 = sb("even1", [32, 4, P], stack=ffn_ctx)
        masked2 = sb("masked2", [32, GT * P], stack=ffn_ctx)
        picked2 = sb("picked2", [32, GT, 32], stack=ffn_ctx)
        even2 = sb("even2", [32, GT, 4, 32], stack=ffn_ctx)
        hT = sb("hT", [P, HC, GTOK], stack=ffn_ctx)
        low = sb("low", [P, GT * HC, 8], stack=ffn_ctx)
        lowT = sb("lowT", [32, GTOK], stack=ffn_ctx)
        fin = sb("fin", [P, GT, D], stack=ffn_ctx)
        names = ("o_staged o_turned oT_ready y_done x1_ready stats_f rstd_f xn_f x_turned xT_ready even_picked "
                 "odd_ready up_done up_ready even1_ready even2_ready h_done h_ready low_done low_ready "
                 "low_turned lowT_ready ffn_done dve_f pool_f x_ffn").split()
        F = {name: sem(name) for name in names}
        scale_col = prm("scale")

        with nc.Block() as block:
            @block.sync
            def _(sp):
                sp.dma_start(W1E[:, :, :], w1e).then_inc(experts_loaded, 16)
                sp.dma_start(W2E[:, :, :, :], w2e).then_inc(experts_loaded, 16)
                sp.dma_start(B2E[:, :], b2e).then_inc(experts_loaded, 16)
                sp.wait_ge(experts_loaded, 48)

            @block.gpsimd
            def _(pool):
                count = Count(pool, F["pool_f"])
                ov = O_all[:, :, :, :].rearrange("p (g t) h s -> p g t (h s)", g=GROUPS)
                with pool.Fori(0, GROUPS) as g:
                    count.enter(g, 1)
                    pool.wait_ge(F["o_turned"], g)
                    pool.tensor_copy(o_now[:, :, :], ov[:, g, :, :]).then_inc(F["o_staged"], 1)
                    pool.wait_ge(F["stats_f"], g + 1)
                    ln_rstd(pool, count, F["rstd_f"])
                    count.leave(GROUPS)

            @block.scalar
            def _(act):
                with act.Fori(0, GROUPS) as g:
                    act.wait_ge(F["o_turned"], g + 1)
                    act.activation(oT[:, :], psum[:, 0, :], ACT.Copy).then_inc(F["oT_ready"], 1)
                    act.wait_ge(F["x_turned"], g + 1)
                    act.activation(xT[:, :], psum[:, 0, :], ACT.Copy).then_inc(F["xT_ready"], 1)
                    for e in range(HC):
                        act.wait_ge(F["h_done"], HC * g + e + 1)
                        act.activation(hT[:, e, :], psum[:, 5 + e % 2, :], ACT.Gelu, bias=prm("b1_0", e))\
                           .then_inc(F["h_ready"], 1)
                    act.wait_ge(F["low_turned"], g + 1)
                    act.activation(lowT[:, :], psum[0:32, 4, :], ACT.Copy).then_inc(F["lowT_ready"], 1)

            @block.vector
            def _(dve):
                count = Count(dve, F["dve_f"])
                same_e = cst("same_e", 32)
                with dve.Fori(0, GROUPS) as g:
                    count.enter(g, 5)
                    dve.wait_ge(F["y_done"], g + 1)
                    dve.scalar_tensor_tensor(out=x1[:, :, :], in0=tiles(psum[:, 1, :]), scalar=tanh_x[:, 0:1],
                                             in1=tiles(X[:, g, :]), op0=ALU.mult, op1=ALU.add)\
                       .then_inc(F["x1_ready"], 1)
                    dve.wait_ge(F["x1_ready"], g + 1)
                    ln_stats(dve, count, x1, F["stats_f"])
                    dve.wait_ge(F["rstd_f"], g + 1)
                    dve.wait_ge(F["stats_f"], g + 1)
                    ln_apply(dve, xn, x1).then_inc(F["xn_f"], 1)
                    dve.wait_ge(F["xT_ready"], g + 1)
                    xv = xT[:, :].rearrange("p (n i) -> p n i", n=GN)
                    dve.tensor_copy(odd1[:, :, :], xv[:, :, 2:10:2])
                    dve.tensor_copy(odd2[:, :, :], xv[:, :, 10:18:2]).then_inc(F["odd_ready"], 1)
                    dve.wait_ge(F["even_picked"], g + 1)
                    dve.tensor_tensor(
                        even1[:, :, :], psum[0:32, 2, 0:P].rearrange("p (o a) -> p o a", o=1).broadcast_to([32, 4, P]),
                        same_e.rearrange("p (e o) -> p e o", o=1).broadcast_to([32, 4, P]), ALU.mult)\
                       .then_inc(F["even1_ready"], 1)
                    count.step(dve.tensor_tensor(
                        tiles(masked2[:, :]), tiles(psum[0:32, 3, :]),
                        cst("same_r", 32).rearrange("p (o a) -> p o a", o=1).broadcast_to([32, GT, P]), ALU.mult))
                    count.step(dve.tensor_reduce(picked2[:, :, :].rearrange("p t a -> p (t a)"),
                                                 masked2[:, :].rearrange("p (c r) -> p c r", r=4), AX, ALU.add))
                    dve.tensor_tensor(
                        even2[:, :, :, :],
                        picked2[:, :, :].rearrange("p t (o a) -> p t o a", o=1).broadcast_to([32, GT, 4, 32]),
                        same_e.rearrange("p (u e o) -> p u e o", o=1, u=1).broadcast_to([32, GT, 4, 32]), ALU.mult)\
                       .then_inc(F["even2_ready"], 1)
                    dve.wait_ge(F["up_done"], g + 1)
                    dve.scalar_tensor_tensor(out=up[:, :], in0=psum[0:32, 4, :], scalar=scale_col[0:32, :],
                                             in1=cst("same_seq", 32), op0=ALU.mult, op1=ALU.mult)\
                       .then_inc(F["up_ready"], 1)
                    dve.wait_ge(F["low_done"], g + 1)
                    dve.scalar_tensor_tensor(
                        out=low[:, :, :], in0=psum[:, 1, 0:P].rearrange("p (c e) -> p c e", e=8), scalar=scale_col,
                        in1=cst("same_seq_tok").rearrange("p (o e) -> p o e", o=1).broadcast_to([P, GT * HC, 8]),
                        op0=ALU.mult, op1=ALU.mult).then_inc(F["low_ready"], 1)
                    dve.wait_ge(F["ffn_done"], g + 1)
                    count.step(dve.tensor_tensor(
                        fin[:, :, :], tiles(psum[:, 7, :]),
                        prm("b2_0").rearrange("p (o d) -> p o d", o=1).broadcast_to([P, GT, D]), ALU.add))
                    count.step(dve.scalar_tensor_tensor(
                        out=tiles(X[:, g, :]), in0=fin[:, :, :], scalar=tanh_f[:, 0:1], in1=x1[:, :, :],
                        op0=ALU.mult, op1=ALU.add))
                    count.leave(GROUPS)

            @block.tensor
            def _(pe):
                with pe.Fori(0, GROUPS) as g:
                    pe.wait_ge(F["o_staged"], g + 1)
                    pe.wait_ge(F["xT_ready"], g)
                    for t in range(GT):
                        mm = pe.transpose(psum[:, 0, t * P:(t + 1) * P], o_now[:, t, :], ident)
                    mm.then_inc(F["o_turned"], 1)
                    pe.wait_ge(F["oT_ready"], g + 1)
                    pe.wait_ge(F["low_ready"], g)
                    for t in range(GT):
                        mm = pe.matmul(psum[:, 1, t * P:(t + 1) * P], oT[:, t * P:(t + 1) * P], wt1("wo0"),
                                       start=True, stop=True)
                    mm.then_inc(F["y_done"], 1)
                    pe.wait_ge(F["xn_f"], g + 1)
                    for t in range(GT):
                        mm = pe.transpose(psum[:, 0, t * P:(t + 1) * P], xn[:, t, :], ident)
                    mm.then_inc(F["x_turned"], 1)
                    pe.wait_ge(F["even2_ready"], g)
                    for t in range(GT):
                        pe.matmul(psum[0:32, 2, 0:P], cst("sel_first")[:, 32 * t:32 * t + 32], xn[:, t, :],
                                  start=(t == 0), stop=(t == GT - 1))
                    for t in range(GT):
                        mm = pe.matmul(psum[0:32, 3, t * P:(t + 1) * P], cst("sel_second"), xn[:, t, :],
                                       start=True, stop=True)
                    mm.then_inc(F["even_picked"], 1)
                    pe.wait_ge(F["odd_ready"], g + 1)
                    pe.wait_ge(F["lowT_ready"], g)
                    pe.matmul(psum[0:32, 4, :], odd1[:, :, :].rearrange("p n e -> p (n e)"), xT[:, :],
                              start=True, stop=True).then_inc(F["up_done"], 1)
                    pe.wait_ge(F["up_ready"], g + 1)
                    pe.wait_ge(F["even1_ready"], g + 1)
                    for e in range(HC):
                        if e >= 2:
                            pe.wait_ge(F["h_ready"], HC * g + e - 1)
                        bank = psum[:, 5 + e % 2, :]
                        pe.matmul(bank, wt1("w1t")[:, e * P:(e + 1) * P], xT[:, :], start=True, stop=False)
                        pe.matmul(bank, even1[:, e, :], up[:, :], start=False, stop=True).then_inc(F["h_done"], 1)
                    pe.wait_ge(F["h_ready"], HC * g + HC)
                    for t in range(GT):
                        for r in range(HC):
                            mm = pe.matmul(psum[:, 1, 32 * t + 8 * r:32 * t + 8 * r + 8],
                                           hT[:, r, t * P:(t + 1) * P],
                                           odd2[:, 2 * t:2 * t + 2, :].rearrange("p n e -> p (n e)"),
                                           start=True, stop=True)
                    mm.then_inc(F["low_done"], 1)
                    for t in range(GT):
                        for r in range(HC):
                            pe.matmul(psum[:, 7, t * P:(t + 1) * P], hT[:, r, t * P:(t + 1) * P],
                                      wt1("w2t")[:, r * P:(r + 1) * P], start=(t == 0 and r == 0), stop=False,
                                      skip_group_check=True)
                    pe.wait_ge(F["low_ready"], g + 1)
                    for t in range(GT):
                        mm = pe.transpose(psum[0:32, 4, t * P:(t + 1) * P],
                                          low[:, HC * t:HC * t + HC, :].rearrange("p c e -> p (c e)"), ident)
                    mm.then_inc(F["low_turned"], 1)
                    pe.wait_ge(F["lowT_ready"], g + 1)
                    pe.wait_ge(F["even2_ready"], g + 1)
                    for t in range(GT):
                        mm = pe.matmul(psum[:, 7, t * P:(t + 1) * P], lowT[:, t * P:(t + 1) * P],
                                       even2[:, t, :, :].rearrange("p e a -> p (e a)"), start=False, stop=True,
                                       skip_group_check=True)
                    mm.then_inc(F["ffn_done"], 1)
        ffn_ctx.close()

        a1_ctx = ExitStack()
        x2 = sb("x2", [P, GT, D], stack=a1_ctx)
        c2 = sb("c2", [P, GT, D], stack=a1_ctx)
        xm = sb("xm", [P, GT, D], stack=a1_ctx)
        cn = sb("cn", [P, GT, D], stack=a1_ctx)
        qnT = sb("qnT", [P, GTOK], stack=a1_ctx)
        knT = sb("knT", [P, GTOK], stack=a1_ctx)
        cT = sb("cT", [P, GTOK], stack=a1_ctx)
        q1 = sb("q1", [P, 2, GTOK], stack=a1_ctx)
        k1 = sb("k1", [P, 2, GTOK], stack=a1_ctx)
        v1 = sb("v1", [P, GT, 2, D], stack=a1_ctx)
        s1 = [sb(f"s1_{b}", [P, 4, 2, SEQ], stack=a1_ctx) for b in range(2)]
        e1 = [sb(f"e1_{b}", [P, 4, 2, SEQ], stack=a1_ctx) for b in range(2)]
        eT = [sb(f"eT_{b}", [P, 4, P], stack=a1_ctx) for b in range(2)]
        top1 = [sb(f"top1_{b}", [P, 4, 2], stack=a1_ctx) for b in range(2)]
        sum1 = [sb(f"sum1_{b}", [P, 4, 2], stack=a1_ctx) for b in range(2)]
        inv1 = [sb(f"inv1_{t}", [P, 4, 2], stack=a1_ctx) for t in range(GT)]
        o1 = sb("o1", [P, GT, D], stack=a1_ctx)
        on = sb("on", [P, GT, D], stack=a1_ctx)
        onT = sb("onT", [P, GTOK], stack=a1_ctx)
        gl = sb("gl", [P, GT, D], stack=a1_ctx)
        names = ("c_staged1 stats_1 rstd_1 dve_1 pool_1 xm_ready xm_turned cn_ready cn_turned c_turned qnT_ready "
                 "knT_ready cT_ready q_done1 k_done1 v_done1 q_ready1 k_ready1 v_ready1 scored1 s_ready e_ready "
                 "e_turned eT_ready o_done1 o_ready1 on_ready on_turned onT_ready gate_done gelu_ready x_att").split()
        A = {name: sem(name) for name in names}

        with nc.Block() as block:
            @block.gpsimd
            def _(pool):
                count = Count(pool, A["pool_1"])
                with pool.Fori(0, GROUPS) as g:
                    count.enter(g, 4)
                    pool.wait_ge(A["c_turned"], g)
                    pool.tensor_copy(c2[:, :, :], tiles(C[:, g, :])).then_inc(A["c_staged1"], 1)
                    for n in range(4):
                        pool.wait_ge(A["stats_1"], 4 * g + n + 1)
                        ln_rstd(pool, count, A["rstd_1"])
                    count.leave(GROUPS)

            @block.scalar
            def _(act):
                with act.Fori(0, GROUPS) as g:
                    act.wait_ge(A["xm_turned"], g + 1)
                    act.activation(qnT[:, :], psum[:, 0, :], ACT.Identity, bias=prm("pre_b"), scale=prm("pre_g"))\
                       .then_inc(A["qnT_ready"], 1)
                    act.wait_ge(A["c_turned"], g + 1)
                    act.activation(cT[:, :], psum[:, 2, :], ACT.Copy).then_inc(A["cT_ready"], 1)
                    act.wait_ge(A["cn_turned"], g + 1)
                    act.activation(knT[:, :], psum[:, 1, :], ACT.Identity, bias=prm("pre_b"), scale=prm("pre_g"))\
                       .then_inc(A["knT_ready"], 1)
                    for a in range(2):
                        act.wait_ge(A["q_done1"], 2 * g + a + 1)
                        act.activation(q1[:, a, :], psum[:, 3, :], ACT.Copy, scale=SCALE1).then_inc(A["q_ready1"], 1)
                        act.wait_ge(A["k_done1"], 2 * g + a + 1)
                        act.activation(k1[:, a, :], psum[:, 4, :], ACT.Copy).then_inc(A["k_ready1"], 1)
                    act.wait_ge(A["v_done1"], g + 1)
                    act.activation(v1[:, :, :, :].rearrange("p t m d -> p (t m d)"),
                                   psum[:, 5:7, :].rearrange("p a b -> p (a b)"), ACT.Copy)\
                       .then_inc(A["v_ready1"], 1)
                    for t in range(GT + 1):
                        if t < GT:
                            act.wait_ge(A["s_ready"], GT * g + t + 1)
                            act.wait_ge(A["e_turned"], GT * g + max(t - 1, 0))
                            act.activation(e1[t % 2][:, :, :, :], s1[t % 2][:, :, :, :], ACT.Exp)\
                               .then_inc(A["e_ready"], 1)
                        if t >= 1:
                            act.wait_ge(A["e_turned"], GT * g + t)
                            act.wait_ge(A["o_done1"], GT * g + max(t - 2, 0))
                            act.activation(eT[(t - 1) % 2][:, :, :].rearrange("p c q -> p (c q)"),
                                           psum[:, 3 + (t - 1) % 2, :], ACT.Copy).then_inc(A["eT_ready"], 1)
                    act.wait_ge(A["on_turned"], g + 1)
                    act.activation(onT[:, :], psum[:, 0, :], ACT.Copy).then_inc(A["onT_ready"], 1)
                    act.wait_ge(A["gate_done"], g + 1)
                    act.activation(gl[:, :, :].rearrange("p t d -> p (t d)"), psum[:, 1, :], ACT.Gelu)\
                       .then_inc(A["gelu_ready"], 1)

            @block.vector
            def _(dve):
                count = Count(dve, A["dve_1"])

                def norm(n, g, dst, src):
                    ln_stats(dve, count, src, A["stats_1"])
                    dve.wait_ge(A["stats_1"], 4 * g + n + 1)
                    dve.wait_ge(A["rstd_1"], 4 * g + n + 1)
                    return ln_apply(dve, dst, src)

                with dve.Fori(0, GROUPS) as g:
                    count.enter(g, 4 + 1 + 4 * GT + 4)
                    count.step(norm(0, g, xn, tiles(X[:, g, :])))
                    norm(1, g, xm, xn).then_inc(A["xm_ready"], 1)
                    dve.wait_ge(A["c_staged1"], g + 1)
                    norm(2, g, cn, c2).then_inc(A["cn_ready"], 1)
                    for t in range(GT + 1):
                        if t < GT:
                            b = t % 2
                            dve.wait_ge(A["scored1"], g + 1)
                            dve.wait_ge(A["e_ready"], GT * g + max(t - 1, 0))
                            for half in range(2):
                                banks = psum[:, (1, 5)[half]:(1, 5)[half] + 2, t * P:(t + 1) * P]
                                ins = dve.tensor_scalar(
                                    s1[b][:, 2 * half:2 * half + 2, :, :].rearrange("p c a j -> p c (a j)"),
                                    banks, CLIP, -CLIP, ALU.min, ALU.max)
                            count.step(ins)
                            count.step(dve.tensor_reduce(top1[b][:, :, :], s1[b][:, :, :, :], AX, ALU.max))
                            dve.tensor_tensor(s1[b][:, :, :, :].rearrange("p c a j -> p (c a) j"),
                                              s1[b][:, :, :, :].rearrange("p c a j -> p (c a) j"),
                                              top1[b][:, :, :].rearrange("p c (a o) -> p (c a) o", o=1)
                                              .broadcast_to([P, H1, SEQ]), ALU.subtract)\
                               .then_inc(A["s_ready"], 1)
                        if t >= 1:
                            u, b = t - 1, (t - 1) % 2
                            dve.wait_ge(A["e_ready"], GT * g + u + 1)
                            count.step(dve.tensor_reduce(sum1[b][:, :, :], e1[b][:, :, :, :], AX, ALU.add))
                            count.step(dve.reciprocal(inv1[u][:, :, :], sum1[b][:, :, :]))
                    dve.wait_ge(A["o_done1"], GT * g + GT)
                    for u in range(GT):
                        for a in range(2):
                            ins = dve.tensor_tensor(
                                o1[:, u, 64 * a:64 * a + 64].rearrange("p (c s) -> p c s", c=4),
                                psum[:, (7, 0)[a], u * 64:(u + 1) * 64].rearrange("p (c s) -> p c s", c=4),
                                inv1[u][:, :, a:a + 1].broadcast_to([P, 4, S1]), ALU.mult)
                    ins.then_inc(A["o_ready1"], 1)
                    dve.wait_ge(A["o_ready1"], g + 1)
                    count.step(norm(3, g, on, o1))

                    def row(name):
                        return prm(name).rearrange("p (o d) -> p o d", o=1).broadcast_to([P, GT, D])

                    count.step(dve.tensor_tensor(on[:, :, :], on[:, :, :], row("ln_g"), ALU.mult))
                    dve.tensor_tensor(on[:, :, :], on[:, :, :], row("ln_b"), ALU.add).then_inc(A["on_ready"], 1)
                    dve.wait_ge(A["on_ready"], g + 1)
                    dve.wait_ge(A["gelu_ready"], g + 1)
                    count.step(dve.tensor_tensor(x2[:, :, :], gl[:, :, :], on[:, :, :], ALU.add))
                    count.step(dve.scalar_tensor_tensor(
                        out=tiles(X[:, g, :]), in0=x2[:, :, :], scalar=tanh_x[:, 1:2], in1=tiles(X[:, g, :]),
                        op0=ALU.mult, op1=ALU.add))
                    count.leave(GROUPS)

            @block.tensor
            def _(pe):
                def turn(bank, src, done):
                    for t in range(GT):
                        mm = pe.transpose(psum[:, bank, t * P:(t + 1) * P], src[:, t, :], ident)
                    mm.then_inc(done, 1)

                with pe.Fori(0, GROUPS) as g:
                    pe.wait_ge(A["c_staged1"], g + 1)
                    turn(2, c2, A["c_turned"])
                    pe.wait_ge(A["xm_ready"], g + 1)
                    turn(0, xm, A["xm_turned"])
                    pe.wait_ge(A["cn_ready"], g + 1)
                    pe.wait_ge(A["gelu_ready"], g)
                    turn(1, cn, A["cn_turned"])
                    pe.wait_ge(A["qnT_ready"], g + 1)
                    pe.wait_ge(A["knT_ready"], g + 1)
                    for a in range(2):
                        pe.wait_ge(A["q_ready1"], 2 * g + a)
                        pe.matmul(psum[:, 3, :], wt1("wq1")[:, a * P:(a + 1) * P], qnT[:, :], start=True, stop=True)\
                          .then_inc(A["q_done1"], 1)
                        pe.wait_ge(A["k_ready1"], 2 * g + a)
                        pe.matmul(psum[:, 4, :], wt1("wk1")[:, a * P:(a + 1) * P], knT[:, :], start=True, stop=True)\
                          .then_inc(A["k_done1"], 1)
                    pe.wait_ge(A["cT_ready"], g + 1)
                    for t in range(GT):
                        bank, at = 5 + t // 2, (t % 2) * 2 * D
                        pe.matmul(psum[:, bank, at:at + D], cT[:, t * P:(t + 1) * P], wt1("wv1"),
                                  start=True, stop=True)
                        for m in range(2):
                            mm = pe.matmul(psum[64 * m:64 * m + 64, bank, at + D:at + 2 * D],
                                           cT[:, t * P + SEQ * (1 - m):t * P + SEQ * (2 - m)], wt1("wv1"),
                                           start=True, stop=True)
                    mm.then_inc(A["v_done1"], 1)
                    pe.wait_ge(A["v_ready1"], g + 1)
                    pe.wait_ge(A["q_ready1"], 2 * g + 2)
                    pe.wait_ge(A["k_ready1"], 2 * g + 2)
                    for t in range(GT):
                        for h in range(H1):
                            r = slice(32 * (h % 4), 32 * (h % 4) + S1)
                            for m in range(2):
                                c = slice(t * P + SEQ * m, t * P + SEQ * (m + 1))
                                mm = pe.matmul(psum[64 * m:64 * m + 64, (1, 2, 5, 6)[h % 4],
                                                    t * P + SEQ * (h // 4):t * P + SEQ * (h // 4 + 1)],
                                               q1[r, h // 4, c], k1[r, h // 4, c], start=True, stop=True,
                                               tile_position=(32 * (h % 4), 64 * m))
                    mm.then_inc(A["scored1"], 1)
                    for t in range(GT + 2):
                        if 1 <= t <= GT:
                            u = t - 1
                            pe.wait_ge(A["e_ready"], GT * g + u + 1)
                            pe.wait_ge(A["eT_ready"], GT * g + max(u - 1, 0))
                            ev = e1[u % 2][:, :, :, :].rearrange("p c a j -> p c (a j)")
                            for c in range(4):
                                mm = pe.transpose(psum[:, 3 + u % 2, c * P:(c + 1) * P], ev[:, c, :], ident)
                            mm.then_inc(A["e_turned"], 1)
                        if t >= 2:
                            u = t - 2
                            pe.wait_ge(A["eT_ready"], GT * g + u + 1)
                            carry(pe)
                            for h in range(H1):
                                a, c = h // 4, h % 4
                                for m in range(2):
                                    mm = pe.matmul(
                                        psum[64 * m:64 * m + 64, (7, 0)[a], u * 64 + S1 * c:u * 64 + S1 * (c + 1)],
                                        eT[u % 2][64 * a:64 * a + 64, c, SEQ * m:SEQ * (m + 1)],
                                        v1[64 * a:64 * a + 64, u, a ^ m, S1 * h:S1 * (h + 1)],
                                        start=True, stop=True, tile_position=(64 * a, 64 * m))
                            mm.then_inc(A["o_done1"], 1)
                    pe.wait_ge(A["on_ready"], g + 1)
                    turn(0, on, A["on_turned"])
                    pe.wait_ge(A["onT_ready"], g + 1)
                    for t in range(GT):
                        mm = pe.matmul(psum[:, 1, t * P:(t + 1) * P], onT[:, t * P:(t + 1) * P], wt1("wo1"),
                                       start=True, stop=True)
                    mm.then_inc(A["gate_done"], 1)
        a1_ctx.close()

        x3 = [sb(f"x3_{b}", [P, GT, D]) for b in range(2)]
        x3T = [sb(f"x3T_{b}", [P, GTOK]) for b in range(2)]
        logits = sb("logits", [P, GT, NE])
        best = sb("best", [P, GT, NE])
        place = sb("place", [P, GT, NE], U32)
        placef = sb("placef", [P, GT, NE])
        second = sb("second", [P, GT])
        both = sb("both", [P, GT])
        weight = sb("weight", [P, 2, GT])
        pick = sb("pick", [P, 2, NE])
        gates = [sb(f"gates{b}", [P, GT, NE]) for b in range(2)]
        gT = sb("gT", [NE, GTOK])
        hE = [sb(f"hE{b}", [P, HC, GTOK]) for b in range(2)]
        acc = [sb(f"acc{b}", [P, GT, D]) for b in range(2)]
        res = [sb(f"res{b}", [P, GT, D]) for b in range(2)]
        names = ("dve_e pool_e stats_e rstd_e xn_e turned_e xT_e routed second_ready gates_done g_turned gT_ready "
                 "hidden_done relu_act relu_dve expert_done added bias_done res_ready").split()
        M = {name: sem(name) for name in names}
        stored = [sem(f"stored{b}") for b in range(2)]
        ov = out.rearrange("(g t m) s d -> (m s) g t d", t=GT, m=2)
        NB = NE * HC

        with nc.Block() as block:
            @block.sync
            def _(sp):
                with sp.Fori(0, GROUPS // 2) as gg:
                    for b in range(2):
                        sp.wait_ge(M["res_ready"], 2 * gg + b + 1)
                        sp.dma_start(ov[:, 2 * gg + b, :, :], res[b][:, :, :]).then_inc(stored[b], 16)
                for b in range(2):
                    sp.wait_ge(stored[b], 16 * (GROUPS // 2))

            @block.gpsimd
            def _(pool):
                count = Count(pool, M["pool_e"])
                with pool.Fori(0, GROUPS) as g:
                    count.enter(g, 1)
                    pool.wait_ge(M["stats_e"], g + 1)
                    ln_rstd(pool, count, M["rstd_e"])
                    count.leave(GROUPS)

            @block.scalar
            def _(act):
                with act.Fori(0, GROUPS // 2) as gg:
                    for b in range(2):
                        g = 2 * gg + b
                        act.wait_ge(M["turned_e"], g + 1)
                        act.activation(x3T[b][:, :], psum[:, 0, :], ACT.Copy).then_inc(M["xT_e"], 1)
                        act.wait_ge(M["routed"], g + 1)
                        act.activation(second[:, :], both[:, :], ACT.Exp).then_inc(M["second_ready"], 1)
                        act.wait_ge(M["g_turned"], g + 1)
                        act.activation(gT[:, :], psum[0:NE, 1, :], ACT.Copy).then_inc(M["gT_ready"], 1)
                        for e in range(NE):
                            act.wait_ge(M["expert_done"], NE * g + max(e - 1, 0))
                            for c in range(0, HC, 2):
                                act.wait_ge(M["hidden_done"], NB * g + HC * e + c + 1)
                                act.activation(hE[e % 2][:, c, :], psum[:, 2 + c, :], ACT.Relu,
                                               bias=prm("b1_1", HC * e + c)).then_inc(M["relu_act"], 1)

            @block.vector
            def _(dve):
                count = Count(dve, M["dve_e"])
                with dve.Fori(0, GROUPS // 2) as gg:
                    count.enter(gg, 2 * (9 + 2 * GT - 1))
                    for b in range(2):
                        g = 2 * gg + b
                        ln_stats(dve, count, tiles(X[:, g, :]), M["stats_e"])
                        dve.wait_ge(M["stats_e"], g + 1)
                        dve.wait_ge(M["rstd_e"], g + 1)
                        ln_apply(dve, x3[b], tiles(X[:, g, :])).then_inc(M["xn_e"], 1)

                        dve.wait_ge(M["bias_done"], 2 * g + 1)
                        count.step(dve.tensor_tensor(
                            logits[:, :, :], psum[:, 1, 0:GT * NE].rearrange("p (t e) -> p t e", e=NE),
                            prm("br").rearrange("p (o e) -> p o e", o=1).broadcast_to([P, GT, NE]), ALU.add))
                        carry(dve)
                        for t in range(GT):
                            ins = dve.max(best[:, t, :], logits[:, t, :])
                        count.step(ins)
                        carry(dve)
                        for t in range(GT):
                            ins = dve.max_index(place[:, t, :], best[:, t, :], logits[:, t, :])
                        count.step(ins)
                        count.step(dve.tensor_copy(placef[:, :, :], place[:, :, :]))
                        dve.tensor_tensor(both[:, :], best[:, :, 1], best[:, :, 0], ALU.subtract)\
                           .then_inc(M["routed"], 1)
                        dve.wait_ge(M["second_ready"], g + 1)
                        count.step(dve.tensor_scalar(weight[:, 1, :], second[:, :], 1.0, None, ALU.add))
                        count.step(dve.reciprocal(weight[:, 0, :], weight[:, 1, :]))
                        count.step(dve.tensor_tensor(weight[:, 1, :], second[:, :], weight[:, 0, :], ALU.mult))
                        for t in range(GT):
                            for n in range(2):
                                ins = dve.tensor_scalar(pick[:, n, :], cst("iota"), placef[:, t, n:n + 1],
                                                        weight[:, n, t:t + 1], ALU.is_equal, ALU.mult)
                            count.step(ins)
                            ins = dve.tensor_tensor(gates[b][:, t, :], pick[:, 0, :], pick[:, 1, :], ALU.add)
                            if t < GT - 1:
                                count.step(ins)
                        ins.then_inc(M["gates_done"], 1)
                        dve.wait_ge(M["gates_done"], g + 1)
                        dve.wait_ge(M["bias_done"], 2 * g + 2)
                        count.step(dve.tensor_copy(acc[b][:, :, :], tiles(psum[:, 0, :])))
                        for e in range(NE + 1):
                            if e < NE:
                                dve.wait_ge(M["expert_done"], NE * g + max(e - 1, 0))
                                for c in range(1, HC, 2):
                                    dve.wait_ge(M["hidden_done"], NB * g + HC * e + c + 1)
                                    dve.tensor_scalar(hE[e % 2][:, c, :], psum[:, 2 + c, :],
                                                      prm("b1_1", HC * e + c), 0.0, ALU.add, ALU.max)\
                                       .then_inc(M["relu_dve"], 1)
                            if e >= 1:
                                u = e - 1
                                dve.wait_ge(M["expert_done"], NE * g + u + 1)
                                dve.wait_ge(M["added"], NE * g + u)
                                for t in range(GT):
                                    ins = dve.scalar_tensor_tensor(
                                        out=acc[b][:, t, :], in0=psum[:, 6 + u % 2, t * P:(t + 1) * P],
                                        scalar=gates[b][:, t, u:u + 1], in1=acc[b][:, t, :],
                                        op0=ALU.mult, op1=ALU.add)
                                ins.then_inc(M["added"], 1)
                        dve.wait_ge(M["added"], NE * g + NE)
                        dve.wait_ge(stored[b], 16 * gg)
                        dve.scalar_tensor_tensor(out=res[b][:, :, :], in0=acc[b][:, :, :], scalar=tanh_f[:, 1:2],
                                                 in1=tiles(X[:, g, :]), op0=ALU.mult, op1=ALU.add)\
                           .then_inc(M["res_ready"], 1)
                    count.leave(GROUPS // 2)

            @block.tensor
            def _(pe):
                pe.wait_ge(experts_loaded, 48)
                with pe.Fori(0, GROUPS // 2) as gg:
                    for b in range(2):
                        g = 2 * gg + b
                        pe.wait_ge(M["xn_e"], g + 1)
                        for t in range(GT):
                            mm = pe.transpose(psum[:, 0, t * P:(t + 1) * P], x3[b][:, t, :], ident)
                        mm.then_inc(M["turned_e"], 1)
                        pe.wait_ge(M["xT_e"], g + 1)
                        for t in range(GT):
                            mm = pe.matmul(psum[:, 1, t * NE:(t + 1) * NE], x3T[b][:, t * P:(t + 1) * P],
                                           wt1("wr"), start=True, stop=True)
                        mm.then_inc(M["bias_done"], 1)
                        pe.wait_ge(M["gates_done"], g + 1)
                        for t in range(GT):
                            mm = pe.transpose(psum[0:NE, 1, t * P:(t + 1) * P], gates[b][:, t, :], ident)
                        mm.then_inc(M["g_turned"], 1)
                        pe.wait_ge(M["gT_ready"], g + 1)
                        for t in range(GT):
                            mm = pe.matmul(psum[:, 0, t * P:(t + 1) * P], gT[:, t * P:(t + 1) * P], B2E[:, :],
                                           start=True, stop=True)
                        mm.then_inc(M["bias_done"], 1)
                        for e in range(NE + 1):
                            if e < NE:
                                for c in range(HC):
                                    if c % 2 == 0:
                                        pe.wait_ge(M["relu_act"], 2 * NE * g + (2 * e + c // 2 - 1 if e else 0))
                                    else:
                                        pe.wait_ge(M["relu_dve"], 2 * NE * g + (2 * e + c // 2 - 1 if e else 0))
                                    pe.matmul(psum[:, 2 + c, :], W1E[:, e, c * P:(c + 1) * P], x3T[b][:, :],
                                              start=True, stop=True).then_inc(M["hidden_done"], 1)
                            if e >= 1:
                                u = e - 1
                                pe.wait_ge(M["relu_act"], 2 * NE * g + 2 * u + 2)
                                pe.wait_ge(M["relu_dve"], 2 * NE * g + 2 * u + 2)
                                pe.wait_ge(M["added"], NE * g + max(u - 1, 0))
                                for t in range(GT):
                                    for c in range(HC):
                                        mm = pe.matmul(psum[:, 6 + u % 2, t * P:(t + 1) * P],
                                                       hE[u % 2][:, c, t * P:(t + 1) * P], W2E[:, u, c, :],
                                                       start=(c == 0), stop=(c == HC - 1))
                                mm.then_inc(M["expert_done"], 1)


def kernel(**inputs):
    from concourse import bacc
    from concourse.bass_utils import run_bass_kernel_spmd

    w = {k: np.asarray(v) for k, v in inputs.items()}

    def packed(pieces, width):
        a = np.concatenate([p.reshape(P, -1) for p in pieces], 1)
        assert a.shape == (P, width), a.shape
        return np.ascontiguousarray(a)

    def row(v):
        return np.tile(v.reshape(1, -1), (P, 1))

    def spread(m):
        a = np.zeros((D, H1, 32), m.dtype)
        a[:, :, :S1] = m.reshape(D, H1, S1)
        return a

    params = packed([
        w["L0_xattn_content_bias"], w["L0_xattn_position_bias"], w["L0_ffn_b1"].reshape(HC, P).T,
        w["L1_xattn_pre_g"], w["L1_xattn_pre_b"], w["L1_ffn_b1"].reshape(NE * HC, P).T,
        row(w["L0_ffn_b2"]), row(w["L1_xattn_ln_g"]), row(w["L1_xattn_ln_b"]), row(w["L1_ffn_br"]),
        row(w["L0_ffn_scale"]), row(w["g_xattn"]), row(w["g_ffn"])], PARAM_W)
    weights0 = packed([w["L0_xattn_Wq"], w["L0_xattn_Wkc"], w["L0_xattn_Wkp"], w["L0_xattn_Wv"],
                       w["L0_xattn_positional_encoding"]], WEIGHT0_W)
    weights1 = packed([
        w["L0_xattn_Wo"], w["L0_ffn_W1"].T, w["L0_ffn_W2"].T.reshape(HC, P, D).transpose(1, 0, 2),
        spread(w["L1_xattn_Wq"]), spread(w["L1_xattn_Wk"]), w["L1_xattn_Wv"], w["L1_xattn_Wo"], w["L1_ffn_Wr"]],
        WEIGHT1_W)
    arrays = {
        "x": w["x"], "ctx": w["ctx_1024"], "mask": w["mask_1x1xSx1024_fk0"].reshape(SEQ, KEYS),
        "consts": constants(), "params": params, "weights0": weights0, "weights1": weights1,
        "w1e": w["L1_ffn_W1"].transpose(1, 0, 2), "w2e": w["L1_ffn_W2"].reshape(NE, HC, P, D).transpose(2, 0, 1, 3),
        "b2e": w["L1_ffn_b2"]}
    arrays = {k: np.ascontiguousarray(a) for k, a in arrays.items()}

    nc = bacc.Bacc("TRN2", target_bir_lowering=False, num_devices=1)
    ins = [nc.dram_tensor(k, a.shape, mybir.dt.from_np(a.dtype), kind="ExternalInput").ap()
           for k, a in arrays.items()]
    scratch = [nc.dram_tensor("q_scratch", [PARTS, P, GROUPS, GTOK], BF16, kind="Internal").ap(),
               nc.dram_tensor("k_scratch", [PARTS, P, GROUPS, 2 * GTOK], BF16, kind="Internal").ap(),
               nc.dram_tensor("kp_scratch", [PARTS, P, KEYS], BF16, kind="Internal").ap()]
    out = nc.dram_tensor("out", [NSEQ, SEQ, D], F32, kind="ExternalOutput").ap()
    flamingo_kernel(nc, *ins, *scratch, out)
    r = run_bass_kernel_spmd(nc, [arrays], core_ids=[0])
    return r.results[0]["out"]
```

```python
from contextlib import ExitStack

import numpy as np

import concourse.bass as bass
from concourse import mybir

F32 = mybir.dt.float32
BF16 = mybir.dt.bfloat16
F32R = mybir.dt.float32r
U32 = mybir.dt.uint32
ALU = mybir.AluOpType
ACT = mybir.ActivationFunctionType
AX = mybir.AxisListType.X

P = 128
NSEQ, SEQ, D = 64, 64, 128
TILES = NSEQ * SEQ // P
GROUPS, GT = 8, 4
GN = NSEQ // GROUPS
GTOK = GT * P
NEG_INF = -1.0e9
EPS = 1e-5

H0, S0 = 16, 8
KEYS = 2 * SEQ
BLK = 16
NBLK = NSEQ // BLK
SCALE0 = 1.0 / float(np.sqrt(S0))
PARTS = 3
Q_PARTS = (0, 1, 2, 0, 1, 0)
K_PARTS = (0, 0, 0, 1, 1, 2)
WIN = SEQ - 1 + KEYS + 1
REV = KEYS + 1

H1, S1 = 8, 16
SCALE1 = 1.0 / float(np.sqrt(D))
CLIP = 10000.0

HID = 512
HC = HID // P
NE = 8


def layout(widths):
    at, out = 0, {}
    for name, w in widths:
        out[name] = (at, at + w)
        at += w
    return out, at


CONSTS, CONST_W = layout([
    ("ident", P), ("tokens_of_i", 2 * 512), ("sel_first", GT * 32), ("sel_second", 32),
    ("same_seq", GTOK), ("same_e", 4), ("same_r", P), ("same_seq_tok", 8), ("head_rows", H0), ("iota", NE), ("bias_on", 1), ("minus_upper", 1),
    ("head_of_pair", 2), ("seq_of_tile", 2), ("same_block", 32)])
PARAMS, PARAM_W = layout([
    ("cb", 1), ("pb", 1), ("b1_0", HC), ("pre_g", 1), ("pre_b", 1), ("b1_1", NE * HC),
    ("b2_0", D), ("ln_g", D), ("ln_b", D), ("br", NE), ("scale", 1), ("g_xattn", 2), ("g_ffn", 2)])
WEIGHTS0, WEIGHT0_W = layout([("wq", D), ("wkc", D), ("wkp", D), ("wv", D), ("pe", D)])
WEIGHTS1, WEIGHT1_W = layout([
    ("wo0", D), ("w1t", HID), ("w2t", HID), ("wq1", D), ("wk1", D), ("wv1", D), ("wo1", D), ("wr", NE)])


def constants():
    c = np.zeros((P, CONST_W), np.float32)

    def put(name, a):
        c[:a.shape[0], CONSTS[name][0]:CONSTS[name][0] + a.shape[1]] = a

    p = np.arange(P)[:, None]
    put("ident", np.eye(P))
    i_of = np.repeat(np.arange(SEQ), BLK)[None, :]
    put("tokens_of_i", p % SEQ == i_of)
    col = np.arange(32)[None, :]
    put("sel_first", np.concatenate(
        [(2 * t + p // SEQ == col // 4) & (p % SEQ == 1 + 2 * (col % 4)) for t in range(GT)], 1))
    put("sel_second", (p // SEQ == col // 4 % 2) & (p % SEQ == 9 + 2 * (col % 4)))
    row = np.arange(32)[:, None]
    put("same_seq", row // 4 == np.arange(GTOK)[None, :] // SEQ)
    put("same_e", row % 4 == np.arange(4)[None, :])
    put("same_r", row // 8 == np.arange(P)[None, :] % 4)
    put("same_seq_tok", p // SEQ == np.arange(8)[None, :] // 4)
    put("head_rows", p // S0 == np.arange(H0)[None, :])
    put("bias_on", (p % 64 >= 48) & (p % 64 < 48 + PARTS))
    put("minus_upper", -1.0 * (p >= 64))
    put("head_of_pair", SCALE1 * (p // S1 % 2 == np.arange(2)[None, :]))
    put("same_block", p % 32 == np.arange(32)[None, :])
    put("seq_of_tile", p // SEQ == np.arange(2)[None, :])
    put("iota", np.broadcast_to(np.arange(NE), (P, NE)))
    return c


class Count:

    def __init__(self, eng, sem):
        self.eng, self.sem, self.base, self.it, self.per, self.k = eng, sem, 0, 0, 0, 0

    def enter(self, it, per):
        self.base, self.it, self.per, self.k = self.base + self.k, it, per, 0

    def leave(self, rounds):
        assert self.k == self.per, (self.k, self.per)
        self.base, self.it, self.per, self.k = self.base + rounds * self.per, 0, 0, 0

    def step(self, ins):
        self.k += 1
        ins.then_inc(self.sem, 1)
        self.eng.wait_ge(self.sem, self.base + self.it * self.per + self.k)


def flamingo_kernel(nc, x, ctx_in, mask, consts, params, weights0, weights1, w1e, w2e, b2e,
                    q_scratch, k_scratch, kp_scratch, ot_scratch, st_scratch, out):
    with ExitStack() as ctx:
        def sb(name, shape, dt=F32, stack=ctx):
            return stack.enter_context(nc.sbuf_tensor(name, shape, dt))

        def sem(name):
            return ctx.enter_context(nc.semaphore(name))

        psum = ctx.enter_context(nc.psum_tensor("psum", [P, 8, 512], F32))
        X = sb("X", [P, GROUPS, GTOK])
        C = sb("C", [P, GROUPS, GTOK])
        CST = sb("CST", [P, CONST_W])
        PRM = sb("PRM", [P, PARAM_W])
        WT1 = sb("WT1", [P, WEIGHT1_W])
        O_all = sb("O_all", [P, GROUPS, GTOK])
        sums = sb("sums", [P, GROUPS, GTOK])
        xn = sb("xn", [P, GT, D])
        stats = sb("stats", [P, GT, 6])
        moments = sb("moments", [P, GT, 2])
        rstd = sb("rstd", [P, GT])
        neg_half = sb("neg_half", [P, GT])
        eps_tile = sb("eps_tile", [P, GT])
        tanh_x = sb("tanh_x", [P, 2])
        tanh_f = sb("tanh_f", [P, 2])

        def cst(name, rows=P):
            return CST[0:rows, CONSTS[name][0]:CONSTS[name][1]]

        def prm(name, k=None):
            a, b = PARAMS[name]
            return PRM[:, a:b] if k is None else PRM[:, a + k:a + k + 1]

        def wt1(name):
            return WT1[:, WEIGHTS1[name][0]:WEIGHTS1[name][1]]

        ident = cst("ident")

        passed = sem("passed")

        def carry(eng):
            eng.sem_inc(passed, 1)

        def ln_stats(dve, count, src, ready):
            for t in range(GT):
                ins = dve.bn_stats(stats[:, t, :], src[:, t, :])
                if t == GT - 1:
                    count.step(ins)
            carry(dve)
            for t in range(GT):
                ins = dve.bn_aggr(moments[:, t, :], stats[:, t, :])
            ins.then_inc(ready, 1)

        def ln_rstd(pool, count, done):
            count.step(pool.tensor_tensor(rstd[:, :], moments[:, :, 1], eps_tile[:, :], ALU.add))
            pool.tensor_tensor(rstd[:, :], rstd[:, :], neg_half[:, :], ALU.pow).then_inc(done, 1)

        def ln_apply(dve, dst, src):
            for t in range(GT):
                ins = dve.tensor_scalar(dst[:, t, :], src[:, t, :], moments[:, t, 0:1], rstd[:, t:t + 1],
                                        ALU.subtract, ALU.mult)
            return ins

        def tiles(ap):
            return ap.rearrange("p (t c) -> p t c", t=GT)

        heads_ctx = ExitStack()
        V_all = sb("V_all", [P, NSEQ, H0, S0 + 1], stack=heads_ctx)
        kp_stack = sb("kp_stack", [P, H0, WIN], BF16, heads_ctx)
        proj_ctx = ExitStack()
        WT0 = sb("WT0", [P, WEIGHT0_W], stack=proj_ctx)
        c_now = sb("c_now", [P, GT, D], stack=proj_ctx)
        refT = sb("refT", [P, GN, KEYS], stack=proj_ctx)
        qz = sb("qz", [P, GTOK], stack=proj_ctx)
        qr = sb("qr", [P, GTOK], stack=proj_ctx)
        kr = sb("kr", [P, 2 * GTOK], stack=proj_ctx)
        q_part = sb("q_part", [P, PARTS, GTOK], BF16, proj_ctx)
        k_part = sb("k_part", [P, PARTS, 2 * GTOK], BF16, proj_ctx)
        peT = sb("peT", [P, KEYS], stack=proj_ctx)
        kpT = sb("kpT", [P, KEYS], stack=proj_ctx)
        kp_r = sb("kp_r", [P, KEYS], stack=proj_ctx)
        kp_part = sb("kp_part", [P, PARTS, KEYS], BF16, proj_ctx)
        bias_rows = sb("bias_rows", [P, H0], stack=proj_ctx)
        bias_diff = sb("bias_diff", [P, 1], stack=proj_ctx)
        bp = sb("bp", [H0, KEYS], stack=proj_ctx)
        bp_part = sb("bp_part", [H0, PARTS, KEYS], BF16, proj_ctx)

        def wt0(name):
            return WT0[:, WEIGHTS0[name][0]:WEIGHTS0[name][1]]

        loaded = sem("loaded")
        x_loaded = sem("x_loaded")
        dve_p = sem("dve_p")
        pool_p = sem("pool_p")
        half_set = sem("half_set")
        stats_p = sem("stats_p")
        rstd_p = sem("rstd_p")
        xn_p = sem("xn_p")
        pe_turned = sem("pe_turned")
        peT_ready = sem("peT_ready")
        kp_done = sem("kp_done")
        kpT_ready = sem("kpT_ready")
        bias_ready = sem("bias_ready")
        bp_done = sem("bp_done")
        kp_split = sem("kp_split")
        kp_stored = sem("kp_stored")
        stack_zero = sem("stack_zero")
        kp_stacked = sem("kp_stacked")
        turned_p = sem("turned_p")
        c_staged = sem("c_staged")
        loaded1 = sem("loaded1")
        refx_ready = sem("refx_ready")
        refc_ready = sem("refc_ready")
        q_done = sem("q_done")
        k_done = sem("k_done")
        v_done = sem("v_done")
        qz_ready = sem("qz_ready")
        q_first = sem("q_first")
        qr_ready = sem("qr_ready")
        q_second = sem("q_second")
        q_third = sem("q_third")
        k_first = sem("k_first")
        kr_ready = sem("kr_ready")
        k_second = sem("k_second")
        k_third = sem("k_third")
        v_kept = sem("v_kept")
        q_stored = sem("q_stored")
        k_stored = sem("k_stored")
        gates_ready = sem("gates_ready")
        T_x, T_c, Q_ps = psum[:, 0, :], psum[:, 1, :], psum[:, 2, :]
        K_ps, V_ps = psum[:, 3:5, :], psum[:, 5:7, :]

        with nc.Block() as block:
            @block.sync
            def _(sp):
                sp.dma_start(PRM[:, :], params).then_inc(loaded, 16)
                sp.dma_start(CST[:, :], consts).then_inc(loaded, 16)
                sp.dma_start(WT0[:, :], weights0).then_inc(loaded, 16)
                xv = x.rearrange("(g t m) s d -> (m s) g t d", t=GT, m=2)
                cv = ctx_in.rearrange("(g t m) s d -> (m s) g t d", t=GT, m=2)
                for g in range(GROUPS):
                    sp.dma_start(tiles(X[:, g, :]), xv[:, g]).then_inc(x_loaded, 16)
                    sp.dma_start(tiles(C[:, g, :]), cv[:, g]).then_inc(x_loaded, 16)
                sp.dma_start(WT1[:, :], weights1).then_inc(loaded1, 16)
                sp.wait_ge(kp_split, 1)
                sp.dma_start(kp_scratch.rearrange("a p r -> p a r"), kp_part[:, :, :]).then_inc(kp_stored, 16)
                sp.wait_ge(kp_stored, 16)
                sp.wait_ge(stack_zero, 1)
                kv = kp_scratch.rearrange("a (h s) r -> a s h r", s=S0)
                for half, at in ((0, 0), (64, REV)):
                    w = min(KEYS, WIN - at)
                    for row, part in enumerate(K_PARTS):
                        sp.dma_start(kp_stack[half + S0 * row:half + S0 * (row + 1), :, at:at + w],
                                     kv[part, :, :, 0:w]).then_inc(kp_stacked, 16)
                    for part in range(PARTS):
                        sp.dma_start(kp_stack[half + 48 + part:half + 49 + part, :, at:at + w],
                                     bp_part[:, part, 0:w]).then_inc(kp_stacked, 16)
                with sp.Fori(0, GROUPS) as g:
                    sp.wait_ge(q_third, g + 1)
                    for c, part in enumerate(Q_PARTS):
                        sp.dma_start(q_scratch[:, c, :, g, :], q_part[:, part, :]).then_inc(q_stored, 16)
                    sp.wait_ge(k_third, g + 1)
                    for c, part in enumerate(K_PARTS):
                        sp.dma_start(k_scratch[:, c, :, g, :], k_part[:, part, :]).then_inc(k_stored, 16)
                sp.wait_ge(q_stored, 16 * 6 * GROUPS)
                sp.wait_ge(k_stored, 16 * 6 * GROUPS)
                sp.wait_ge(kp_stacked, 16 * 18)
                sp.wait_ge(loaded1, 16)

            @block.gpsimd
            def _(pool):
                count = Count(pool, pool_p)
                pool.memset(neg_half[:, :], -0.5).then_inc(half_set, 1)
                pool.memset(eps_tile[:, :], EPS).then_inc(half_set, 1)
                pool.wait_ge(half_set, 2)
                pool.memset(kp_stack[:, :, :], 0.0).then_inc(stack_zero, 1)
                pool.memset(V_all[:, :, :, :], 1.0).then_inc(v_kept, 1)
                pool.wait_ge(x_loaded, 32 * GROUPS)
                with pool.Fori(0, GROUPS) as g:
                    count.enter(g, 1)
                    pool.wait_ge(turned_p, 2 * g)
                    pool.tensor_copy(c_now[:, :, :], tiles(C[:, g, :])).then_inc(c_staged, 1)
                    pool.wait_ge(stats_p, g + 1)
                    ln_rstd(pool, count, rstd_p)
                    pool.wait_ge(q_second, g + 1)
                    pool.tensor_tensor(q_part[:, 2, :], qr[:, :], q_part[:, 1, :], ALU.subtract)\
                        .then_inc(q_third, 1)
                    pool.wait_ge(k_second, g + 1)
                    pool.tensor_tensor(k_part[:, 2, :], kr[:, :], k_part[:, 1, :], ALU.subtract)\
                        .then_inc(k_third, 1)
                    count.leave(GROUPS)

            @block.scalar
            def _(act):
                act.wait_ge(loaded, 48)
                act.activation(tanh_x[:, :], prm("g_xattn"), ACT.Tanh).then_inc(gates_ready, 1)
                act.activation(tanh_f[:, :], prm("g_ffn"), ACT.Tanh).then_inc(gates_ready, 1)
                with act.Fori(0, GROUPS) as g:
                    act.wait_ge(turned_p, 2 * g + 2)
                    act.wait_ge(v_done, g)
                    act.activation(refT[:, :, 0:SEQ], T_c.rearrange("p (n i) -> p n i", n=GN), ACT.Copy)\
                        .then_inc(refc_ready, 1)
                    act.wait_ge(qz_ready, g + 1)
                    act.wait_ge(q_stored, 16 * 6 * g)
                    act.activation(q_part[:, 0, :], qz[:, :], ACT.Copy).then_inc(q_first, 1)
                    act.wait_ge(k_done, g + 1)
                    act.wait_ge(k_stored, 16 * 6 * g)
                    act.activation(k_part[:, 0, :], K_ps.rearrange("p a b -> p (a b)"), ACT.Copy)\
                        .then_inc(k_first, 1)
                    act.wait_ge(qr_ready, g + 1)
                    act.activation(q_part[:, 1, :], qr[:, :], ACT.Copy).then_inc(q_second, 1)
                    act.wait_ge(kr_ready, g + 1)
                    act.activation(k_part[:, 1, :], kr[:, :], ACT.Copy).then_inc(k_second, 1)

            @block.vector
            def _(dve):
                count = Count(dve, dve_p)
                dve.wait_ge(loaded, 48)
                dve.wait_ge(pe_turned, 1)
                dve.tensor_copy(peT[:, :], T_x[:, 0:P]).then_inc(peT_ready, 1)
                count.step(dve.tensor_tensor(bias_diff[:, :], prm("pb"), prm("cb"), ALU.subtract))
                dve.tensor_scalar(bias_rows[:, :], cst("head_rows"), bias_diff[:, :], SCALE0,
                                  ALU.mult, ALU.mult).then_inc(bias_ready, 1)
                dve.wait_ge(kp_done, 1)
                dve.tensor_copy(kpT[:, :], T_c[:, 0:P]).then_inc(kpT_ready, 1)
                dve.wait_ge(kpT_ready, 1)

                def split(src, rest, part):
                    count.step(dve.tensor_copy(part[:, 0, :], src))
                    count.step(dve.tensor_tensor(rest, src, part[:, 0, :], ALU.subtract))
                    count.step(dve.tensor_copy(part[:, 1, :], rest))
                    return dve.tensor_tensor(part[:, 2, :], rest, part[:, 1, :], ALU.subtract)

                count.step(split(kpT[:, :], kp_r[:, :], kp_part))
                dve.wait_ge(bp_done, 1)
                count.step(dve.tensor_copy(bp[:, :], Q_ps[0:H0, 0:KEYS]))
                split(bp[:, :], kp_r[0:H0, :], bp_part).then_inc(kp_split, 1)
                dve.wait_ge(x_loaded, 32 * GROUPS)
                with dve.Fori(0, GROUPS) as g:
                    count.enter(g, 1)
                    ln_stats(dve, count, tiles(X[:, g, :]), stats_p)
                    dve.wait_ge(stats_p, g + 1)
                    dve.wait_ge(rstd_p, g + 1)
                    dve.wait_ge(turned_p, 2 * g)
                    ln_apply(dve, xn, tiles(X[:, g, :])).then_inc(xn_p, 1)
                    dve.wait_ge(turned_p, 2 * g + 1)
                    dve.wait_ge(v_done, g)
                    dve.tensor_copy(refT[:, :, SEQ:KEYS], T_x.rearrange("p (n i) -> p n i", n=GN))\
                       .then_inc(refx_ready, 1)
                    dve.wait_ge(q_done, g + 1)
                    dve.wait_ge(q_first, g)
                    dve.tensor_scalar(qz[:, :], Q_ps, prm("cb"), SCALE0, ALU.add, ALU.mult)\
                       .then_inc(qz_ready, 1)
                    dve.wait_ge(q_first, g + 1)
                    dve.wait_ge(q_third, g)
                    dve.tensor_tensor(qr[:, :], qz[:, :], q_part[:, 0, :], ALU.subtract).then_inc(qr_ready, 1)
                    dve.wait_ge(k_first, g + 1)
                    dve.wait_ge(k_third, g)
                    dve.tensor_tensor(kr[:, :], K_ps.rearrange("p a b -> p (a b)"), k_part[:, 0, :],
                                      ALU.subtract).then_inc(kr_ready, 1)
                    dve.wait_ge(v_done, g + 1)
                    dve.wait_ge(v_kept, 1)
                    dve.tensor_copy(
                        V_all[:, :, :, :].rearrange("p (g n) h s -> p g n h s", n=GN)[:, g, :, :, 0:S0]
                        .rearrange("p n h s -> p (n h) s"),
                        V_ps.rearrange("p a (n h s) -> p (a n h) s", h=H0, s=S0)).then_inc(v_kept, 1)
                    count.leave(GROUPS)

            @block.tensor
            def _(pe):
                pe.wait_ge(loaded, 48)
                pe.transpose(T_x[:, 0:P], wt0("pe"), ident).then_inc(pe_turned, 1)
                pe.wait_ge(peT_ready, 1)
                pe.matmul(T_c[:, 0:P], wt0("wkp"), peT[:, :], start=True, stop=True).then_inc(kp_done, 1)
                pe.wait_ge(kpT_ready, 1)
                pe.wait_ge(bias_ready, 1)
                pe.matmul(Q_ps[0:H0, 0:KEYS], bias_rows[:, :], kpT[:, :], start=True, stop=True)\
                  .then_inc(bp_done, 1)
                pe.wait_ge(kp_split, 1)
                with pe.Fori(0, GROUPS) as g:
                    pe.wait_ge(xn_p, g + 1)
                    pe.wait_ge(refx_ready, g)
                    for t in range(GT):
                        mm = pe.transpose(T_x[:, t * P:(t + 1) * P], xn[:, t, :], ident)
                    mm.then_inc(turned_p, 1)
                    pe.wait_ge(refc_ready, g)
                    pe.wait_ge(c_staged, g + 1)
                    for t in range(GT):
                        mm = pe.transpose(T_c[:, t * P:(t + 1) * P], c_now[:, t, :], ident)
                    mm.then_inc(turned_p, 1)
                    pe.wait_ge(refx_ready, g + 1)
                    pe.wait_ge(qz_ready, g)
                    pe.matmul(Q_ps, wt0("wq"), refT[:, :, SEQ:KEYS], start=True, stop=True).then_inc(q_done, 1)
                    pe.wait_ge(refc_ready, g + 1)
                    pe.wait_ge(kr_ready, g)
                    for a in range(2):
                        mm = pe.matmul(K_ps[:, a, :], wt0("wkc"), refT[:, a * 4:a * 4 + 4, :],
                                       start=True, stop=True)
                    mm.then_inc(k_done, 1)
                    pe.wait_ge(v_kept, g + 1)
                    for n in range(GN):
                        mm = pe.matmul(V_ps[:, n // 4, (n % 4) * P:(n % 4 + 1) * P], refT[:, n, :],
                                       wt0("wv"), start=True, stop=True)
                    mm.then_inc(v_done, 1)

        proj_ctx.close()

        att_ctx = ExitStack()
        UTOK = BLK * SEQ
        UNITS = H0 * NBLK
        ROUND = 3 * NBLK
        ROUNDS = UNITS // ROUND
        q_stack = [sb(f"q_stack{b}", [P, UTOK], BF16, att_ctx) for b in range(3)]
        k_stack = [sb(f"k_stack{b}", [64, BLK * KEYS], BF16, att_ctx) for b in range(3)]
        window = [sb(f"window{b}", [P, WIN], BF16, att_ctx) for b in range(3)]
        probs = [sb(f"probs{b}", [P, UTOK], stack=att_ctx) for b in range(2)]
        max_rows = [sb(f"max_rows{b}", [32 * PARTS, UTOK], BF16, att_ctx) for b in range(2)]
        max_quads = [sb(f"max_quads{b}", [P, 32], stack=att_ctx) for b in range(2)]
        neg_max = sb("neg_max", [32, 32], stack=att_ctx)
        max_rest = sb("max_rest", [32, 32], stack=att_ctx)
        max_mid = sb("max_mid", [32, 32], BF16, att_ctx)
        max_part = sb("max_part", [32 * PARTS, 32], BF16, att_ctx)
        same_block = sb("same_block", [32 * PARTS, 32], BF16, att_ctx)
        ones_rows = sb("ones_rows", [32 * PARTS, P], BF16, att_ctx)
        v_now = [sb(f"v_now{b}", [P, BLK, S0 + 1], stack=att_ctx) for b in range(2)]
        o_sum = [sb(f"o_sum{b}", [P, UTOK], stack=att_ctx) for b in range(2)]
        mask_sb = sb("mask_sb", [P, KEYS], stack=att_ctx)
        neg_mask = sb("neg_mask", [P, KEYS], stack=att_ctx)
        mask_high = sb("mask_high", [P, KEYS], F32R, att_ctx)
        mask2 = sb("mask2", [P, KEYS], F32R, att_ctx)
        tokens2 = sb("tokens2", [P, UTOK], F32R, att_ctx)
        stack_set = sem("stack_set")
        mask_loaded = sem("mask_loaded")
        mask_ready = sem("mask_ready")
        unit_loaded = [sem(f"unit_loaded{b}") for b in range(3)]
        window_ready = sem("window_ready")
        scored = sem("scored")
        quads_ready = sem("quads_ready")
        quads_turned = sem("quads_turned")
        max_ready = sem("max_ready")
        rows_ready = sem("rows_ready")
        shifted = sem("shifted")
        exp_done = sem("exp_done")
        values_done = sem("values_done")
        dve_a = sem("dve_a")
        v_staged = sem("v_staged")
        o_copied = sem("o_copied")
        o_moved = [sem(f"o_moved{b}") for b in range(2)]
        S_ps = [psum[:, 2 * b:2 * b + 2, :] for b in range(3)]
        R_ps = psum[0:32, 6, 0:P]
        o_rows = [slice(32 * (b + 1), 32 * (b + 1) + S0 + 1) for b in range(2)]
        O_ps = [psum[o_rows[b], 6:8, :] for b in range(2)]
        qv = q_scratch.rearrange("h c s g t -> h (c s) (g t)")
        kv = k_scratch.rearrange("h c s g t -> h (c s) (g t)")

        def is_unit(it, k):
            return not isinstance(it, int) or 0 <= ROUND * it + k < UNITS

        def head_of(it, k):
            return (ROUND // NBLK) * it + k // NBLK

        def wait_units(eng, sem, it, k, per=1, of=1):
            done = per * ((ROUND // of) * it + (k - 1) // of + 1)
            if not isinstance(done, int) or done > 0:
                eng.wait_ge(sem, done)

        def run_steps(eng, step, rounds=ROUNDS, count=None, per=0):
            for k in range(-3, 1):
                step(0, k)
            with eng.Fori(0, rounds) as it:
                if count:
                    count.enter(it, per)
                for k in range(1, ROUND + 1):
                    step(it, k)
                if count:
                    count.leave(rounds)
            for k in range(1, UNITS - ROUND * rounds):
                step(rounds, k)

        with nc.Block() as block:
            @block.sync
            def _(sp):
                for m in range(2):
                    sp.dma_start(mask_sb[64 * m:64 * m + 64, :], mask).then_inc(mask_loaded, 16)
                sp.wait_ge(stack_set, 6)

                def load_unit(it, k):
                    h, blk, b = head_of(it, k), k % NBLK, k % 3
                    for half, shift in ((0, 0), (64, 1)):
                        sp.dma_start(q_stack[b][half:half + 48, 0:UTOK - shift],
                                     qv[h, :, blk * UTOK + shift:(blk + 1) * UTOK]).then_inc(unit_loaded[b], 16)
                    sp.dma_start(k_stack[b][0:48, :], kv[h, :, blk * 2 * UTOK:(blk + 1) * 2 * UTOK])\
                      .then_inc(unit_loaded[b], 16)

                for n in range(3):
                    load_unit(0, n)

                def step(it, k):
                    if is_unit(it, k):
                        b, h, blk = k % 2, head_of(it, k), k % NBLK
                        wait_units(sp, o_copied, it, k + 1)
                        carry(sp)
                        at, rows = blk * UTOK, o_rows[b]
                        sp.dma_start(ot_scratch[h, :, at:at + UTOK], o_sum[b][rows.start:rows.start + S0, :])                          .then_inc(o_moved[b], 16)
                        sp.dma_start(st_scratch[h, :, at:at + UTOK], o_sum[b][rows.stop - 1:rows.stop, :])                          .then_inc(o_moved[b], 16)
                    if is_unit(it, k + 6):
                        wait_units(sp, scored, it, k + 4)
                        carry(sp)
                        load_unit(it, k + 6)

                run_steps(sp, step, ROUNDS - 1)
                for b in range(2):
                    sp.wait_ge(o_moved[b], 32 * UNITS // 2)

            @block.gpsimd
            def _(pool):
                for b in range(3):
                    pool.memset(k_stack[b][:, :], 0.0).then_inc(stack_set, 1)

                vv = V_all[:, :, :, :].rearrange("p (b n) h s -> p b n h s", b=NBLK)

                def step(it, k):
                    if is_unit(it, k + 3) and (k + 3) % NBLK == 0:
                        wait_units(pool, scored, it, k + 2)
                        carry(pool)
                        pool.tensor_copy(window[(k + 3) // NBLK % 3][:, :], kp_stack[:, head_of(it, k + 3), :])                            .then_inc(window_ready, 1)
                    if is_unit(it, k + 1):
                        wait_units(pool, values_done, it, k)
                        carry(pool)
                        pool.tensor_copy(v_now[(k + 1) % 2][:, :, :], vv[:, (k + 1) % NBLK, :, head_of(it, k + 1), :])                            .then_inc(v_staged, 1)

                run_steps(pool, step)

            @block.scalar
            def _(act):
                def step(it, k):
                    if is_unit(it, k):
                        b = k % 2
                        wait_units(act, values_done, it, k + 1)
                        wait_units(act, o_moved[b], it, k - 1, 32, 2)
                        act.activation(o_sum[b][o_rows[b], :].rearrange("p (a c) -> p a c", a=2), O_ps[b], ACT.Copy)\
                           .then_inc(o_copied, 1)
                    if is_unit(it, k + 1):
                        wait_units(act, shifted, it, k + 2)
                        wait_units(act, values_done, it, k)
                        act.activation(probs[(k + 1) % 2][:, :].rearrange("p (n i) -> p i n", n=BLK),
                                       S_ps[(k + 1) % 3].rearrange("p a (i n) -> p (a i) n", n=BLK), ACT.Exp)\
                           .then_inc(exp_done, 1)

                run_steps(act, step)

            @block.vector
            def _(dve):
                count = Count(dve, dve_a)
                for b in range(3):
                    dve.tensor_copy(q_stack[b][:, :], cst("bias_on").broadcast_to([P, UTOK])).then_inc(stack_set, 1)
                dve.memset(ones_rows[:, :], 1.0)
                count.step(dve.tensor_copy(same_block[:, :], cst("same_block", 32 * PARTS)))
                dve.tensor_copy(tokens2[:, :], cst("tokens_of_i")).then_inc(mask_ready, 1)
                dve.wait_ge(mask_loaded, 32)
                count.step(dve.tensor_scalar(neg_mask[:, :], mask_sb[:, :], NEG_INF, None, ALU.mult))
                count.step(dve.tensor_copy(mask_high[:, :], neg_mask[:, :]))
                dve.scalar_tensor_tensor(out=mask2[:, :], in0=mask_high[:, :].bitcast(F32), scalar=cst("minus_upper"),
                                         in1=neg_mask[:, :], op0=ALU.mult, op1=ALU.add).then_inc(mask_ready, 1)

                def step(it, k):
                    if is_unit(it, k + 2):
                        wait_units(dve, quads_turned, it, k + 3)
                        count.step(dve.tensor_reduce(neg_max[:, :], R_ps.rearrange("p (q c) -> p c q", q=4), AX,
                                                     ALU.max, negate=True))
                        count.step(dve.tensor_copy(max_part[0:32, :], neg_max[:, :]))
                        count.step(dve.tensor_tensor(max_rest[:, :], neg_max[:, :], max_part[0:32, :], ALU.subtract))
                        dve.tensor_copy(max_part[32:64, :], max_rest[:, :])
                        count.step(dve.tensor_copy(max_mid[:, :], max_rest[:, :]))
                        dve.tensor_tensor(max_part[64:96, :], max_rest[:, :], max_mid[:, :], ALU.subtract)\
                           .then_inc(max_ready, 1)
                        wait_units(dve, max_ready, it, k + 3)
                        wait_units(dve, shifted, it, k + 1)
                        dve.tensor_tensor(
                            max_rows[k % 2][:, :].rearrange("p (b c) -> p b c", c=32),
                            max_part[:, :].rearrange("p (o c) -> p o c", o=1).broadcast_to([32 * PARTS, 32, 32]),
                            same_block[:, :].rearrange("p (b o) -> p b o", o=1).broadcast_to([32 * PARTS, 32, 32]),
                            ALU.mult).then_inc(rows_ready, 1)
                    if is_unit(it, k + 3):
                        wait_units(dve, scored, it, k + 4)
                        dve.tensor_reduce(max_quads[(k + 3) % 2][:, :],
                                          S_ps[(k + 3) % 3].rearrange("p a (b c) -> p (a b) c", c=32), AX, ALU.max,
                                          apply_transpose=True).then_inc(quads_ready, 1)

                run_steps(dve, step, count=count, per=4 * ROUND)

            @block.tensor
            def _(pe):
                pe.wait_ge(mask_ready, 2)
                pe.wait_ge(stack_set, 6)

                def content(it, k, part):
                    b = k % 3
                    sv = S_ps[b].rearrange("p a (i n) -> p a i n", n=BLK)
                    qn = q_stack[b][0:64, :].rearrange("p (n a i) -> p n a i", n=BLK, a=2)
                    if part == 0:
                        wait_units(pe, exp_done, it, k - 2)
                        for a in range(2):
                            pe.matmul(S_ps[b][:, a, :], mask2[:, :], tokens2[:, 512 * a:512 * a + 512],
                                      start=True, stop=False, skip_group_check=True)
                        wait_units(pe, unit_loaded[b], it, k + 1, 48, 3)
                    for n in range(part * BLK // 2, (part + 1) * BLK // 2):
                        for a in range(2):
                            pe.matmul(sv[:, a, :, n], k_stack[b][:, n * KEYS:(n + 1) * KEYS], qn[:, n, a, :],
                                      start=False, stop=False, skip_group_check=True)

                def positions(it, k):
                    b, wnd = k % 3, window[k // NBLK % 3]
                    sv = S_ps[b].rearrange("p a (i n) -> p a i n", n=BLK)
                    qi = q_stack[b][:, :].rearrange("p (n i) -> p i n", n=BLK)
                    if k % NBLK == 0:
                        pe.wait_ge(window_ready, head_of(it, k) + 1)
                    for i in range(SEQ):
                        mm = pe.matmul(sv[:, i // 32, i % 32, :], wnd[:, SEQ - 1 - i:SEQ - 1 - i + KEYS], qi[:, i, :],
                                       start=False, stop=False, skip_group_check=True)
                    mm.then_inc(scored, 1)

                def step(it, k):
                    if is_unit(it, k):
                        b = k % 2
                        wait_units(pe, v_staged, it, k + 1)
                        wait_units(pe, exp_done, it, k + 1)
                        wait_units(pe, o_copied, it, k - 1)
                        for n in range(BLK):
                            mm = pe.matmul(O_ps[b][:, n // 8, n % 8 * SEQ:(n % 8 + 1) * SEQ], v_now[b][:, n, :],
                                           probs[b][:, n * SEQ:(n + 1) * SEQ], start=True, stop=True,
                                           tile_position=(0, 32 * (b + 1)))
                        mm.then_inc(values_done, 1)
                    if is_unit(it, k + 3):
                        content(it, k + 3, 0)
                    if is_unit(it, k + 2):
                        wait_units(pe, quads_ready, it, k + 3)
                        wait_units(pe, max_ready, it, k + 2)
                        pe.transpose(R_ps, max_quads[k % 2][:, :], ident).then_inc(quads_turned, 1)
                    if is_unit(it, k + 3):
                        content(it, k + 3, 1)
                    if is_unit(it, k + 1):
                        wait_units(pe, rows_ready, it, k + 2)
                        for a in range(2):
                            mm = pe.matmul(S_ps[(k + 1) % 3][:, a, :], ones_rows[:, :],
                                           max_rows[(k + 1) % 2][:, 512 * a:512 * a + 512],
                                           start=False, stop=True, skip_group_check=True)
                        mm.then_inc(shifted, 1)
                    if is_unit(it, k + 3):
                        positions(it, k + 3)

                run_steps(pe, step)
        att_ctx.close()
        heads_ctx.close()

        W1E = sb("W1E", [P, NE, HID])
        W2E = sb("W2E", [P, NE, HC, D])
        B2E = sb("B2E", [NE, D])
        experts_loaded = sem("experts_loaded")

        R = {name: sem(name) for name in (
            "first_loaded o_loaded oT_ready y_done x1_ready stats_r rstd_r dve_r pool_r xn_ready x_turned xT_ready "
            "even1_picked even2_picked odd_ready up_done up_ready even1_ready even2_ready h_done h_ready low_done "
            "low_ready low_turned lowT_ready ffn_done "
            "c_staged1 c_turned cT_ready cn_ready cn_turned knT_ready k_done1 k_ready1 v_done1 v_ready1 "
            "xm_ready xm_turned qnT_ready q_done1 q_ready1 scored1 clipped s_ready e_ready summed e_turned eT_ready o_done1 "
            "o_ready1 on_ready on_turned onT_ready gate_done gelu_ready "
            "x3_ready x3_turned x3T_ready logits_done routed second_ready gates_done g_turned gT_ready bias_done "
            "acc_ready hidden_done relu_done expert_done added res_ready").split()}
        stored = [sem(f"stored{b}") for b in range(2)]
        oT = sb("oT", [P, GTOK])
        x1 = sb("x1", [P, GT, D])
        xT = sb("xT", [P, GTOK])
        odd1 = sb("odd1", [P, GN, 4])
        odd2 = sb("odd2", [P, GN, 4])
        even1 = sb("even1", [32, 4, P])
        picked2 = sb("picked2", [32, GT, 32])
        even2 = sb("even2", [32, GT, 4, 32])
        hT = sb("hT", [P, HC, GTOK])
        low = sb("low", [P, GT * HC, 8])
        c2 = sb("c2", [P, GT, D])
        cn = sb("cn", [P, GT, D])
        knT = sb("knT", [P, GTOK])
        cT = sb("cT", [P, GTOK])
        up, masked2, lowT, fin = knT[0:32, :], cT[0:32, :], cT[0:32, :], cn
        k1 = [sb(f"k1_{b}", [P, GTOK]) for b in range(2)]
        v1 = [sb(f"v1_{b}", [P, GT * 4, 2, 2 * S1]) for b in range(2)]
        xm = sb("xm", [P, GT, D])
        qnT = sb("qnT", [P, GTOK])
        q1 = sb("q1", [P, GN, 2, SEQ])
        s1 = sb("s1", [P, 4, GTOK])
        top1 = sb("top1", [P, 4 * GN])
        sum1 = sb("sum1", [P, 4 * GN])
        inv1 = sb("inv1", [P, 4 * GN])
        on = sb("on", [P, GT, D])
        gl = sb("gl", [P, GT, D])
        o1, onT, x3 = xm, qnT, gl
        x3T = [sb(f"x3T_{b}", [P, GTOK]) for b in range(2)]
        logits = sb("logits", [P, GT, NE])
        best = sb("best", [P, GT, NE])
        place = sb("place", [P, GT, NE], U32)
        placef = sb("placef", [P, GT, NE])
        second = sb("second", [P, GT])
        both = sb("both", [P, GT])
        weight = sb("weight", [P, 2, GT])
        pick = sb("pick", [P, 2, GT, NE])
        gates = [sb(f"gates{b}", [P, GT, NE]) for b in range(2)]
        gT = sb("gT", [NE, GTOK])
        hE = [sb(f"hE{b}", [P, HC, GTOK]) for b in range(2)]
        acc = [sb(f"acc{b}", [P, GT, D]) for b in range(2)]
        ov = out.rearrange("(g t m) s d -> (m s) g t d", t=GT, m=2)
        bank = [psum[:, n, :] for n in range(8)]
        AHEAD = {"relu_done": 2, "expert_done": 2, "added": 1}
        LOWER_AT = {0: 0, 1: 1, 2: 3, 3: 6, 4: 8, 5: 10, 6: 12, 7: 14, 8: 16, 9: 21, 10: 23}
        UPPER_AT = {0: 0, 1: 2, 2: 3, 3: 4, 4: 7, 5: 8, 6: 9, 7: 10, 8: 12, 9: 15, 10: 17, 11: 19, 12: 20,
                    13: 22, 14: 24}
        before = {}

        def half_before(g, b):
            return (g - b) // 2 if isinstance(g, int) else before[b]

        def since(eng, name, value):
            if not isinstance(value, int) or value > 0:
                eng.wait_ge(R[name], value + AHEAD.get(name, 0))

        def over_rounds(eng, lower, upper, experts, counts=()):
            def a_round(g_lower, g_upper, g_experts, b):
                low_at = {at: s for s, at in LOWER_AT.items()}
                up_at = {at: s for s, at in UPPER_AT.items()}
                for slot in range(3 * (NE + 1)):
                    if g_experts is not None:
                        experts(g_experts, b, slot // 3, slot % 3)
                    if g_lower is not None and slot in low_at:
                        lower(low_at[slot], g_lower, b)
                    if g_upper is not None and slot in up_at:
                        upper(up_at[slot], g_upper, 1 - b)

            a_round(0, None, None, 0)
            a_round(1, 0, None, 1)
            with eng.Fori(0, GROUPS // 2 - 1) as i:
                for count, per in counts:
                    count.enter(i, per)
                before[0], before[1] = i + 1, i
                a_round(2 * i + 2, 2 * i + 1, 2 * i, 0)
                a_round(2 * i + 3, 2 * i + 2, 2 * i + 1, 1)
                for count, per in counts:
                    count.leave(GROUPS // 2 - 1)
            a_round(None, GROUPS - 1, GROUPS - 2, 0)
            a_round(None, None, GROUPS - 1, 1)

        with nc.Block() as block:
            @block.sync
            def _(sp):
                def load_group(g, sem):
                    cols = slice(g * GTOK, (g + 1) * GTOK)
                    for h in range(H0):
                        sp.dma_start(sums[S0 * h:S0 * h + S0, g, :], st_scratch[h, :, cols].broadcast_to([S0, GTOK]))\
                          .then_inc(sem, 16)
                    sp.dma_start(O_all[:, g, :], ot_scratch.rearrange("h s t -> (h s) t")[:, cols]).then_inc(sem, 16)

                sp.sem_inc(stored[1], 16)
                load_group(0, R["first_loaded"])
                for h in range(H0):
                    sp.dma_start(sums[S0 * h:S0 * h + S0, 1:GROUPS, :].rearrange("p g t -> p (g t)"),
                                 st_scratch[h, :, GTOK:].broadcast_to([S0, (GROUPS - 1) * GTOK]))\
                      .then_inc(R["o_loaded"], 16)
                sp.dma_start(O_all[:, 1:GROUPS, :].rearrange("p g t -> p (g t)"),
                             ot_scratch.rearrange("h s t -> (h s) t")[:, GTOK:]).then_inc(R["o_loaded"], 16)
                sp.dma_start(W1E[:, :, :], w1e).then_inc(experts_loaded, 16)
                sp.dma_start(W2E[:, :, :, :], w2e).then_inc(experts_loaded, 16)
                sp.dma_start(B2E[:, :], b2e).then_inc(experts_loaded, 16)
                with sp.Fori(0, GROUPS // 2) as i:
                    for b in range(2):
                        sp.wait_ge(R["res_ready"], 2 * i + b + 1)
                        sp.dma_start(ov[:, 2 * i + b, :, :], acc[b][:, :, :]).then_inc(stored[b], 16)
                for b in range(2):
                    sp.wait_ge(stored[b], 16 * (GROUPS // 2 + b))

            @block.gpsimd
            def _(pool):
                count = Count(pool, R["pool_r"])

                def stage(g):
                    since(pool, "c_turned", g)
                    since(pool, "cn_ready", g)
                    carry(pool)
                    pool.tensor_copy(c2[:, :, :], tiles(C[:, g, :])).then_inc(R["c_staged1"], 1)

                def norms(first, n):
                    for k in range(n):
                        pool.wait_ge(R["stats_r"], first + k + 1)
                        ln_rstd(pool, count, R["rstd_r"])

                stage(0)
                norms(0, 1)
                stage(1)
                norms(1, 3)
                with pool.Fori(1, GROUPS - 1) as g:
                    count.enter(g - 1, 6)
                    norms(6 * g - 2, 3)
                    stage(g + 1)
                    norms(6 * g + 1, 3)
                    count.leave(GROUPS - 2)
                norms(6 * GROUPS - 8, 6)
                norms(6 * GROUPS - 2, 2)

            @block.scalar
            def _(act):
                act.sem_inc(R["relu_done"], AHEAD["relu_done"])

                def copy(dst, src, need, ready, n, **kw):
                    act.wait_ge(R[need], n)
                    act.activation(dst, src, kw.pop("func", ACT.Copy), **kw).then_inc(R[ready], 1)

                affine = dict(func=ACT.Identity, bias=prm("pre_b"), scale=prm("pre_g"))

                def lower(s, g, b):
                    if s == 1:
                        since(act, "ffn_done", g)
                        copy(cT[:, :], bank[0], "c_turned", "cT_ready", g + 1)
                        copy(knT[:, :], bank[2], "cn_turned", "knT_ready", g + 1, **affine)
                    if s == 2:
                        since(act, "scored1", 4 * (g - 1))
                        copy(k1[b][:, :], bank[0], "k_done1", "k_ready1", g + 1)
                        since(act, "o_done1", g - 1)
                        for m in range(2):
                            copy(v1[b][:, :, m, :], bank[2].rearrange("p (c s) -> p c s", s=2 * S1), "v_done1",
                                 "v_ready1", g + 1, scale=cst("seq_of_tile")[:, m:m + 1])
                    if s == 3:
                        copy(xT[:, :], bank[0], "x_turned", "xT_ready", g + 1)
                    if s in (5, 6):
                        for e in (2 * s - 10, 2 * s - 9):
                            copy(hT[:, e, :], bank[1 + e % 2], "h_done", "h_ready", HC * g + e + 1,
                                 func=ACT.Gelu, bias=prm("b1_0", e))
                    if s == 8:
                        copy(lowT, bank[2][0:32, :], "low_turned", "lowT_ready", g + 1)

                def upper(s, g, b):
                    if s == 0:
                        copy(qnT[:, :], bank[3], "xm_turned", "qnT_ready", g + 1, **affine)
                    if s == 1:
                        since(act, "scored1", 4 * g)
                        for a in range(2):
                            copy(q1[:, :, a, :], bank[4].rearrange("p (n i) -> p n i", n=GN), "q_done1", "q_ready1",
                                 g + 1, scale=cst("head_of_pair")[:, a:a + 1])
                    if s == 4:
                        for c in range(4):
                            copy(s1[:, c, :], s1[:, c, :], "s_ready", "e_ready", g + 1, func=ACT.Exp)
                    if s in (6, 7):
                        act.wait_ge(R["summed"], g + 1)
                        for c in (2 * s - 12, 2 * s - 11):
                            copy(s1[:, c, :], bank[3 + c % 2], "e_turned", "eT_ready", 4 * g + c + 1)
                    if s == 9:
                        copy(onT[:, :], bank[3], "on_turned", "onT_ready", g + 1)
                    if s == 10:
                        copy(gl[:, :, :].rearrange("p t d -> p (t d)"), bank[4], "gate_done", "gelu_ready", g + 1,
                             func=ACT.Gelu)
                    if s == 11:
                        copy(x3T[b][:, :], bank[3], "x3_turned", "x3T_ready", g + 1)
                    if s == 12:
                        copy(second[:, :], both[:, :], "routed", "second_ready", g + 1, func=ACT.Exp)
                    if s == 13:
                        copy(gT[:, :], bank[3][0:NE, :], "g_turned", "gT_ready", g + 1)

                def experts(g, b, e, third):
                    if e < NE and third == 0:
                        for c in range(HC):
                            act.wait_ge(R["hidden_done"], NE * HC * g + HC * e + c + 1)
                            if c == 0:
                                since(act, "expert_done", NE * g + e - 1)
                            act.activation(hE[e % 2][:, c, :], bank[5 + c % 2], ACT.Relu,
                                           bias=prm("b1_1", HC * e + c)).then_inc(R["relu_done"], 1)

                over_rounds(act, lower, upper, experts)

            @block.vector
            def _(dve):
                count = Count(dve, R["dve_r"])
                same_e = cst("same_e", 32)

                norms = Count(dve, R["stats_r"])
                dve.sem_inc(R["added"], AHEAD["added"])

                def norm(dst, src):
                    ln_stats(dve, count, src, R["stats_r"])
                    norms.k += 1
                    done = norms.base + norms.it * norms.per + norms.k
                    dve.wait_ge(R["stats_r"], done)
                    dve.wait_ge(R["rstd_r"], done)
                    return ln_apply(dve, dst, src)

                def row(name):
                    return prm(name).rearrange("p (o d) -> p o d", o=1).broadcast_to([P, GT, D])

                def turn_sums(group):
                    count.step(dve.reciprocal(sums[:, group, :], sums[:, group, :]))

                def lower(s, g, b):
                    xg = tiles(X[:, g, :])
                    if isinstance(g, int) and s in (5, 8):
                        dve.wait_ge(R["o_loaded"], 16 * (H0 + 1))
                        for group in {(0, 5): (1, 2), (0, 8): (3,), (1, 5): (4, 5), (1, 8): (6, 7)}[g, s]:
                            turn_sums(group)
                    if s == 0:
                        since(dve, "cn_turned", g)
                        dve.wait_ge(R["c_staged1"], g + 1)
                        norm(cn, c2).then_inc(R["cn_ready"], 1)
                        if isinstance(g, int) and g == 0:
                            dve.wait_ge(R["first_loaded"], 16 * (H0 + 1))
                            turn_sums(0)
                        since(dve, "y_done", g)
                        dve.tensor_tensor(oT[:, :], O_all[:, g, :], sums[:, g, :], ALU.mult)\
                           .then_inc(R["oT_ready"], 1)
                    if s == 1:
                        dve.wait_ge(R["y_done"], g + 1)
                        dve.scalar_tensor_tensor(out=x1[:, :, :], in0=tiles(bank[1]), scalar=tanh_x[:, 0:1], in1=xg,
                                                 op0=ALU.mult, op1=ALU.add).then_inc(R["x1_ready"], 1)
                        dve.wait_ge(R["x1_ready"], g + 1)
                        norm(xn, x1).then_inc(R["xn_ready"], 1)
                    if s == 3:
                        dve.wait_ge(R["even1_picked"], g + 1)
                        dve.tensor_tensor(
                            even1[:, :, :],
                            bank[1][0:32, 0:P].rearrange("p (o a) -> p o a", o=1).broadcast_to([32, 4, P]),
                            same_e.rearrange("p (e o) -> p e o", o=1).broadcast_to([32, 4, P]), ALU.mult)\
                           .then_inc(R["even1_ready"], 1)
                        dve.wait_ge(R["xT_ready"], g + 1)
                        xv = xT[:, :].rearrange("p (n i) -> p n i", n=GN)
                        dve.tensor_copy(odd1[:, :, :], xv[:, :, 2:10:2])
                        dve.tensor_copy(odd2[:, :, :], xv[:, :, 10:18:2]).then_inc(R["odd_ready"], 1)
                        dve.wait_ge(R["even2_picked"], g + 1)
                        count.step(dve.tensor_tensor(
                            tiles(masked2), tiles(bank[2][0:32, :]),
                            cst("same_r", 32).rearrange("p (o a) -> p o a", o=1).broadcast_to([32, GT, P]),
                            ALU.mult))
                        count.step(dve.tensor_reduce(picked2[:, :, :].rearrange("p t a -> p (t a)"),
                                                     masked2.rearrange("p (c r) -> p c r", r=4), AX, ALU.add))
                        dve.tensor_tensor(
                            even2[:, :, :, :],
                            picked2[:, :, :].rearrange("p t (o a) -> p t o a", o=1).broadcast_to([32, GT, 4, 32]),
                            same_e.rearrange("p (u e o) -> p u e o", o=1, u=1).broadcast_to([32, GT, 4, 32]),
                            ALU.mult).then_inc(R["even2_ready"], 1)
                    if s == 4:
                        dve.wait_ge(R["up_done"], g + 1)
                        dve.scalar_tensor_tensor(out=up, in0=bank[1][0:32, :], scalar=prm("scale")[0:32, :],
                                                 in1=cst("same_seq", 32), op0=ALU.mult, op1=ALU.mult)\
                           .then_inc(R["up_ready"], 1)
                    if s == 7:
                        dve.wait_ge(R["low_done"], g + 1)
                        dve.scalar_tensor_tensor(
                            out=low[:, :, :], in0=bank[1][:, 0:P].rearrange("p (c e) -> p c e", e=8),
                            scalar=prm("scale"),
                            in1=cst("same_seq_tok").rearrange("p (o e) -> p o e", o=1).broadcast_to([P, GT * HC, 8]),
                            op0=ALU.mult, op1=ALU.mult).then_inc(R["low_ready"], 1)
                    if s == 9:
                        dve.wait_ge(R["ffn_done"], g + 1)
                        count.step(dve.tensor_tensor(fin[:, :, :], tiles(bank[0]), row("b2_0"), ALU.add))
                        count.step(dve.scalar_tensor_tensor(out=xg, in0=fin[:, :, :], scalar=tanh_f[:, 0:1],
                                                            in1=x1[:, :, :], op0=ALU.mult, op1=ALU.add))
                        carry(dve)
                        count.step(norm(xn, xg))
                    if s == 10:
                        since(dve, "xm_turned", g)
                        norm(xm, xn).then_inc(R["xm_ready"], 1)

                def upper(s, g, b):
                    xg = tiles(X[:, g, :])
                    if s in (2, 3):
                        since(dve, "o_done1", g)
                        for c in (2 * s - 4, 2 * s - 3):
                            dve.wait_ge(R["scored1"], 4 * g + c + 1)
                            dve.tensor_scalar(s1[:, c, :], bank[3 + c % 2], CLIP, -CLIP, ALU.min, ALU.max)\
                               .then_inc(R["clipped"], 1)
                    if s == 3:
                        dve.wait_ge(R["clipped"], 4 * g + 4)
                        sv = s1[:, :, :].rearrange("p c (n j) -> p (c n) j", n=GN)
                        count.step(dve.tensor_reduce(top1[:, :], sv, AX, ALU.max))
                        dve.tensor_tensor(sv, sv, top1[:, :].rearrange("p (h o) -> p h o", o=1)
                                          .broadcast_to([P, 4 * GN, SEQ]), ALU.subtract)\
                           .then_inc(R["s_ready"], 1)
                    if s == 5:
                        dve.wait_ge(R["e_ready"], 4 * g + 4)
                        dve.tensor_reduce(sum1[:, :], s1[:, :, :].rearrange("p c (n j) -> p (c n) j", n=GN), AX,
                                          ALU.add).then_inc(R["summed"], 1)
                        dve.wait_ge(R["summed"], g + 1)
                        count.step(dve.reciprocal(inv1[:, :], sum1[:, :]))
                    if s == 8:
                        dve.wait_ge(R["o_done1"], g + 1)
                        inv = inv1[:, :].rearrange("p (c t m) -> p t c m", c=4, m=2)
                        o_ps = psum[:, 3:5, :].rearrange("p a (t c m h s) -> p (a t) c m h s", t=2, c=4, m=2, h=2)
                        for a in range(2):
                            rows = slice(64 * a, 64 * a + 64)
                            for m in range(2):
                                ins = dve.tensor_tensor(
                                    o1[64 * m:64 * m + 64, :, :].rearrange("p t (c h s) -> p t c h s", c=4, h=2)
                                    [:, :, :, a, :], o_ps[rows, :, :, m, a, :],
                                    inv[rows, :, :, m:m + 1].broadcast_to([64, GT, 4, S1]), ALU.mult)
                        ins.then_inc(R["o_ready1"], 1)
                        dve.wait_ge(R["o_ready1"], g + 1)
                        count.step(norm(on, o1))
                        count.step(dve.tensor_tensor(on[:, :, :], on[:, :, :], row("ln_g"), ALU.mult))
                        dve.tensor_tensor(on[:, :, :], on[:, :, :], row("ln_b"), ALU.add).then_inc(R["on_ready"], 1)
                    if s == 10:
                        dve.wait_ge(R["on_ready"], g + 1)
                        dve.wait_ge(R["gelu_ready"], g + 1)
                        count.step(dve.tensor_tensor(on[:, :, :], gl[:, :, :], on[:, :, :], ALU.add))
                        count.step(dve.scalar_tensor_tensor(out=xg, in0=on[:, :, :], scalar=tanh_x[:, 1:2],
                                                            in1=xg, op0=ALU.mult, op1=ALU.add))
                        carry(dve)
                        norm(x3, xg).then_inc(R["x3_ready"], 1)
                    if s == 12:
                        dve.wait_ge(R["logits_done"], g + 1)
                        since(dve, "g_turned", g - 1)
                        count.step(dve.tensor_tensor(
                            logits[:, :, :], bank[4][:, 0:GT * NE].rearrange("p (t e) -> p t e", e=NE),
                            prm("br").rearrange("p (o e) -> p o e", o=1).broadcast_to([P, GT, NE]), ALU.add))
                        carry(dve)
                        for t in range(GT):
                            ins = dve.max(best[:, t, :], logits[:, t, :])
                        count.step(ins)
                        carry(dve)
                        for t in range(GT):
                            ins = dve.max_index(place[:, t, :], best[:, t, :], logits[:, t, :])
                        dve.tensor_tensor(both[:, :], best[:, :, 1], best[:, :, 0], ALU.subtract)\
                           .then_inc(R["routed"], 1)
                        dve.wait_ge(R["routed"], g + 1)
                        count.step(dve.tensor_copy(placef[:, :, :], place[:, :, :]))
                        for n in range(2):
                            ins = dve.tensor_tensor(
                                pick[:, n, :, :],
                                cst("iota").rearrange("p (o e) -> p o e", o=1).broadcast_to([P, GT, NE]),
                                placef[:, :, n:n + 1].broadcast_to([P, GT, NE]), ALU.is_equal)
                        count.step(ins)
                        dve.wait_ge(R["second_ready"], g + 1)
                        count.step(dve.tensor_scalar(weight[:, 1, :], second[:, :], 1.0, None, ALU.add))
                        count.step(dve.reciprocal(weight[:, 0, :], weight[:, 1, :]))
                        count.step(dve.tensor_tensor(weight[:, 1, :], second[:, :], weight[:, 0, :], ALU.mult))
                        for n in range(2):
                            ins = dve.tensor_tensor(
                                pick[:, n, :, :], pick[:, n, :, :],
                                weight[:, n, :].rearrange("p (t o) -> p t o", o=1).broadcast_to([P, GT, NE]),
                                ALU.mult)
                        count.step(ins)
                        dve.tensor_tensor(gates[b][:, :, :], pick[:, 0, :, :], pick[:, 1, :, :], ALU.add)\
                           .then_inc(R["gates_done"], 1)
                    if s == 14:
                        dve.wait_ge(R["gates_done"], g + 1)
                        dve.wait_ge(R["bias_done"], g + 1)
                        if not (isinstance(g, int) and g < 2):
                            dve.wait_ge(stored[b], 16 * (half_before(g, b) + b))
                        dve.tensor_copy(acc[b][:, :, :], tiles(bank[4])).then_inc(R["acc_ready"], 1)

                def experts(g, b, e, third):
                    if e >= 1 and third == 2:
                        u = e - 1
                        dve.wait_ge(R["expert_done"], AHEAD["expert_done"] + NE * g + u + 1)
                        if u == 0:
                            dve.wait_ge(R["acc_ready"], g + 1)
                        since(dve, "added", NE * g + u)
                        for t in range(GT):
                            ins = dve.scalar_tensor_tensor(
                                out=acc[b][:, t, :], in0=bank[7][:, t * P:(t + 1) * P],
                                scalar=gates[b][:, t, u:u + 1], in1=acc[b][:, t, :], op0=ALU.mult, op1=ALU.add)
                        ins.then_inc(R["added"], 1)
                        if e == NE:
                            dve.wait_ge(R["added"], AHEAD["added"] + NE * g + NE)
                            dve.scalar_tensor_tensor(out=acc[b][:, :, :], in0=acc[b][:, :, :],
                                                     scalar=tanh_f[:, 1:2], in1=tiles(X[:, g, :]), op0=ALU.mult,
                                                     op1=ALU.add).then_inc(R["res_ready"], 1)

                over_rounds(dve, lower, upper, experts, ((count, 2 * 25), (norms, 12)))

            @block.tensor
            def _(pe):
                def turn(dst, src, done):
                    for t in range(GT):
                        mm = pe.transpose(dst[:, t * P:(t + 1) * P], src[:, t, :], ident)
                    mm.then_inc(R[done], 1)

                pe.sem_inc(R["expert_done"], AHEAD["expert_done"])

                def second_ffn(g, tiles_now):
                    for t in tiles_now:
                        for r in range(HC):
                            pe.matmul(bank[0][:, t * P:(t + 1) * P], hT[:, r, t * P:(t + 1) * P],
                                      wt1("w2t")[:, r * P:(r + 1) * P], start=(t == 0 and r == 0), stop=False,
                                      skip_group_check=True)

                def lower(s, g, b):
                    if s == 1:
                        pe.wait_ge(R["c_staged1"], g + 1)
                        since(pe, "xm_ready", g)
                        turn(bank[0], c2, "c_turned")
                        pe.wait_ge(R["cn_ready"], g + 1)
                        turn(bank[2], cn, "cn_turned")
                        pe.wait_ge(R["oT_ready"], g + 1)
                        for t in range(GT):
                            mm = pe.matmul(bank[1][:, t * P:(t + 1) * P], oT[:, t * P:(t + 1) * P], wt1("wo0"),
                                           start=True, stop=True)
                        mm.then_inc(R["y_done"], 1)
                    if s == 2:
                        pe.wait_ge(R["cT_ready"], g + 1)
                        pe.wait_ge(R["knT_ready"], g + 1)
                        pe.matmul(bank[0], wt1("wk1"), knT[:, :], start=True, stop=True).then_inc(R["k_done1"], 1)
                        for t in range(GT):
                            mm = pe.matmul(bank[2][:, t * P:(t + 1) * P], cT[:, t * P:(t + 1) * P], wt1("wv1"),
                                           start=True, stop=True)
                        mm.then_inc(R["v_done1"], 1)
                    if s == 3:
                        pe.wait_ge(R["xn_ready"], g + 1)
                        pe.wait_ge(R["k_ready1"], g + 1)
                        turn(bank[0], xn, "x_turned")
                        for t in range(GT):
                            mm = pe.matmul(bank[1][0:32, 0:P], cst("sel_first")[:, 32 * t:32 * t + 32], xn[:, t, :],
                                           start=(t == 0), stop=(t == GT - 1))
                        mm.then_inc(R["even1_picked"], 1)
                        pe.wait_ge(R["v_ready1"], 2 * g + 2)
                        for t in range(GT):
                            mm = pe.matmul(bank[2][0:32, t * P:(t + 1) * P], cst("sel_second"), xn[:, t, :],
                                           start=True, stop=True)
                        mm.then_inc(R["even2_picked"], 1)
                    if s == 4:
                        pe.wait_ge(R["odd_ready"], g + 1)
                        pe.matmul(bank[1][0:32, :], odd1[:, :, :].rearrange("p n e -> p (n e)"), xT[:, :],
                                  start=True, stop=True).then_inc(R["up_done"], 1)
                    if s in (5, 6):
                        pe.wait_ge(R["up_ready"], g + 1)
                        pe.wait_ge(R["even2_ready"], g + 1)
                        for e in (2 * s - 10, 2 * s - 9):
                            since(pe, "h_ready", HC * g + e - 1)
                            h = bank[1 + e % 2]
                            pe.matmul(h, wt1("w1t")[:, e * P:(e + 1) * P], xT[:, :], start=True, stop=False)
                            pe.matmul(h, even1[:, e, :], up, start=False, stop=True).then_inc(R["h_done"], 1)
                    if s == 7:
                        pe.wait_ge(R["h_ready"], HC * g + HC)
                        for t in range(GT):
                            for r in range(HC):
                                mm = pe.matmul(bank[1][:, 32 * t + 8 * r:32 * t + 8 * r + 8],
                                               hT[:, r, t * P:(t + 1) * P],
                                               odd2[:, 2 * t:2 * t + 2, :].rearrange("p n e -> p (n e)"),
                                               start=True, stop=True)
                        mm.then_inc(R["low_done"], 1)
                        second_ffn(g, (0, 1))
                    if s == 8:
                        pe.wait_ge(R["low_ready"], g + 1)
                        for t in range(GT):
                            mm = pe.transpose(bank[2][0:32, t * P:(t + 1) * P],
                                              low[:, HC * t:HC * t + HC, :].rearrange("p c e -> p (c e)"), ident)
                        mm.then_inc(R["low_turned"], 1)
                        second_ffn(g, (2, 3))
                    if s == 9:
                        pe.wait_ge(R["lowT_ready"], g + 1)
                        for t in range(GT):
                            mm = pe.matmul(bank[0][:, t * P:(t + 1) * P], lowT[:, t * P:(t + 1) * P],
                                           even2[:, t, :, :].rearrange("p e a -> p (e a)"), start=False, stop=True,
                                           skip_group_check=True)
                        mm.then_inc(R["ffn_done"], 1)

                def upper(s, g, b):
                    if s == 0:
                        pe.wait_ge(R["xm_ready"], g + 1)
                        turn(bank[3], xm, "xm_turned")
                    if s == 1:
                        pe.wait_ge(R["qnT_ready"], g + 1)
                        since(pe, "acc_ready", g)
                        pe.matmul(bank[4], wt1("wq1"), qnT[:, :], start=True, stop=True).then_inc(R["q_done1"], 1)
                    if s in (2, 3):
                        pe.wait_ge(R["q_ready1"], 2 * g + 2)
                        pe.wait_ge(R["k_ready1"], g + 1)
                        for c in (2 * s - 4, 2 * s - 3):
                            if c >= 2:
                                pe.wait_ge(R["clipped"], 4 * g + c - 1)
                            r = slice(32 * c, 32 * c + 32)
                            for n in range(GN):
                                mm = pe.matmul(bank[3 + c % 2][:, SEQ * n:SEQ * n + SEQ],
                                               q1[r, n, :, :].rearrange("p a i -> p (a i)"),
                                               k1[b][r, SEQ * n:SEQ * n + SEQ], start=True, stop=True,
                                               tile_position=(32 * c, 0))
                            mm.then_inc(R["scored1"], 1)
                    if s in (6, 7):
                        pe.wait_ge(R["clipped"], 4 * g + 4)
                        for c in (2 * s - 12, 2 * s - 11):
                            pe.wait_ge(R["e_ready"], 4 * g + c + 1)
                            if c >= 2:
                                pe.wait_ge(R["eT_ready"], 4 * g + c - 1)
                            for t in range(GT):
                                mm = pe.transpose(bank[3 + c % 2][:, t * P:(t + 1) * P],
                                                  s1[:, c, t * P:(t + 1) * P], ident)
                            mm.then_inc(R["e_turned"], 1)
                    if s == 8:
                        pe.wait_ge(R["eT_ready"], 4 * g + 4)
                        pe.wait_ge(R["v_ready1"], 2 * g + 2)
                        for t in range(GT):
                            for c in range(4):
                                at = 64 * (4 * (t % 2) + c)
                                mm = pe.matmul(bank[3 + t // 2][:, at:at + 64], s1[:, c, t * P:(t + 1) * P],
                                               v1[b][:, 4 * t + c, :, :].rearrange("p m s -> p (m s)"),
                                               start=True, stop=True)
                        mm.then_inc(R["o_done1"], 1)
                    if s == 9:
                        pe.wait_ge(R["on_ready"], g + 1)
                        turn(bank[3], on, "on_turned")
                    if s == 10:
                        pe.wait_ge(R["onT_ready"], g + 1)
                        for t in range(GT):
                            mm = pe.matmul(bank[4][:, t * P:(t + 1) * P], onT[:, t * P:(t + 1) * P], wt1("wo1"),
                                           start=True, stop=True)
                        mm.then_inc(R["gate_done"], 1)
                    if s == 11:
                        pe.wait_ge(R["x3_ready"], g + 1)
                        turn(bank[3], x3, "x3_turned")
                    if s == 12:
                        pe.wait_ge(R["x3T_ready"], g + 1)
                        for t in range(GT):
                            mm = pe.matmul(bank[4][:, t * NE:(t + 1) * NE], x3T[b][:, t * P:(t + 1) * P],
                                           wt1("wr"), start=True, stop=True)
                        mm.then_inc(R["logits_done"], 1)
                    if s == 13:
                        pe.wait_ge(R["gates_done"], g + 1)
                        for t in range(GT):
                            mm = pe.transpose(bank[3][0:NE, t * P:(t + 1) * P], gates[b][:, t, :], ident)
                        mm.then_inc(R["g_turned"], 1)
                    if s == 14:
                        pe.wait_ge(experts_loaded, 48)
                        pe.wait_ge(R["gT_ready"], g + 1)
                        for t in range(GT):
                            mm = pe.matmul(bank[4][:, t * P:(t + 1) * P], gT[:, t * P:(t + 1) * P], B2E[:, :],
                                           start=True, stop=True)
                        mm.then_inc(R["bias_done"], 1)

                def experts(g, b, e, third):
                    if third == 0:
                        if e < NE:
                            for c in range(HC):
                                since(pe, "relu_done", NE * HC * g + HC * e + c - 1)
                                pe.matmul(bank[5 + c % 2], W1E[:, e, c * P:(c + 1) * P], x3T[b][:, :],
                                          start=True, stop=True).then_inc(R["hidden_done"], 1)
                    elif e >= 1:
                        u = e - 1
                        if third == 1:
                            pe.wait_ge(R["relu_done"], AHEAD["relu_done"] + NE * HC * g + HC * e)
                            since(pe, "added", NE * g + u)
                        for t in (2 * third - 2, 2 * third - 1):
                            for c in range(HC):
                                mm = pe.matmul(bank[7][:, t * P:(t + 1) * P], hE[u % 2][:, c, t * P:(t + 1) * P],
                                               W2E[:, u, c, :], start=(c == 0), stop=(c == HC - 1))
                        if third == 2:
                            mm.then_inc(R["expert_done"], 1)

                over_rounds(pe, lower, upper, experts)


def kernel(**inputs):
    from concourse import bacc
    from concourse.bass_utils import run_bass_kernel_spmd

    w = {k: np.asarray(v) for k, v in inputs.items()}

    def packed(pieces, width):
        a = np.concatenate([p.reshape(P, -1) for p in pieces], 1)
        assert a.shape == (P, width), a.shape
        return np.ascontiguousarray(a)

    def row(v):
        return np.tile(v.reshape(1, -1), (P, 1))

    params = packed([
        w["L0_xattn_content_bias"], w["L0_xattn_position_bias"], w["L0_ffn_b1"].reshape(HC, P).T,
        w["L1_xattn_pre_g"], w["L1_xattn_pre_b"], w["L1_ffn_b1"].reshape(NE * HC, P).T,
        row(w["L0_ffn_b2"]), row(w["L1_xattn_ln_g"]), row(w["L1_xattn_ln_b"]), row(w["L1_ffn_br"]),
        row(w["L0_ffn_scale"]), row(w["g_xattn"]), row(w["g_ffn"])], PARAM_W)
    weights0 = packed([w["L0_xattn_Wq"], w["L0_xattn_Wkc"], w["L0_xattn_Wkp"], w["L0_xattn_Wv"],
                       w["L0_xattn_positional_encoding"]], WEIGHT0_W)
    weights1 = packed([
        w["L0_xattn_Wo"], w["L0_ffn_W1"].T, w["L0_ffn_W2"].T.reshape(HC, P, D).transpose(1, 0, 2),
        w["L1_xattn_Wq"], w["L1_xattn_Wk"], w["L1_xattn_Wv"], w["L1_xattn_Wo"], w["L1_ffn_Wr"]],
        WEIGHT1_W)
    arrays = {
        "x": w["x"], "ctx": w["ctx_1024"], "mask": w["mask_1x1xSx1024_fk0"].reshape(SEQ, KEYS),
        "consts": constants(), "params": params, "weights0": weights0, "weights1": weights1,
        "w1e": w["L1_ffn_W1"].transpose(1, 0, 2), "w2e": w["L1_ffn_W2"].reshape(NE, HC, P, D).transpose(2, 0, 1, 3),
        "b2e": w["L1_ffn_b2"]}
    arrays = {k: np.ascontiguousarray(a) for k, a in arrays.items()}

    nc = bacc.Bacc("TRN2", target_bir_lowering=False, num_devices=1)
    ins = [nc.dram_tensor(k, a.shape, mybir.dt.from_np(a.dtype), kind="ExternalInput").ap()
           for k, a in arrays.items()]
    scratch = [nc.dram_tensor("q_scratch", [H0, len(Q_PARTS), S0, GROUPS, GTOK], BF16, kind="Internal").ap(),
               nc.dram_tensor("k_scratch", [H0, len(K_PARTS), S0, GROUPS, 2 * GTOK], BF16, kind="Internal").ap(),
               nc.dram_tensor("kp_scratch", [PARTS, P, KEYS], BF16, kind="Internal").ap(),
               nc.dram_tensor("ot_scratch", [H0, S0, NSEQ * SEQ], F32, kind="Internal").ap(),
               nc.dram_tensor("st_scratch", [H0, 1, NSEQ * SEQ], F32, kind="Internal").ap()]
    out = nc.dram_tensor("out", [NSEQ, SEQ, D], F32, kind="ExternalOutput").ap()
    flamingo_kernel(nc, *ins, *scratch, out)
    r = run_bass_kernel_spmd(nc, [arrays], core_ids=[0])
    return r.results[0]["out"]
```

```python
from contextlib import ExitStack

import numpy as np

import concourse.bass as bass
from concourse import mybir

F32 = mybir.dt.float32
BF16 = mybir.dt.bfloat16
F32R = mybir.dt.float32r
U32 = mybir.dt.uint32
ALU = mybir.AluOpType
ACT = mybir.ActivationFunctionType
AX = mybir.AxisListType.X

P = 128
NSEQ, SEQ, D = 64, 64, 128
TILES = NSEQ * SEQ // P
GROUPS, GT = 8, 4
GN = NSEQ // GROUPS
GTOK = GT * P
NEG_INF = -1.0e9
EPS = 1e-5

H0, S0 = 16, 8
KEYS = 2 * SEQ
BLK = 16
NBLK = NSEQ // BLK
SCALE0 = 1.0 / float(np.sqrt(S0))
PARTS = 3
Q_PARTS = (0, 1, 2, 0, 1, 0)
K_PARTS = (0, 0, 0, 1, 1, 2)
WIN = SEQ - 1 + KEYS + 1
REV = KEYS + 1

H1, S1 = 8, 16
SCALE1 = 1.0 / float(np.sqrt(D))
CLIP = 10000.0

HID = 512
HC = HID // P
NE = 8


def layout(widths):
    at, out = 0, {}
    for name, w in widths:
        out[name] = (at, at + w)
        at += w
    return out, at


CONSTS, CONST_W = layout([
    ("ident", P), ("same_token", SEQ), ("sel_first", GT * 32), ("sel_second", 32),
    ("same_seq", GTOK), ("same_e", 4), ("same_r", P), ("same_seq_tok", 8 * HC), ("head_rows", H0),
    ("iota", NE), ("bias_on", 1), ("minus_upper", 1),
    ("head_of_pair", 2), ("seq_of_tile", 2), ("same_block", 32)])
PARAMS, PARAM_W = layout([
    ("cb", 1), ("pb", 1), ("b1_0", HC), ("pre_g", 1), ("pre_b", 1), ("b1_1", NE * HC),
    ("b2_0", D), ("ln_g", D), ("ln_b", D), ("br", NE), ("scale", 1), ("g_xattn", 2), ("g_ffn", 2)])
WEIGHTS0, WEIGHT0_W = layout([("wq", D), ("wkc", D), ("wkp", D), ("wv", D), ("pe", D)])
WEIGHTS1, WEIGHT1_W = layout([
    ("wo0", D), ("w1t", HID), ("w2t", HID), ("wq1", D), ("wk1", D), ("wv1", D), ("wo1", D), ("wr", NE)])


def constants():
    c = np.zeros((P, CONST_W), np.float32)

    def put(name, a):
        c[:a.shape[0], CONSTS[name][0]:CONSTS[name][0] + a.shape[1]] = a

    p = np.arange(P)[:, None]
    put("ident", np.eye(P))
    put("same_token", p % SEQ == np.arange(SEQ)[None, :])
    col = np.arange(32)[None, :]
    put("sel_first", np.concatenate(
        [(2 * t + p // SEQ == col // 4) & (p % SEQ == 1 + 2 * (col % 4)) for t in range(GT)], 1))
    put("sel_second", (p // SEQ == col // 4 % 2) & (p % SEQ == 9 + 2 * (col % 4)))
    row = np.arange(32)[:, None]
    put("same_seq", row // 4 == np.arange(GTOK)[None, :] // SEQ)
    put("same_e", row % 4 == np.arange(4)[None, :])
    put("same_r", row // 8 == np.arange(P)[None, :] % 4)
    put("same_seq_tok", p // SEQ == np.arange(8 * HC)[None, :] % 8 // 4)
    put("head_rows", p // S0 == np.arange(H0)[None, :])
    put("bias_on", (p % 64 >= 48) & (p % 64 < 48 + PARTS))
    put("minus_upper", -1.0 * (p >= 64))
    put("head_of_pair", SCALE1 * (p // S1 % 2 == np.arange(2)[None, :]))
    put("same_block", p % 32 == np.arange(32)[None, :])
    put("seq_of_tile", p // SEQ == np.arange(2)[None, :])
    put("iota", np.broadcast_to(np.arange(NE), (P, NE)))
    return c


class Count:

    def __init__(self, eng, sem):
        self.eng, self.sem, self.base, self.it, self.per, self.k = eng, sem, 0, 0, 0, 0

    def enter(self, it, per):
        self.base, self.it, self.per, self.k = self.base + self.k, it, per, 0

    def leave(self, rounds):
        assert self.k == self.per, (self.k, self.per)
        self.base, self.it, self.per, self.k = self.base + rounds * self.per, 0, 0, 0

    def step(self, ins):
        self.k += 1
        ins.then_inc(self.sem, 1)
        self.eng.wait_ge(self.sem, self.base + self.it * self.per + self.k)


def flamingo_kernel(nc, x, ctx_in, mask, consts, params, weights0, weights1, w1e, w2e, b2e,
                    q_scratch, k_scratch, kp_scratch, ot_scratch, st_scratch, out):
    with ExitStack() as ctx:
        def sb(name, shape, dt=F32, stack=ctx):
            return stack.enter_context(nc.sbuf_tensor(name, shape, dt))

        def sem(name):
            return ctx.enter_context(nc.semaphore(name))

        psum = ctx.enter_context(nc.psum_tensor("psum", [P, 8, 512], F32))
        X = sb("X", [P, GROUPS, GTOK])
        C = sb("C", [P, GROUPS, GTOK])
        CST = sb("CST", [P, CONST_W])
        PRM = sb("PRM", [P, PARAM_W])
        WT1 = sb("WT1", [P, WEIGHT1_W])
        O_all = sb("O_all", [P, GROUPS, GTOK])
        sums = sb("sums", [P, GROUPS, GTOK])
        xn = sb("xn", [P, GT, D])
        stats = sb("stats", [P, GT, 6])
        moments = sb("moments", [P, GT, 2])
        rstd = sb("rstd", [P, GT])
        neg_half = sb("neg_half", [P, GT])
        eps_tile = sb("eps_tile", [P, GT])
        tanh_x = sb("tanh_x", [P, 2])
        tanh_f = sb("tanh_f", [P, 2])

        def cst(name, rows=P):
            return CST[0:rows, CONSTS[name][0]:CONSTS[name][1]]

        def prm(name, k=None):
            a, b = PARAMS[name]
            return PRM[:, a:b] if k is None else PRM[:, a + k:a + k + 1]

        def wt1(name):
            return WT1[:, WEIGHTS1[name][0]:WEIGHTS1[name][1]]

        ident = cst("ident")

        passed = sem("passed")

        def carry(eng):
            eng.sem_inc(passed, 1)

        def ln_stats(dve, count, src, ready):
            for t in range(GT):
                ins = dve.bn_stats(stats[:, t, :], src[:, t, :])
                if t == GT - 1:
                    count.step(ins)
            carry(dve)
            for t in range(GT):
                ins = dve.bn_aggr(moments[:, t, :], stats[:, t, :])
            ins.then_inc(ready, 1)

        def ln_rstd(pool, count, done):
            count.step(pool.tensor_tensor(rstd[:, :], moments[:, :, 1], eps_tile[:, :], ALU.add))
            pool.tensor_tensor(rstd[:, :], rstd[:, :], neg_half[:, :], ALU.pow).then_inc(done, 1)

        def ln_apply(dve, dst, src):
            for t in range(GT):
                ins = dve.tensor_scalar(dst[:, t, :], src[:, t, :], moments[:, t, 0:1], rstd[:, t:t + 1],
                                        ALU.subtract, ALU.mult)
            return ins

        def tiles(ap):
            return ap.rearrange("p (t c) -> p t c", t=GT)

        heads_ctx = ExitStack()
        V_all = sb("V_all", [P, NSEQ, H0, S0], stack=heads_ctx)
        kp_stack = sb("kp_stack", [P, H0, WIN], BF16, heads_ctx)
        att_ctx = ExitStack()
        UTOK = BLK * SEQ
        q_stack = [sb(f"q_stack{b}", [P, UTOK], BF16, att_ctx) for b in range(3)]
        q_content = [sb(f"q_content{b}", [P, UTOK], BF16, att_ctx) for b in range(3)]
        k_stack = [sb(f"k_stack{b}", [P, BLK * KEYS], BF16, att_ctx) for b in range(3)]
        same_block = sb("same_block", [32 * PARTS, 32], BF16, att_ctx)
        ones_rows = sb("ones_rows", [32 * PARTS, P], BF16, att_ctx)
        mask_sb = sb("mask_sb", [P, KEYS], stack=att_ctx)
        neg_mask = sb("neg_mask", [P, KEYS], stack=att_ctx)
        mask_first = sb("mask_first", [P, KEYS], BF16, att_ctx)
        mask_rest = sb("mask_rest", [P, KEYS], stack=att_ctx)
        mask_second = sb("mask_second", [P, KEYS], BF16, att_ctx)
        mask_parts = sb("mask_parts", [P, KEYS], BF16, att_ctx)
        tokens2 = sb("tokens2", [P, UTOK], BF16, att_ctx)
        q_part = [sb(f"q_part{b}", [P, PARTS, GTOK], BF16, att_ctx) for b in range(2)]
        k_part = [sb(f"k_part{b}", [P, PARTS, 2 * GTOK], BF16, att_ctx) for b in range(2)]
        proj_ctx = ExitStack()
        WT0 = sb("WT0", [P, WEIGHT0_W], stack=proj_ctx)
        c_now = sb("c_now", [P, GT, D], stack=proj_ctx)
        refT = sb("refT", [P, GN, KEYS], stack=proj_ctx)
        qz = sb("qz", [P, GTOK], stack=proj_ctx)
        qr = sb("qr", [P, GTOK], stack=proj_ctx)
        kr = sb("kr", [P, 2 * GTOK], stack=proj_ctx)
        peT = sb("peT", [P, KEYS], stack=proj_ctx)
        kpT = sb("kpT", [P, KEYS], stack=proj_ctx)
        kp_r = sb("kp_r", [P, KEYS], stack=proj_ctx)
        kp_part = sb("kp_part", [P, PARTS, KEYS], BF16, proj_ctx)
        bias_rows = sb("bias_rows", [P, H0], stack=proj_ctx)
        bias_diff = sb("bias_diff", [P, 1], stack=proj_ctx)
        bp = sb("bp", [H0, KEYS], stack=proj_ctx)
        bp_part = sb("bp_part", [H0, PARTS, KEYS], BF16, proj_ctx)

        def wt0(name):
            return WT0[:, WEIGHTS0[name][0]:WEIGHTS0[name][1]]

        loaded = sem("loaded")
        x_loaded = [sem(f"x_loaded{n}") for n in range(3)]
        mask_loaded = sem("mask_loaded")
        mask_ready = sem("mask_ready")
        stack_set = sem("stack_set")
        dve_p = sem("dve_p")
        pool_p = sem("pool_p")
        half_set = sem("half_set")
        stats_p = sem("stats_p")
        rstd_p = sem("rstd_p")
        xn_p = sem("xn_p")
        pe_turned = sem("pe_turned")
        peT_ready = sem("peT_ready")
        kp_done = sem("kp_done")
        kpT_ready = sem("kpT_ready")
        bias_ready = sem("bias_ready")
        bp_done = sem("bp_done")
        kp_split = sem("kp_split")
        kp_stored = sem("kp_stored")
        stack_zero = sem("stack_zero")
        kp_stacked = sem("kp_stacked")
        turned_p = sem("turned_p")
        c_staged = sem("c_staged")
        loaded1 = sem("loaded1")
        refx_ready = sem("refx_ready")
        refc_ready = sem("refc_ready")
        q_done = sem("q_done")
        k_done = sem("k_done")
        v_done = sem("v_done")
        qz_ready = sem("qz_ready")
        q_first = sem("q_first")
        qr_ready = sem("qr_ready")
        q_second = sem("q_second")
        q_third = sem("q_third")
        k_first = sem("k_first")
        kr_ready = sem("kr_ready")
        k_second = sem("k_second")
        k_third = sem("k_third")
        v_kept = sem("v_kept")
        q_stored = [sem(f"q_stored{b}") for b in range(2)]
        k_stored = [sem(f"k_stored{b}") for b in range(2)]
        gates_ready = sem("gates_ready")
        def passed_since(eng, sem, value):
            if not isinstance(value, int) or value > 0:
                eng.wait_ge(sem, value)

        def wait_x(eng, g):
            if isinstance(g, int) and g <= 2:
                eng.wait_ge(x_loaded[g], 32 if g < 2 else 32 * (GROUPS - 2))

        def over_groups(eng, body, count=None):
            for g in range(2):
                body(g, g % 2, g // 2)
            with eng.Fori(1, GROUPS // 2 - 1) as i:
                if count:
                    count.enter(i - 1, 2)
                for b in range(2):
                    body(2 * i + b, b, i)
                if count:
                    count.leave(GROUPS // 2 - 2)
            for g in range(GROUPS - 2, GROUPS):
                body(g, g % 2, g // 2)

        def has_next(g):
            return not isinstance(g, int) or g + 1 < GROUPS

        UNITS = H0 * NBLK
        ROUND = 3 * NBLK
        ROUNDS = UNITS // ROUND
        unit_loaded = [sem(f"unit_loaded{b}") for b in range(3)]
        qv = q_scratch.rearrange("h s c g t -> h (s c) (g t)")
        kv = k_scratch.rearrange("h s c g t -> h (s c) (g t)")

        def head_of(it, k):
            return (ROUND // NBLK) * it + k // NBLK

        def load_unit(sp, it, k):
            h, blk, b = head_of(it, k), k % NBLK, k % 3
            for half, shift in ((0, 0), (64, 1)):
                sp.dma_start(q_stack[b][half:half + 48, 0:UTOK - shift],
                             qv[h, :, blk * UTOK + shift:(blk + 1) * UTOK]).then_inc(unit_loaded[b], 16)
            sp.dma_start(q_content[b][0:48, :], qv[h, :, blk * UTOK:(blk + 1) * UTOK])\
              .then_inc(unit_loaded[b], 16)
            sp.dma_start(k_stack[b][0:48, :], kv[h, :, blk * 2 * UTOK:(blk + 1) * 2 * UTOK])\
              .then_inc(unit_loaded[b], 16)

        T_x, T_c, Q_ps = psum[:, 0, :], psum[:, 1, :], psum[:, 2, :]
        K_ps, V_ps = psum[:, 3:5, :], psum[:, 5:7, :]

        with nc.Block() as block:
            @block.sync
            def _(sp):
                sp.dma_start(PRM[:, :], params).then_inc(loaded, 16)
                sp.dma_start(CST[:, :], consts).then_inc(loaded, 16)
                sp.dma_start(WT0[:, :], weights0).then_inc(loaded, 16)
                for m in range(2):
                    sp.dma_start(mask_sb[64 * m:64 * m + 64, :], mask).then_inc(mask_loaded, 16)
                xv = x.rearrange("(g t m) s d -> (m s) g t d", t=GT, m=2)
                cv = ctx_in.rearrange("(g t m) s d -> (m s) g t d", t=GT, m=2)
                for g in range(GROUPS):
                    sp.dma_start(tiles(X[:, g, :]), xv[:, g]).then_inc(x_loaded[min(g, 2)], 16)
                    sp.dma_start(tiles(C[:, g, :]), cv[:, g]).then_inc(x_loaded[min(g, 2)], 16)
                sp.dma_start(WT1[:, :], weights1).then_inc(loaded1, 16)
                sp.wait_ge(kp_split, 1)
                sp.dma_start(kp_scratch.rearrange("a p r -> p a r"), kp_part[:, :, :]).then_inc(kp_stored, 16)
                sp.wait_ge(kp_stored, 16)
                sp.wait_ge(stack_zero, 1)
                kv = kp_scratch.rearrange("a (h s) r -> a s h r", s=S0)
                for half, at in ((0, 0), (64, REV)):
                    w = min(KEYS, WIN - at)
                    for row, part in enumerate(K_PARTS):
                        sp.dma_start(kp_stack[half + row:half + 48:len(K_PARTS), :, at:at + w],
                                     kv[part, :, :, 0:w]).then_inc(kp_stacked, 16)
                    for part in range(PARTS):
                        sp.dma_start(kp_stack[half + 48 + part:half + 49 + part, :, at:at + w],
                                     bp_part[:, part, 0:w]).then_inc(kp_stacked, 16)

                def store(scratch, part, parts, g, done):
                    at = 0
                    while at < len(parts):
                        n = at + 1
                        step = parts[n] - parts[at] if n < len(parts) and parts[n] - parts[at] in (0, 1) else None
                        while n < len(parts) and parts[n] - parts[n - 1] == step:
                            n += 1
                        src = part[:, parts[at]:parts[at] + n - at, :] if step else \
                            part[:, parts[at]:parts[at] + 1, :].broadcast_to([P, n - at, part.shape[2]])
                        sp.dma_start(scratch[:, :, at:n, g, :].rearrange("h s c t -> (h s) c t"), src)\
                          .then_inc(done, 16)
                        at = n

                def body(g, b, before):
                    if isinstance(g, int) and g == GROUPS - 2:
                        for parity in range(2):
                            sp.wait_ge(q_stored[parity], 48 * before)
                            sp.wait_ge(k_stored[parity], 48 * before)
                        sp.wait_ge(stack_set, 13)
                        for n in range(3):
                            load_unit(sp, 0, n)
                    sp.wait_ge(q_third, g + 1)
                    store(q_scratch, q_part[b], Q_PARTS, g, q_stored[b])
                    sp.wait_ge(k_third, g + 1)
                    store(k_scratch, k_part[b], K_PARTS, g, k_stored[b])

                over_groups(sp, body)
                sp.wait_ge(kp_stacked, 16 * 18)
                sp.wait_ge(loaded1, 16)

            @block.gpsimd
            def _(pool):
                count = Count(pool, pool_p)
                pool.memset(neg_half[:, :], -0.5).then_inc(half_set, 1)
                pool.memset(eps_tile[:, :], EPS).then_inc(half_set, 1)
                for b in range(3):
                    pool.memset(q_content[b][0:64, :], 0.0).then_inc(stack_set, 1)
                pool.wait_ge(half_set, 2)
                pool.memset(kp_stack[:, :, :], 0.0).then_inc(stack_zero, 1)
                for b in range(3):
                    pool.memset(k_stack[b][0:64, :], 0.0).then_inc(stack_set, 1)

                def front(g):
                    pool.wait_ge(stats_p, g + 1)
                    ln_rstd(pool, count, rstd_p)
                    passed_since(pool, turned_p, 2 * g)
                    wait_x(pool, g)
                    carry(pool)
                    pool.tensor_copy(c_now[:, :, :], tiles(C[:, g, :])).then_inc(c_staged, 1)

                def body(g, b, before):
                    if has_next(g):
                        front(g + 1)
                    pool.wait_ge(q_second, g + 1)
                    pool.tensor_tensor(q_part[b][:, 2, :], qr[:, :], q_part[b][:, 1, :], ALU.subtract)\
                        .then_inc(q_third, 1)
                    pool.wait_ge(k_second, g + 1)
                    pool.tensor_tensor(k_part[b][:, 2, :], kr[:, :], k_part[b][:, 1, :], ALU.subtract)\
                        .then_inc(k_third, 1)

                front(0)
                over_groups(pool, body, count)

            @block.scalar
            def _(act):
                act.wait_ge(loaded, 48)
                act.activation(tanh_x[:, :], prm("g_xattn"), ACT.Tanh).then_inc(gates_ready, 1)
                act.activation(tanh_f[:, :], prm("g_ffn"), ACT.Tanh).then_inc(gates_ready, 1)
                for b in range(3):
                    act.activation(q_content[b][64:P, :].rearrange("p (n i) -> p n i", n=BLK),
                                   cst("same_token")[64:P, :].rearrange("p (o i) -> p o i", o=1)
                                   .broadcast_to([64, BLK, SEQ]), ACT.Copy).then_inc(stack_set, 1)
                act.activation(tokens2[:, :].rearrange("p (i n) -> p i n", n=BLK),
                               cst("same_token").rearrange("p (i o) -> p i o", o=1).broadcast_to([P, SEQ, BLK]),
                               ACT.Copy).then_inc(stack_set, 1)

                def front(g):
                    act.wait_ge(turned_p, 2 * g + 2)
                    passed_since(act, v_done, g)
                    act.activation(refT[:, :, 0:SEQ], T_c.rearrange("p (n i) -> p n i", n=GN), ACT.Copy)\
                        .then_inc(refc_ready, 1)

                def body(g, b, before):
                    act.wait_ge(qz_ready, g + 1)
                    passed_since(act, q_stored[b], 48 * before)
                    act.activation(q_part[b][:, 0, :], qz[:, :], ACT.Copy).then_inc(q_first, 1)
                    act.wait_ge(k_done, g + 1)
                    passed_since(act, k_stored[b], 48 * before)
                    act.activation(k_part[b][:, 0, :], K_ps.rearrange("p a b -> p (a b)"), ACT.Copy)\
                        .then_inc(k_first, 1)
                    act.wait_ge(qr_ready, g + 1)
                    act.activation(q_part[b][:, 1, :], qr[:, :], ACT.Copy).then_inc(q_second, 1)
                    if has_next(g):
                        front(g + 1)
                    act.wait_ge(kr_ready, g + 1)
                    act.activation(k_part[b][:, 1, :], kr[:, :], ACT.Copy).then_inc(k_second, 1)

                front(0)
                over_groups(act, body)

            @block.vector
            def _(dve):
                count = Count(dve, dve_p)
                dve.wait_ge(loaded, 48)
                dve.wait_ge(pe_turned, 1)
                dve.tensor_copy(peT[:, :], T_x[:, 0:P]).then_inc(peT_ready, 1)
                count.step(dve.tensor_tensor(bias_diff[:, :], prm("pb"), prm("cb"), ALU.subtract))
                dve.tensor_scalar(bias_rows[:, :], cst("head_rows"), bias_diff[:, :], SCALE0,
                                  ALU.mult, ALU.mult).then_inc(bias_ready, 1)
                dve.wait_ge(kp_done, 1)
                dve.tensor_copy(kpT[:, :], T_c[:, 0:P]).then_inc(kpT_ready, 1)
                dve.wait_ge(kpT_ready, 1)

                def split(src, rest, part):
                    count.step(dve.tensor_copy(part[:, 0, :], src))
                    count.step(dve.tensor_tensor(rest, src, part[:, 0, :], ALU.subtract))
                    count.step(dve.tensor_copy(part[:, 1, :], rest))
                    return dve.tensor_tensor(part[:, 2, :], rest, part[:, 1, :], ALU.subtract)

                count.step(split(kpT[:, :], kp_r[:, :], kp_part))
                dve.wait_ge(bp_done, 1)
                count.step(dve.tensor_copy(bp[:, :], Q_ps[0:H0, 0:KEYS]))
                split(bp[:, :], kp_r[0:H0, :], bp_part).then_inc(kp_split, 1)
                for b in range(3):
                    dve.tensor_copy(q_stack[b][:, :], cst("bias_on").broadcast_to([P, UTOK])).then_inc(stack_set, 1)
                dve.memset(ones_rows[:, :], 1.0)
                count.step(dve.tensor_copy(same_block[:, :], cst("same_block", 32 * PARTS)))
                dve.wait_ge(mask_loaded, 32)
                count.step(dve.tensor_scalar(neg_mask[:, :], mask_sb[:, :], NEG_INF, None, ALU.mult))
                count.step(dve.tensor_copy(mask_first[:, :], neg_mask[:, :]))
                for b in range(3):
                    dve.tensor_copy(k_stack[b][64:P, :].rearrange("p (n r) -> p n r", n=BLK),
                                    mask_first[64:P, :].rearrange("p (o r) -> p o r", o=1)
                                    .broadcast_to([64, BLK, KEYS])).then_inc(mask_ready, 1)
                count.step(dve.tensor_tensor(mask_rest[:, :], neg_mask[:, :], mask_first[:, :], ALU.subtract))
                count.step(dve.tensor_copy(mask_second[:, :], mask_rest[:, :]))
                dve.scalar_tensor_tensor(out=mask_parts[:, :], in0=mask_second[:, :], scalar=cst("minus_upper"),
                                         in1=mask_rest[:, :], op0=ALU.mult, op1=ALU.add).then_inc(mask_ready, 1)

                def norm_stats(g):
                    wait_x(dve, g)
                    ln_stats(dve, count, tiles(X[:, g, :]), stats_p)

                def norm(g):
                    dve.wait_ge(stats_p, g + 1)
                    dve.wait_ge(rstd_p, g + 1)
                    passed_since(dve, turned_p, 2 * g)
                    ln_apply(dve, xn, tiles(X[:, g, :])).then_inc(xn_p, 1)

                def front(g):
                    dve.wait_ge(turned_p, 2 * g + 1)
                    passed_since(dve, v_done, g)
                    dve.tensor_copy(refT[:, :, SEQ:KEYS], T_x.rearrange("p (n i) -> p n i", n=GN))\
                       .then_inc(refx_ready, 1)

                def body(g, b, before):
                    if has_next(g):
                        carry(dve)
                        norm_stats(g + 1)
                    dve.wait_ge(q_done, g + 1)
                    passed_since(dve, q_first, g)
                    dve.tensor_scalar(qz[:, :], Q_ps, prm("cb"), SCALE0, ALU.add, ALU.mult)\
                       .then_inc(qz_ready, 1)
                    if has_next(g):
                        norm(g + 1)
                    dve.wait_ge(q_first, g + 1)
                    passed_since(dve, q_third, g)
                    dve.tensor_tensor(qr[:, :], qz[:, :], q_part[b][:, 0, :], ALU.subtract).then_inc(qr_ready, 1)
                    dve.wait_ge(k_first, g + 1)
                    passed_since(dve, k_third, g)
                    dve.tensor_tensor(kr[:, :], K_ps.rearrange("p a b -> p (a b)"), k_part[b][:, 0, :],
                                      ALU.subtract).then_inc(kr_ready, 1)
                    if has_next(g):
                        front(g + 1)
                    dve.wait_ge(v_done, g + 1)
                    dve.tensor_copy(
                        V_all[:, :, :, :].rearrange("p (g n) h s -> p g (n h s)", n=GN)[:, g, :],
                        V_ps.rearrange("p a c -> p (a c)")).then_inc(v_kept, 1)

                norm_stats(0)
                norm(0)
                front(0)
                over_groups(dve, body, count)

            @block.tensor
            def _(pe):
                pe.wait_ge(loaded, 48)
                pe.transpose(T_x[:, 0:P], wt0("pe"), ident).then_inc(pe_turned, 1)
                pe.wait_ge(peT_ready, 1)
                pe.matmul(T_c[:, 0:P], wt0("wkp"), peT[:, :], start=True, stop=True).then_inc(kp_done, 1)
                pe.wait_ge(kpT_ready, 1)
                pe.wait_ge(bias_ready, 1)
                pe.matmul(Q_ps[0:H0, 0:KEYS], bias_rows[:, :], kpT[:, :], start=True, stop=True)\
                  .then_inc(bp_done, 1)
                pe.wait_ge(kp_split, 1)

                def front(g):
                    pe.wait_ge(xn_p, g + 1)
                    passed_since(pe, refx_ready, g)
                    for t in range(GT):
                        mm = pe.transpose(T_x[:, t * P:(t + 1) * P], xn[:, t, :], ident)
                    mm.then_inc(turned_p, 1)
                    passed_since(pe, refc_ready, g)
                    pe.wait_ge(c_staged, g + 1)
                    for t in range(GT):
                        mm = pe.transpose(T_c[:, t * P:(t + 1) * P], c_now[:, t, :], ident)
                    mm.then_inc(turned_p, 1)

                def body(g, b, before):
                    pe.wait_ge(refx_ready, g + 1)
                    passed_since(pe, qz_ready, g)
                    pe.matmul(Q_ps, wt0("wq"), refT[:, :, SEQ:KEYS], start=True, stop=True).then_inc(q_done, 1)
                    pe.wait_ge(refc_ready, g + 1)
                    passed_since(pe, kr_ready, g)
                    for a in range(2):
                        mm = pe.matmul(K_ps[:, a, :], wt0("wkc"), refT[:, a * 4:a * 4 + 4, :],
                                       start=True, stop=True)
                    mm.then_inc(k_done, 1)
                    passed_since(pe, v_kept, g)
                    for n in range(GN):
                        mm = pe.matmul(V_ps[:, n // 4, (n % 4) * P:(n % 4 + 1) * P], refT[:, n, :],
                                       wt0("wv"), start=True, stop=True)
                    mm.then_inc(v_done, 1)
                    if has_next(g):
                        front(g + 1)

                front(0)
                over_groups(pe, body)

        proj_ctx.close()

        window = [sb(f"window{b}", [P, WIN], BF16, att_ctx) for b in range(3)]
        probs = [sb(f"probs{b}", [P, UTOK], stack=att_ctx) for b in range(2)]
        max_rows = [sb(f"max_rows{b}", [32 * PARTS, UTOK], BF16, att_ctx) for b in range(2)]
        max_quads = [sb(f"max_quads{b}", [P, 32], stack=att_ctx) for b in range(2)]
        neg_max = sb("neg_max", [32, 32], stack=att_ctx)
        max_rest = sb("max_rest", [32, 32], stack=att_ctx)
        max_mid = sb("max_mid", [32, 32], BF16, att_ctx)
        max_part = sb("max_part", [32 * PARTS, 32], BF16, att_ctx)
        v_now = [sb(f"v_now{b}", [P, BLK, 2 * S0], stack=att_ctx) for b in range(2)]
        o_sum = [sb(f"o_sum{b}", [P, UTOK], stack=att_ctx) for b in range(2)]
        window_ready = sem("window_ready")
        scored = sem("scored")
        quads_ready = sem("quads_ready")
        quads_turned = sem("quads_turned")
        max_ready = sem("max_ready")
        rows_ready = sem("rows_ready")
        shifted = sem("shifted")
        exp_done = sem("exp_done")
        values_done = sem("values_done")
        dve_a = sem("dve_a")
        v_staged = sem("v_staged")
        o_copied = sem("o_copied")
        o_moved = [sem(f"o_moved{b}") for b in range(2)]
        S_ps = [psum[:, 2 * b:2 * b + 2, :] for b in range(3)]
        R_ps = psum[0:32, 6, 0:P]
        o_rows = [slice(32 * (b + 1), 32 * (b + 1) + 2 * S0) for b in range(2)]
        O_ps = [psum[o_rows[b], 6:8, :] for b in range(2)]

        def is_unit(it, k):
            return not isinstance(it, int) or 0 <= ROUND * it + k < UNITS

        def wait_units(eng, sem, it, k, per=1, of=1, ahead=0):
            done = per * ((ROUND // of) * it + (k - 1) // of + 1) + ahead
            if not isinstance(done, int) or done > 0:
                eng.wait_ge(sem, done)

        def run_steps(eng, step, rounds=ROUNDS, count=None, per=0):
            for k in range(-3, 1):
                step(0, k)
            with eng.Fori(0, rounds) as it:
                if count:
                    count.enter(it, per)
                for k in range(1, ROUND + 1):
                    step(it, k)
                if count:
                    count.leave(rounds)
            for k in range(1, UNITS - ROUND * rounds):
                step(rounds, k)

        with nc.Block() as block:
            @block.sync
            def _(sp):
                for b in range(2):
                    sp.sem_inc(o_moved[b], 32)

                for b in range(2):
                    sp.wait_ge(q_stored[b], 48 * (GROUPS // 2))
                    sp.wait_ge(k_stored[b], 48 * (GROUPS // 2))

                def step(it, k):
                    if is_unit(it, k):
                        b, h, blk = k % 2, head_of(it, k), k % NBLK
                        wait_units(sp, o_copied, it, k + 1, ahead=1)
                        carry(sp)
                        at, rows = blk * UTOK, o_rows[b]
                        sp.dma_start(ot_scratch[h, :, at:at + UTOK], o_sum[b][rows.start:rows.start + S0, :])\
                          .then_inc(o_moved[b], 16)
                        sp.dma_start(st_scratch[h, :, at:at + UTOK], o_sum[b][rows.start + S0:rows.stop, :])\
                          .then_inc(o_moved[b], 16)
                    if is_unit(it, k + 6):
                        wait_units(sp, scored, it, k + 4)
                        carry(sp)
                        load_unit(sp, it, k + 6)

                run_steps(sp, step, ROUNDS - 1)
                for b in range(2):
                    sp.wait_ge(o_moved[b], 32 * UNITS // 2 + 32)

            @block.gpsimd
            def _(pool):
                for b in range(2):
                    pool.memset(v_now[b][:, :, S0:2 * S0], 1.0)
                vv = V_all[:, :, :, :].rearrange("p (b n) h s -> p b n h s", b=NBLK)

                def step(it, k):
                    if is_unit(it, k + 3) and (k + 3) % NBLK == 0:
                        wait_units(pool, scored, it, k + 2)
                        carry(pool)
                        pool.tensor_copy(window[(k + 3) // NBLK % 3][:, :], kp_stack[:, head_of(it, k + 3), :])\
                            .then_inc(window_ready, 1)
                    if is_unit(it, k + 1):
                        wait_units(pool, values_done, it, k)
                        carry(pool)
                        pool.tensor_copy(v_now[(k + 1) % 2][:, :, 0:S0],
                                         vv[:, (k + 1) % NBLK, :, head_of(it, k + 1), :])\
                            .then_inc(v_staged, 1)

                run_steps(pool, step)

            @block.scalar
            def _(act):
                act.sem_inc(o_copied, 1)

                def step(it, k):
                    if is_unit(it, k):
                        b = k % 2
                        wait_units(act, values_done, it, k + 1)
                        wait_units(act, o_moved[b], it, k - 1, 32, 2, ahead=32)
                        act.activation(o_sum[b][o_rows[b], :].rearrange("p (a c) -> p a c", a=2), O_ps[b], ACT.Copy)\
                           .then_inc(o_copied, 1)
                    if is_unit(it, k + 1):
                        wait_units(act, shifted, it, k + 2)
                        wait_units(act, values_done, it, k)
                        act.activation(probs[(k + 1) % 2][:, :].rearrange("p (n i) -> p i n", n=BLK),
                                       S_ps[(k + 1) % 3].rearrange("p a (i n) -> p (a i) n", n=BLK), ACT.Exp)\
                           .then_inc(exp_done, 1)

                run_steps(act, step)

            @block.vector
            def _(dve):
                count = Count(dve, dve_a)
                def step(it, k):
                    if is_unit(it, k + 2):
                        wait_units(dve, quads_turned, it, k + 3)
                        count.step(dve.tensor_reduce(neg_max[:, :], R_ps.rearrange("p (q c) -> p c q", q=4), AX,
                                                     ALU.max, negate=True))
                        count.step(dve.tensor_copy(max_part[0:32, :], neg_max[:, :]))
                        count.step(dve.tensor_tensor(max_rest[:, :], neg_max[:, :], max_part[0:32, :], ALU.subtract))
                        dve.tensor_copy(max_part[32:64, :], max_rest[:, :])
                        count.step(dve.tensor_copy(max_mid[:, :], max_rest[:, :]))
                        dve.tensor_tensor(max_part[64:96, :], max_rest[:, :], max_mid[:, :], ALU.subtract)\
                           .then_inc(max_ready, 1)
                        wait_units(dve, max_ready, it, k + 3)
                        wait_units(dve, shifted, it, k + 1)
                        dve.tensor_tensor(
                            max_rows[k % 2][:, :].rearrange("p (b c) -> p b c", c=32),
                            max_part[:, :].rearrange("p (o c) -> p o c", o=1).broadcast_to([32 * PARTS, 32, 32]),
                            same_block[:, :].rearrange("p (b o) -> p b o", o=1).broadcast_to([32 * PARTS, 32, 32]),
                            ALU.mult).then_inc(rows_ready, 1)
                    if is_unit(it, k + 3):
                        wait_units(dve, scored, it, k + 4)
                        dve.tensor_reduce(max_quads[(k + 3) % 2][:, :],
                                          S_ps[(k + 3) % 3].rearrange("p a (b c) -> p (a b) c", c=32), AX, ALU.max,
                                          apply_transpose=True).then_inc(quads_ready, 1)

                run_steps(dve, step, count=count, per=4 * ROUND)

            @block.tensor
            def _(pe):
                def content(it, k, part):
                    b = k % 3
                    sv = S_ps[b].rearrange("p a (i n) -> p a i n", n=BLK)
                    qn = q_content[b][:, :].rearrange("p (n a i) -> p n a i", n=BLK, a=2)
                    if part == 0:
                        wait_units(pe, exp_done, it, k - 2)
                        for a in range(2):
                            pe.matmul(S_ps[b][:, a, :], mask_parts[:, :], tokens2[:, 512 * a:512 * a + 512],
                                      start=True, stop=False, skip_group_check=True)
                        wait_units(pe, unit_loaded[b], it, k + 1, 64, 3)
                    for n in range(part * BLK // 2, (part + 1) * BLK // 2):
                        for a in range(2):
                            pe.matmul(sv[:, a, :, n], k_stack[b][:, n * KEYS:(n + 1) * KEYS], qn[:, n, a, :],
                                      start=False, stop=False, skip_group_check=True)

                def positions(it, k):
                    b, wnd = k % 3, window[k // NBLK % 3]
                    sv = S_ps[b].rearrange("p a (i n) -> p a i n", n=BLK)
                    qi = q_stack[b][:, :].rearrange("p (n i) -> p i n", n=BLK)
                    if k % NBLK == 0:
                        pe.wait_ge(window_ready, head_of(it, k) + 1)
                    for i in range(SEQ):
                        mm = pe.matmul(sv[:, i // 32, i % 32, :], wnd[:, SEQ - 1 - i:SEQ - 1 - i + KEYS], qi[:, i, :],
                                       start=False, stop=False, skip_group_check=True)
                    mm.then_inc(scored, 1)

                def step(it, k):
                    if is_unit(it, k):
                        b = k % 2
                        wait_units(pe, v_staged, it, k + 1)
                        wait_units(pe, exp_done, it, k + 1)
                        wait_units(pe, o_copied, it, k - 1, ahead=1)
                        for n in range(BLK):
                            mm = pe.matmul(O_ps[b][:, n // 8, n % 8 * SEQ:(n % 8 + 1) * SEQ], v_now[b][:, n, :],
                                           probs[b][:, n * SEQ:(n + 1) * SEQ], start=True, stop=True,
                                           tile_position=(0, 32 * (b + 1)))
                        mm.then_inc(values_done, 1)
                    if is_unit(it, k + 3):
                        content(it, k + 3, 0)
                    if is_unit(it, k + 2):
                        wait_units(pe, quads_ready, it, k + 3)
                        wait_units(pe, max_ready, it, k + 2)
                        pe.transpose(R_ps, max_quads[k % 2][:, :], ident).then_inc(quads_turned, 1)
                    if is_unit(it, k + 3):
                        content(it, k + 3, 1)
                    if is_unit(it, k + 1):
                        wait_units(pe, rows_ready, it, k + 2)
                        for a in range(2):
                            mm = pe.matmul(S_ps[(k + 1) % 3][:, a, :], ones_rows[:, :],
                                           max_rows[(k + 1) % 2][:, 512 * a:512 * a + 512],
                                           start=False, stop=True, skip_group_check=True)
                        mm.then_inc(shifted, 1)
                    if is_unit(it, k + 3):
                        positions(it, k + 3)

                run_steps(pe, step)
        att_ctx.close()
        heads_ctx.close()

        W1E = sb("W1E", [P, NE, HID])
        W2E = sb("W2E", [P, NE, HC, D])
        B2E = sb("B2E", [NE, D])
        experts_loaded = sem("experts_loaded")

        R = {name: sem(name) for name in (
            "first_loaded o_loaded oT_ready y_done x1_ready stats_r rstd_r dve_r pool_r xn_ready x_turned xT_ready "
            "even1_picked even2_picked odd_ready up_done up_ready even1_ready even2_ready h_done h_ready low_done "
            "w2x_set low_ready low_turned lowT_ready ffn_done "
            "c_staged1 c_turned cT_ready cn_ready cn_turned knT_ready k_done1 k_ready1 v_done1 v_ready1 "
            "xm_ready xm_turned qnT_ready q_done1 q_ready1 scored1 clipped s_ready e_ready summed e_turned "
            "eT_ready o_done1 o_ready1 on_ready on_turned onT_ready gate_done gelu_ready "
            "x3_ready x3_turned x3T_ready logits_done routed second_ready gates_done g_turned gT_ready bias_done "
            "acc_ready hidden_done relu_done expert_done added res_ready").split()}
        stored = [sem(f"stored{b}") for b in range(2)]
        oT = sb("oT", [P, GTOK])
        x1 = sb("x1", [P, GT, D])
        xT = sb("xT", [P, GTOK])
        odd1 = sb("odd1", [P, GN, 4])
        even1 = sb("even1", [32, 4, P])
        picked2 = sb("picked2", [32, GT, 32])
        even2 = sb("even2", [32, GT, 4, 32])
        hT = sb("hT", [P, HC, GTOK])
        W_OUT = D + 8 * HC
        w2x = sb("w2x", [P, GT, HC, W_OUT])
        low = sb("low", [P, GT * HC, 8])
        c2 = sb("c2", [P, GT, D])
        cn = sb("cn", [P, GT, D])
        knT = sb("knT", [P, GTOK])
        cT = sb("cT", [P, GTOK])
        up, masked2, lowT, fin = knT[0:32, :], cT[0:32, :], cT[0:32, :], cn
        k1 = [sb(f"k1_{b}", [P, GTOK]) for b in range(2)]
        v1 = [sb(f"v1_{b}", [P, GT * 4, 2, 2 * S1]) for b in range(2)]
        xm = sb("xm", [P, GT, D])
        qnT = sb("qnT", [P, GTOK])
        q1 = sb("q1", [P, GN, 2, SEQ])
        s1 = sb("s1", [P, 4, GTOK])
        top1 = sb("top1", [P, 4 * GN])
        sum1 = sb("sum1", [P, 4 * GN])
        inv1 = sb("inv1", [P, 4 * GN])
        on = sb("on", [P, GT, D])
        gl = sb("gl", [P, GT, D])
        gT = on[0:NE, :, :].rearrange("p t d -> p (t d)")
        o1, onT, x3 = xm, qnT, gl
        x3T = [sb(f"x3T_{b}", [P, GTOK]) for b in range(2)]
        logits = sb("logits", [P, GT, NE])
        best = sb("best", [P, GT, NE])
        place = sb("place", [P, GT, NE], U32)
        placef = sb("placef", [P, GT, NE])
        second = sb("second", [P, GT])
        both = sb("both", [P, GT])
        weight = sb("weight", [P, 2, GT])
        pick = sb("pick", [P, 2, GT, NE])
        gates = [sb(f"gates{b}", [P, GT, NE]) for b in range(2)]
        hE = [sb(f"hE{b}", [P, HC, GTOK]) for b in range(2)]
        acc = [sb(f"acc{b}", [P, GT, D]) for b in range(2)]
        ov = out.rearrange("(g t m) s d -> (m s) g t d", t=GT, m=2)
        bank = [psum[:, n, :] for n in range(8)]
        ffn_ps = psum[:, 0:2, 0:2 * W_OUT].rearrange("p b (u c) -> p b u c", u=2)
        AHEAD = {"relu_done": 2, "expert_done": 2, "added": 1}
        LOWER_AT = {0: 0, 1: 1, 12: 2, 2: 3, 3: 6, 4: 8, 5: 10, 6: 12,
                    7: 14, 8: 16, 9: 18, 10: 21, 13: 23, 11: 24}
        UPPER_AT = {0: 0, 1: 2, 2: 3, 3: 4, 4: 7, 5: 8, 6: 9, 7: 10,
                    8: 12, 15: 13, 9: 15, 10: 17, 16: 18, 11: 19, 12: 20, 17: 21, 18: 22, 13: 24, 14: 26}
        DVE_STEPS, NORMS = 25, 6
        before = {}

        def half_before(g, b):
            return (g - b) // 2 if isinstance(g, int) else before[b]

        def since(eng, name, value):
            if not isinstance(value, int) or value > 0:
                eng.wait_ge(R[name], value + AHEAD.get(name, 0))

        def over_rounds(eng, lower, upper, experts, counts=()):
            def a_round(g_lower, g_upper, g_experts, b):
                low_at = {at: s for s, at in LOWER_AT.items()}
                up_at = {at: s for s, at in UPPER_AT.items()}
                for slot in range(3 * (NE + 1)):
                    if g_experts is not None:
                        experts(g_experts, b, slot // 3, slot % 3)
                    if g_lower is not None and slot in low_at:
                        lower(low_at[slot], g_lower, b)
                    if g_upper is not None and slot in up_at:
                        upper(up_at[slot], g_upper, 1 - b)

            a_round(0, None, None, 0)
            a_round(1, 0, None, 1)
            with eng.Fori(0, GROUPS // 2 - 1) as i:
                for count, per in counts:
                    count.enter(i, per)
                before[0], before[1] = i + 1, i
                a_round(2 * i + 2, 2 * i + 1, 2 * i, 0)
                a_round(2 * i + 3, 2 * i + 2, 2 * i + 1, 1)
                for count, per in counts:
                    count.leave(GROUPS // 2 - 1)
            a_round(None, GROUPS - 1, GROUPS - 2, 0)
            a_round(None, None, GROUPS - 1, 1)

        with nc.Block() as block:
            @block.sync
            def _(sp):
                sp.sem_inc(stored[1], 16)
                both = ((sums, st_scratch.rearrange("h s t -> (h s) t")),
                        (O_all, ot_scratch.rearrange("h s t -> (h s) t")))
                for dst, src in both:
                    sp.dma_start(dst[:, 0, :], src[:, 0:GTOK]).then_inc(R["first_loaded"], 16)
                for dst, src in both:
                    sp.dma_start(dst[:, 1:GROUPS, :].rearrange("p g t -> p (g t)"), src[:, GTOK:])\
                      .then_inc(R["o_loaded"], 16)
                sp.dma_start(W1E[:, :, :], w1e).then_inc(experts_loaded, 16)
                sp.dma_start(W2E[:, :, :, :], w2e).then_inc(experts_loaded, 16)
                sp.dma_start(B2E[:, :], b2e).then_inc(experts_loaded, 16)
                with sp.Fori(0, GROUPS // 2) as i:
                    for b in range(2):
                        sp.wait_ge(R["res_ready"], 2 * i + b + 1)
                        sp.dma_start(ov[:, 2 * i + b, :, :], acc[b][:, :, :]).then_inc(stored[b], 16)
                for b in range(2):
                    sp.wait_ge(stored[b], 16 * (GROUPS // 2 + b))

            @block.gpsimd
            def _(pool):
                count = Count(pool, R["pool_r"])

                def stage(g):
                    since(pool, "c_turned", g)
                    since(pool, "cn_ready", g)
                    carry(pool)
                    pool.tensor_copy(c2[:, :, :], tiles(C[:, g, :])).then_inc(R["c_staged1"], 1)

                def norms(first, n):
                    for k in range(n):
                        pool.wait_ge(R["stats_r"], first + k + 1)
                        ln_rstd(pool, count, R["rstd_r"])

                stage(0)
                pool.memset(w2x[:, :, :, D:], 0.0).then_inc(R["w2x_set"], 1)
                norms(0, 1)
                stage(1)
                norms(1, 3)
                with pool.Fori(1, GROUPS - 1) as g:
                    count.enter(g - 1, 6)
                    norms(6 * g - 2, 3)
                    stage(g + 1)
                    norms(6 * g + 1, 3)
                    count.leave(GROUPS - 2)
                norms(6 * GROUPS - 8, 6)
                norms(6 * GROUPS - 2, 2)

            @block.scalar
            def _(act):
                act.sem_inc(R["relu_done"], AHEAD["relu_done"])
                for t in range(GT):
                    act.activation(w2x[:, t, :, 0:D], wt1("w2t").rearrange("p (r d) -> p r d", r=HC), ACT.Copy)\
                       .then_inc(R["w2x_set"], 1)

                def copy(dst, src, need, ready, n, **kw):
                    act.wait_ge(R[need], n)
                    act.activation(dst, src, kw.pop("func", ACT.Copy), **kw).then_inc(R[ready], 1)

                affine = dict(func=ACT.Identity, bias=prm("pre_b"), scale=prm("pre_g"))

                def lower(s, g, b):
                    if s == 1:
                        since(act, "ffn_done", g)
                        copy(cT[:, :], bank[0], "c_turned", "cT_ready", g + 1)
                        copy(knT[:, :], bank[2], "cn_turned", "knT_ready", g + 1, **affine)
                    if s == 2:
                        since(act, "scored1", 4 * (g - 1))
                        copy(k1[b][:, :], bank[0], "k_done1", "k_ready1", g + 1)
                        since(act, "o_done1", g - 1)
                        for m in range(2):
                            copy(v1[b][:, :, m, :], bank[2].rearrange("p (c s) -> p c s", s=2 * S1), "v_done1",
                                 "v_ready1", g + 1, scale=cst("seq_of_tile")[:, m:m + 1])
                    if s == 3:
                        copy(xT[:, :], bank[0], "x_turned", "xT_ready", g + 1)
                    if s in (5, 6):
                        for e in (2 * s - 10, 2 * s - 9):
                            copy(hT[:, e, :], bank[1 + e % 2], "h_done", "h_ready", HC * g + e + 1,
                                 func=ACT.Gelu, bias=prm("b1_0", e))
                    if s == 9:
                        copy(lowT, bank[2][0:32, :], "low_turned", "lowT_ready", g + 1)

                def upper(s, g, b):
                    if s == 0:
                        copy(qnT[:, :], bank[3], "xm_turned", "qnT_ready", g + 1, **affine)
                    if s == 1:
                        since(act, "scored1", 4 * g)
                        for a in range(2):
                            copy(q1[:, :, a, :], bank[4].rearrange("p (n i) -> p n i", n=GN), "q_done1", "q_ready1",
                                 g + 1, scale=cst("head_of_pair")[:, a:a + 1])
                    if s == 4:
                        for c in range(4):
                            copy(s1[:, c, :], s1[:, c, :], "s_ready", "e_ready", g + 1, func=ACT.Exp)
                    if s in (6, 7):
                        act.wait_ge(R["summed"], g + 1)
                        for c in (2 * s - 12, 2 * s - 11):
                            copy(s1[:, c, :], bank[3 + c % 2], "e_turned", "eT_ready", 4 * g + c + 1)
                    if s == 9:
                        copy(onT[:, :], bank[3], "on_turned", "onT_ready", g + 1)
                    if s == 10:
                        copy(gl[:, :, :].rearrange("p t d -> p (t d)"), bank[4], "gate_done", "gelu_ready", g + 1,
                             func=ACT.Gelu)
                    if s == 11:
                        copy(x3T[b][:, :], bank[3], "x3_turned", "x3T_ready", g + 1)
                    if s == 17:
                        copy(second[:, :], both[:, :], "routed", "second_ready", g + 1, func=ACT.Exp)
                    if s == 13:
                        copy(gT, bank[3][0:NE, :], "g_turned", "gT_ready", g + 1)

                def experts(g, b, e, third):
                    if e < NE and third == 0:
                        for c in range(HC):
                            act.wait_ge(R["hidden_done"], NE * HC * g + HC * e + c + 1)
                            if c == 0:
                                since(act, "expert_done", NE * g + e - 1)
                            act.activation(hE[e % 2][:, c, :], bank[5 + c % 2], ACT.Relu,
                                           bias=prm("b1_1", HC * e + c)).then_inc(R["relu_done"], 1)

                over_rounds(act, lower, upper, experts)

            @block.vector
            def _(dve):
                count = Count(dve, R["dve_r"])
                same_e = cst("same_e", 32)

                norms = Count(dve, R["stats_r"])
                dve.sem_inc(R["added"], AHEAD["added"])

                def norm_stats(src):
                    ln_stats(dve, count, src, R["stats_r"])
                    norms.k += 1

                def norm_apply(dst, src):
                    done = norms.base + norms.it * norms.per + norms.k
                    dve.wait_ge(R["stats_r"], done)
                    dve.wait_ge(R["rstd_r"], done)
                    return ln_apply(dve, dst, src)

                def row(name):
                    return prm(name).rearrange("p (o d) -> p o d", o=1).broadcast_to([P, GT, D])

                def turn_sums(group):
                    count.step(dve.reciprocal(sums[:, group, :], sums[:, group, :]))

                def lower(s, g, b):
                    xg = tiles(X[:, g, :])
                    if isinstance(g, int) and s in (5, 8):
                        dve.wait_ge(R["o_loaded"], 32)
                        for group in {(0, 5): (1, 2), (0, 8): (3,), (1, 5): (4, 5), (1, 8): (6, 7)}[g, s]:
                            turn_sums(group)
                    if s == 0:
                        if isinstance(g, int) and g == 0:
                            dve.wait_ge(R["first_loaded"], 32)
                            turn_sums(0)
                        since(dve, "y_done", g)
                        dve.tensor_tensor(oT[:, :], O_all[:, g, :], sums[:, g, :], ALU.mult)\
                           .then_inc(R["oT_ready"], 1)
                        since(dve, "cn_turned", g)
                        dve.wait_ge(R["c_staged1"], g + 1)
                        norm_stats(c2)
                    if s == 1:
                        norm_apply(cn, c2).then_inc(R["cn_ready"], 1)
                        dve.wait_ge(R["y_done"], g + 1)
                        dve.scalar_tensor_tensor(out=x1[:, :, :], in0=tiles(bank[1]), scalar=tanh_x[:, 0:1], in1=xg,
                                                 op0=ALU.mult, op1=ALU.add).then_inc(R["x1_ready"], 1)
                        dve.wait_ge(R["x1_ready"], g + 1)
                        norm_stats(x1)
                    if s == 12:
                        norm_apply(xn, x1).then_inc(R["xn_ready"], 1)
                    if s == 3:
                        dve.wait_ge(R["even1_picked"], g + 1)
                        dve.tensor_tensor(
                            even1[:, :, :],
                            bank[1][0:32, 0:P].rearrange("p (o a) -> p o a", o=1).broadcast_to([32, 4, P]),
                            same_e.rearrange("p (e o) -> p e o", o=1).broadcast_to([32, 4, P]), ALU.mult)\
                           .then_inc(R["even1_ready"], 1)
                        dve.wait_ge(R["xT_ready"], g + 1)
                        xv = xT[:, :].rearrange("p (n i) -> p n i", n=GN)
                        if isinstance(g, int):
                            dve.wait_ge(R["w2x_set"], GT + 1)
                        for r in range(HC):
                            dve.tensor_copy(w2x[:, :, r, D + 8 * r:D + 8 * r + 8].rearrange(
                                "p t (m e) -> p t m e", m=2),
                                xv[:, :, 10:18:2].rearrange("p (t m) e -> p t m e", m=2))
                        dve.tensor_copy(odd1[:, :, :], xv[:, :, 2:10:2]).then_inc(R["odd_ready"], 1)
                        dve.wait_ge(R["even2_picked"], g + 1)
                        count.step(dve.tensor_tensor(
                            tiles(masked2), tiles(bank[2][0:32, :]),
                            cst("same_r", 32).rearrange("p (o a) -> p o a", o=1).broadcast_to([32, GT, P]),
                            ALU.mult))
                        count.step(dve.tensor_reduce(picked2[:, :, :].rearrange("p t a -> p (t a)"),
                                                     masked2.rearrange("p (c r) -> p c r", r=4), AX, ALU.add))
                        dve.tensor_tensor(
                            even2[:, :, :, :],
                            picked2[:, :, :].rearrange("p t (o a) -> p t o a", o=1).broadcast_to([32, GT, 4, 32]),
                            same_e.rearrange("p (u e o) -> p u e o", o=1, u=1).broadcast_to([32, GT, 4, 32]),
                            ALU.mult).then_inc(R["even2_ready"], 1)
                    if s == 4:
                        dve.wait_ge(R["up_done"], g + 1)
                        dve.scalar_tensor_tensor(out=up, in0=bank[1][0:32, :], scalar=prm("scale")[0:32, :],
                                                 in1=cst("same_seq", 32), op0=ALU.mult, op1=ALU.mult)\
                           .then_inc(R["up_ready"], 1)
                    if s == 8:
                        dve.wait_ge(R["low_done"], g + 1)
                        for half in range(2):
                            ins = dve.scalar_tensor_tensor(
                                out=low[:, 8 * half:8 * half + 8, :].rearrange("p (u r) e -> p u (r e)", u=2),
                                in0=ffn_ps[:, half, :, D:], scalar=prm("scale"),
                                in1=cst("same_seq_tok").rearrange("p (u c) -> p u c", u=1)
                                .broadcast_to([P, 2, 8 * HC]), op0=ALU.mult, op1=ALU.mult)
                        ins.then_inc(R["low_ready"], 1)
                    if s == 10:
                        dve.wait_ge(R["ffn_done"], g + 1)
                        count.step(dve.tensor_tensor(
                            fin[:, :, :].rearrange("p (b u) d -> p b u d", b=2), ffn_ps[:, :, :, 0:D],
                            prm("b2_0").rearrange("p (b u d) -> p b u d", b=1, u=1).broadcast_to([P, 2, 2, D]),
                            ALU.add))
                        count.step(dve.scalar_tensor_tensor(out=xg, in0=fin[:, :, :], scalar=tanh_f[:, 0:1],
                                                            in1=x1[:, :, :], op0=ALU.mult, op1=ALU.add))
                        carry(dve)
                        norm_stats(xg)
                    if s == 13:
                        count.step(norm_apply(xn, xg))
                        norm_stats(xn)
                    if s == 11:
                        since(dve, "xm_turned", g)
                        norm_apply(xm, xn).then_inc(R["xm_ready"], 1)

                def upper(s, g, b):
                    xg = tiles(X[:, g, :])
                    if s in (2, 3):
                        since(dve, "o_done1", g)
                        for c in (2 * s - 4, 2 * s - 3):
                            dve.wait_ge(R["scored1"], 4 * g + c + 1)
                            dve.tensor_scalar(s1[:, c, :], bank[3 + c % 2], CLIP, -CLIP, ALU.min, ALU.max)\
                               .then_inc(R["clipped"], 1)
                    if s == 3:
                        dve.wait_ge(R["clipped"], 4 * g + 4)
                        sv = s1[:, :, :].rearrange("p c (n j) -> p (c n) j", n=GN)
                        count.step(dve.tensor_reduce(top1[:, :], sv, AX, ALU.max))
                        dve.tensor_tensor(sv, sv, top1[:, :].rearrange("p (h o) -> p h o", o=1)
                                          .broadcast_to([P, 4 * GN, SEQ]), ALU.subtract)\
                           .then_inc(R["s_ready"], 1)
                    if s == 5:
                        dve.wait_ge(R["e_ready"], 4 * g + 4)
                        dve.tensor_reduce(sum1[:, :], s1[:, :, :].rearrange("p c (n j) -> p (c n) j", n=GN), AX,
                                          ALU.add).then_inc(R["summed"], 1)
                        dve.wait_ge(R["summed"], g + 1)
                        count.step(dve.reciprocal(inv1[:, :], sum1[:, :]))
                    if s == 8:
                        dve.wait_ge(R["o_done1"], g + 1)
                        inv = inv1[:, :].rearrange("p (c t m) -> p t c m", c=4, m=2)
                        o_ps = psum[:, 3:5, :].rearrange("p a (t c m h s) -> p (a t) c m h s", t=2, c=4, m=2, h=2)
                        for a in range(2):
                            rows = slice(64 * a, 64 * a + 64)
                            for m in range(2):
                                ins = dve.tensor_tensor(
                                    o1[64 * m:64 * m + 64, :, :].rearrange("p t (c h s) -> p t c h s", c=4, h=2)
                                    [:, :, :, a, :], o_ps[rows, :, :, m, a, :],
                                    inv[rows, :, :, m:m + 1].broadcast_to([64, GT, 4, S1]), ALU.mult)
                        ins.then_inc(R["o_ready1"], 1)
                        dve.wait_ge(R["o_ready1"], g + 1)
                        norm_stats(o1)
                    if s == 15:
                        count.step(norm_apply(on, o1))
                        count.step(dve.tensor_tensor(on[:, :, :], on[:, :, :], row("ln_g"), ALU.mult))
                        dve.tensor_tensor(on[:, :, :], on[:, :, :], row("ln_b"), ALU.add).then_inc(R["on_ready"], 1)
                    if s == 10:
                        dve.wait_ge(R["on_ready"], g + 1)
                        dve.wait_ge(R["gelu_ready"], g + 1)
                        count.step(dve.tensor_tensor(on[:, :, :], gl[:, :, :], on[:, :, :], ALU.add))
                        count.step(dve.scalar_tensor_tensor(out=xg, in0=on[:, :, :], scalar=tanh_x[:, 1:2],
                                                            in1=xg, op0=ALU.mult, op1=ALU.add))
                        carry(dve)
                        norm_stats(xg)
                    if s == 16:
                        norm_apply(x3, xg).then_inc(R["x3_ready"], 1)
                    if s == 12:
                        dve.wait_ge(R["logits_done"], g + 1)
                        since(dve, "g_turned", g - 1)
                        count.step(dve.tensor_tensor(
                            logits[:, :, :], bank[4][:, 0:GT * NE].rearrange("p (t e) -> p t e", e=NE),
                            prm("br").rearrange("p (o e) -> p o e", o=1).broadcast_to([P, GT, NE]), ALU.add))
                        carry(dve)
                        for t in range(GT):
                            ins = dve.max(best[:, t, :], logits[:, t, :])
                        count.step(ins)
                        carry(dve)
                        for t in range(GT):
                            ins = dve.max_index(place[:, t, :], best[:, t, :], logits[:, t, :])
                        dve.tensor_tensor(both[:, :], best[:, :, 1], best[:, :, 0], ALU.subtract)\
                           .then_inc(R["routed"], 1)
                        dve.wait_ge(R["routed"], g + 1)
                        count.step(dve.tensor_copy(placef[:, :, :], place[:, :, :]))
                        for n in range(2):
                            ins = dve.tensor_tensor(
                                pick[:, n, :, :],
                                cst("iota").rearrange("p (o e) -> p o e", o=1).broadcast_to([P, GT, NE]),
                                placef[:, :, n:n + 1].broadcast_to([P, GT, NE]), ALU.is_equal)
                        count.step(ins)
                    if s == 18:
                        dve.wait_ge(R["second_ready"], g + 1)
                        count.step(dve.tensor_scalar(weight[:, 1, :], second[:, :], 1.0, None, ALU.add))
                        count.step(dve.reciprocal(weight[:, 0, :], weight[:, 1, :]))
                        count.step(dve.tensor_tensor(weight[:, 1, :], second[:, :], weight[:, 0, :], ALU.mult))
                        for n in range(2):
                            ins = dve.tensor_tensor(
                                pick[:, n, :, :], pick[:, n, :, :],
                                weight[:, n, :].rearrange("p (t o) -> p t o", o=1).broadcast_to([P, GT, NE]),
                                ALU.mult)
                        count.step(ins)
                        dve.tensor_tensor(gates[b][:, :, :], pick[:, 0, :, :], pick[:, 1, :, :], ALU.add)\
                           .then_inc(R["gates_done"], 1)
                    if s == 14:
                        dve.wait_ge(R["gates_done"], g + 1)
                        dve.wait_ge(R["bias_done"], g + 1)
                        if not (isinstance(g, int) and g < 2):
                            dve.wait_ge(stored[b], 16 * (half_before(g, b) + b))
                        dve.tensor_copy(acc[b][:, :, :], tiles(bank[4])).then_inc(R["acc_ready"], 1)

                def experts(g, b, e, third):
                    if e >= 1 and third == 2:
                        u = e - 1
                        dve.wait_ge(R["expert_done"], AHEAD["expert_done"] + NE * g + u + 1)
                        if u == 0:
                            dve.wait_ge(R["acc_ready"], g + 1)
                        since(dve, "added", NE * g + u)
                        for t in range(GT):
                            ins = dve.scalar_tensor_tensor(
                                out=acc[b][:, t, :], in0=bank[7][:, t * P:(t + 1) * P],
                                scalar=gates[b][:, t, u:u + 1], in1=acc[b][:, t, :], op0=ALU.mult, op1=ALU.add)
                        ins.then_inc(R["added"], 1)
                        if e == NE:
                            dve.wait_ge(R["added"], AHEAD["added"] + NE * g + NE)
                            dve.scalar_tensor_tensor(out=acc[b][:, :, :], in0=acc[b][:, :, :],
                                                     scalar=tanh_f[:, 1:2], in1=tiles(X[:, g, :]), op0=ALU.mult,
                                                     op1=ALU.add).then_inc(R["res_ready"], 1)

                over_rounds(dve, lower, upper, experts, ((count, 2 * DVE_STEPS), (norms, 2 * NORMS)))

            @block.tensor
            def _(pe):
                def turn(dst, src, done):
                    for t in range(GT):
                        mm = pe.transpose(dst[:, t * P:(t + 1) * P], src[:, t, :], ident)
                    mm.then_inc(R[done], 1)

                pe.sem_inc(R["expert_done"], AHEAD["expert_done"])

                def second_ffn(g, tiles_now):
                    for t in tiles_now:
                        for r in range(HC):
                            mm = pe.matmul(ffn_ps[:, t // 2, t % 2, :], hT[:, r, t * P:(t + 1) * P], w2x[:, t, r, :],
                                           start=(t % 2 == 0 and r == 0), stop=(r == HC - 1),
                                           skip_group_check=True)
                    return mm

                def lower(s, g, b):
                    if s == 1:
                        pe.wait_ge(R["c_staged1"], g + 1)
                        since(pe, "xm_ready", g)
                        turn(bank[0], c2, "c_turned")
                        pe.wait_ge(R["oT_ready"], g + 1)
                        for t in range(GT):
                            mm = pe.matmul(bank[1][:, t * P:(t + 1) * P], oT[:, t * P:(t + 1) * P], wt1("wo0"),
                                           start=True, stop=True)
                        mm.then_inc(R["y_done"], 1)
                        pe.wait_ge(R["cn_ready"], g + 1)
                        turn(bank[2], cn, "cn_turned")
                    if s == 2:
                        pe.wait_ge(R["cT_ready"], g + 1)
                        pe.wait_ge(R["knT_ready"], g + 1)
                        pe.matmul(bank[0], wt1("wk1"), knT[:, :], start=True, stop=True).then_inc(R["k_done1"], 1)
                        for t in range(GT):
                            mm = pe.matmul(bank[2][:, t * P:(t + 1) * P], cT[:, t * P:(t + 1) * P], wt1("wv1"),
                                           start=True, stop=True)
                        mm.then_inc(R["v_done1"], 1)
                    if s == 3:
                        pe.wait_ge(R["xn_ready"], g + 1)
                        pe.wait_ge(R["k_ready1"], g + 1)
                        turn(bank[0], xn, "x_turned")
                        for t in range(GT):
                            mm = pe.matmul(bank[1][0:32, 0:P], cst("sel_first")[:, 32 * t:32 * t + 32], xn[:, t, :],
                                           start=(t == 0), stop=(t == GT - 1))
                        mm.then_inc(R["even1_picked"], 1)
                        pe.wait_ge(R["v_ready1"], 2 * g + 2)
                        for t in range(GT):
                            mm = pe.matmul(bank[2][0:32, t * P:(t + 1) * P], cst("sel_second"), xn[:, t, :],
                                           start=True, stop=True)
                        mm.then_inc(R["even2_picked"], 1)
                    if s == 4:
                        pe.wait_ge(R["odd_ready"], g + 1)
                        pe.matmul(bank[1][0:32, :], odd1[:, :, :].rearrange("p n e -> p (n e)"), xT[:, :],
                                  start=True, stop=True).then_inc(R["up_done"], 1)
                    if s in (5, 6):
                        pe.wait_ge(R["even1_ready"], g + 1)
                        pe.wait_ge(R["up_ready"], g + 1)
                        pe.wait_ge(R["even2_ready"], g + 1)
                        for e in (2 * s - 10, 2 * s - 9):
                            since(pe, "h_ready", HC * g + e - 1)
                            h = bank[1 + e % 2]
                            pe.matmul(h, wt1("w1t")[:, e * P:(e + 1) * P], xT[:, :], start=True, stop=False)
                            pe.matmul(h, even1[:, e, :], up, start=False, stop=True).then_inc(R["h_done"], 1)
                    if s == 7:
                        pe.wait_ge(R["h_ready"], HC * g + HC)
                        second_ffn(g, (0, 1))
                    if s == 8:
                        second_ffn(g, (2, 3)).then_inc(R["low_done"], 1)
                    if s == 9:
                        pe.wait_ge(R["low_ready"], g + 1)
                        for t in range(GT):
                            mm = pe.transpose(bank[2][0:32, t * P:(t + 1) * P],
                                              low[:, HC * t:HC * t + HC, :].rearrange("p c e -> p (c e)"), ident)
                        mm.then_inc(R["low_turned"], 1)
                    if s == 10:
                        pe.wait_ge(R["lowT_ready"], g + 1)
                        for t in range(GT):
                            mm = pe.matmul(ffn_ps[:, t // 2, t % 2, 0:D], lowT[:, t * P:(t + 1) * P],
                                           even2[:, t, :, :].rearrange("p e a -> p (e a)"), start=False, stop=True,
                                           skip_group_check=True)
                        mm.then_inc(R["ffn_done"], 1)

                def upper(s, g, b):
                    if s == 0:
                        pe.wait_ge(R["xm_ready"], g + 1)
                        turn(bank[3], xm, "xm_turned")
                    if s == 1:
                        pe.wait_ge(R["qnT_ready"], g + 1)
                        since(pe, "acc_ready", g)
                        pe.matmul(bank[4], wt1("wq1"), qnT[:, :], start=True, stop=True).then_inc(R["q_done1"], 1)
                    if s in (2, 3):
                        pe.wait_ge(R["q_ready1"], 2 * g + 2)
                        pe.wait_ge(R["k_ready1"], g + 1)
                        pairs = (2 * s - 4, 2 * s - 3)
                        if s == 3:
                            pe.wait_ge(R["clipped"], 4 * g + 2)
                        for n in range(GN):
                            for c in pairs:
                                r = slice(32 * c, 32 * c + 32)
                                mm = pe.matmul(bank[3 + c % 2][:, SEQ * n:SEQ * n + SEQ],
                                               q1[r, n, :, :].rearrange("p a i -> p (a i)"),
                                               k1[b][r, SEQ * n:SEQ * n + SEQ], start=True, stop=True,
                                               tile_position=(32 * c, 0))
                                if n == GN - 1:
                                    mm.then_inc(R["scored1"], 1)
                    if s in (6, 7):
                        pe.wait_ge(R["clipped"], 4 * g + 4)
                        for c in (2 * s - 12, 2 * s - 11):
                            pe.wait_ge(R["e_ready"], 4 * g + c + 1)
                            if c >= 2:
                                pe.wait_ge(R["eT_ready"], 4 * g + c - 1)
                            for t in range(GT):
                                mm = pe.transpose(bank[3 + c % 2][:, t * P:(t + 1) * P],
                                                  s1[:, c, t * P:(t + 1) * P], ident)
                            mm.then_inc(R["e_turned"], 1)
                    if s == 8:
                        pe.wait_ge(R["eT_ready"], 4 * g + 4)
                        pe.wait_ge(R["v_ready1"], 2 * g + 2)
                        for t in range(GT):
                            for c in range(4):
                                at = 64 * (4 * (t % 2) + c)
                                mm = pe.matmul(bank[3 + t // 2][:, at:at + 64], s1[:, c, t * P:(t + 1) * P],
                                               v1[b][:, 4 * t + c, :, :].rearrange("p m s -> p (m s)"),
                                               start=True, stop=True)
                        mm.then_inc(R["o_done1"], 1)
                    if s == 9:
                        pe.wait_ge(R["on_ready"], g + 1)
                        turn(bank[3], on, "on_turned")
                    if s == 10:
                        pe.wait_ge(R["onT_ready"], g + 1)
                        for t in range(GT):
                            mm = pe.matmul(bank[4][:, t * P:(t + 1) * P], onT[:, t * P:(t + 1) * P], wt1("wo1"),
                                           start=True, stop=True)
                        mm.then_inc(R["gate_done"], 1)
                    if s == 11:
                        pe.wait_ge(R["x3_ready"], g + 1)
                        turn(bank[3], x3, "x3_turned")
                    if s == 12:
                        pe.wait_ge(R["x3T_ready"], g + 1)
                        for t in range(GT):
                            mm = pe.matmul(bank[4][:, t * NE:(t + 1) * NE], x3T[b][:, t * P:(t + 1) * P],
                                           wt1("wr"), start=True, stop=True)
                        mm.then_inc(R["logits_done"], 1)
                    if s == 13:
                        pe.wait_ge(R["gates_done"], g + 1)
                        for t in range(GT):
                            mm = pe.transpose(bank[3][0:NE, t * P:(t + 1) * P], gates[b][:, t, :], ident)
                        mm.then_inc(R["g_turned"], 1)
                    if s == 14:
                        pe.wait_ge(experts_loaded, 48)
                        pe.wait_ge(R["gT_ready"], g + 1)
                        for t in range(GT):
                            mm = pe.matmul(bank[4][:, t * P:(t + 1) * P], gT[:, t * P:(t + 1) * P], B2E[:, :],
                                           start=True, stop=True)
                        mm.then_inc(R["bias_done"], 1)

                def experts(g, b, e, third):
                    if third == 0:
                        if e < NE:
                            for c in range(HC):
                                since(pe, "relu_done", NE * HC * g + HC * e + c - 1)
                                pe.matmul(bank[5 + c % 2], W1E[:, e, c * P:(c + 1) * P], x3T[b][:, :],
                                          start=True, stop=True).then_inc(R["hidden_done"], 1)
                    elif e >= 1:
                        u = e - 1
                        if third == 1:
                            pe.wait_ge(R["relu_done"], AHEAD["relu_done"] + NE * HC * g + HC * e)
                            since(pe, "added", NE * g + u)
                        for t in (2 * third - 2, 2 * third - 1):
                            for c in range(HC):
                                mm = pe.matmul(bank[7][:, t * P:(t + 1) * P], hE[u % 2][:, c, t * P:(t + 1) * P],
                                               W2E[:, u, c, :], start=(c == 0), stop=(c == HC - 1))
                        if third == 2:
                            mm.then_inc(R["expert_done"], 1)

                over_rounds(pe, lower, upper, experts)


def kernel(**inputs):
    from concourse import bacc
    from concourse.bass_utils import run_bass_kernel_spmd

    w = {k: np.asarray(v) for k, v in inputs.items()}

    def packed(pieces, width):
        a = np.concatenate([p.reshape(P, -1) for p in pieces], 1)
        assert a.shape == (P, width), a.shape
        return np.ascontiguousarray(a)

    def row(v):
        return np.tile(v.reshape(1, -1), (P, 1))

    params = packed([
        w["L0_xattn_content_bias"], w["L0_xattn_position_bias"], w["L0_ffn_b1"].reshape(HC, P).T,
        w["L1_xattn_pre_g"], w["L1_xattn_pre_b"], w["L1_ffn_b1"].reshape(NE * HC, P).T,
        row(w["L0_ffn_b2"]), row(w["L1_xattn_ln_g"]), row(w["L1_xattn_ln_b"]), row(w["L1_ffn_br"]),
        row(w["L0_ffn_scale"]), row(w["g_xattn"]), row(w["g_ffn"])], PARAM_W)
    weights0 = packed([w["L0_xattn_Wq"], w["L0_xattn_Wkc"], w["L0_xattn_Wkp"], w["L0_xattn_Wv"],
                       w["L0_xattn_positional_encoding"]], WEIGHT0_W)
    weights1 = packed([
        w["L0_xattn_Wo"], w["L0_ffn_W1"].T, w["L0_ffn_W2"].T.reshape(HC, P, D).transpose(1, 0, 2),
        w["L1_xattn_Wq"], w["L1_xattn_Wk"], w["L1_xattn_Wv"], w["L1_xattn_Wo"], w["L1_ffn_Wr"]],
        WEIGHT1_W)
    arrays = {
        "x": w["x"], "ctx": w["ctx_1024"], "mask": w["mask_1x1xSx1024_fk0"].reshape(SEQ, KEYS),
        "consts": constants(), "params": params, "weights0": weights0, "weights1": weights1,
        "w1e": w["L1_ffn_W1"].transpose(1, 0, 2), "w2e": w["L1_ffn_W2"].reshape(NE, HC, P, D).transpose(2, 0, 1, 3),
        "b2e": w["L1_ffn_b2"]}
    arrays = {k: np.ascontiguousarray(a) for k, a in arrays.items()}

    nc = bacc.Bacc("TRN2", target_bir_lowering=False, num_devices=1)
    ins = [nc.dram_tensor(k, a.shape, mybir.dt.from_np(a.dtype), kind="ExternalInput").ap()
           for k, a in arrays.items()]
    scratch = [nc.dram_tensor("q_scratch", [H0, S0, len(Q_PARTS), GROUPS, GTOK], BF16, kind="Internal").ap(),
               nc.dram_tensor("k_scratch", [H0, S0, len(K_PARTS), GROUPS, 2 * GTOK], BF16, kind="Internal").ap(),
               nc.dram_tensor("kp_scratch", [PARTS, P, KEYS], BF16, kind="Internal").ap(),
               nc.dram_tensor("ot_scratch", [H0, S0, NSEQ * SEQ], F32, kind="Internal").ap(),
               nc.dram_tensor("st_scratch", [H0, S0, NSEQ * SEQ], F32, kind="Internal").ap()]
    out = nc.dram_tensor("out", [NSEQ, SEQ, D], F32, kind="ExternalOutput").ap()
    flamingo_kernel(nc, *ins, *scratch, out)
    r = run_bass_kernel_spmd(nc, [arrays], core_ids=[0])
    return r.results[0]["out"]
```
